# Optimizing a Trainium2 kernel written in Bass

```python
import numpy as np
import jax
import jax.numpy as jnp

def _softmax(x, axis=-1):
    return jax.nn.softmax(x, axis=axis)

def _gelu(x):
    return jax.nn.gelu(x, approximate=True)

def _silu(x):
    return jax.nn.silu(x)

def _sigmoid(x):
    return jax.nn.sigmoid(x)

def _layernorm(x, axis=-1, eps=1e-05):
    m = jnp.mean(x, axis=axis, keepdims=True)
    v = jnp.var(x, axis=axis, keepdims=True)
    return (x - m) / jnp.sqrt(v + eps)

def _scatter_add(tgt, idx, src, axis=0):
    return tgt.at[idx].add(src)

def _segment_sum(src, seg, n):
    return jax.ops.segment_sum(src, seg, n)
kernel_name = 'mk_perceiver_d1_seqx_r4_9a9ef5'

def setup_inputs(seed: int=0):
    np.random.seed(seed)
    _w = jnp.asarray

    def _rec_inputs():
        import jax
        import jax.numpy as jnp
        _rk = jax.random.key(seed)
        x = 7.22e-05 + 1 * jax.random.normal(jax.random.fold_in(_rk, 1), (128, 32, 512), jnp.float32)
        _lenS = 32 - jax.random.randint(jax.random.fold_in(_rk, 7), (128,), 0, max(1, 32 // 4) + 1, jnp.int32)
        _lenS2 = 257 - jax.random.randint(jax.random.fold_in(_rk, 8), (128,), 0, max(1, 257 // 4) + 1, jnp.int32)
        _ctx_512P = jax.random.normal(jax.random.fold_in(_rk, 11), (128, 16, 128), jnp.float32)
        _ctx_512c = jax.random.dirichlet(jax.random.fold_in(_rk, 511), 0.3 * jnp.ones((16,), jnp.float32), (128, 257))
        _ctx_512t = jnp.einsum('bsk,bkd->bsd', _ctx_512c, _ctx_512P)
        _ctx_512t = _ctx_512t * jax.lax.rsqrt(jnp.mean(jnp.square(_ctx_512t)) + 1e-12) * 0.953939
        ctx_512 = -0.000514642 + 1.00011 * (_ctx_512t + 0.3 * jax.random.normal(jax.random.fold_in(_rk, 611), (128, 257, 128), jnp.float32))
        return (x, ctx_512)
    x, ctx_512 = _rec_inputs()

    def _L0_xattn_setup():
        import jax, jax.numpy as jnp
        import numpy as np
        B, S, H, NH, L = (2, 512, 512, 16, 128)
        HD = H // NH
        key = jax.random.key(seed)
        k1, k2, k3, k4, k5 = jax.random.split(key, 5)
        scale = 0.02
        return {'q': jax.random.normal(k1, (B, S, H), dtype=jnp.float32), 'latent_kv': jax.random.normal(k2, (B, S, L), dtype=jnp.float32), 'Wq': jax.random.normal(k3, (H, H), dtype=jnp.float32) * scale, 'Wkv_expand': jax.random.normal(k4, (2 * H, L), dtype=jnp.float32) * scale, 'Wout': jax.random.normal(k5, (H, H), dtype=jnp.float32) * scale}
    _L0_xattn_all = _L0_xattn_setup()
    _L0_xattn_in = {k: v for k, v in _L0_xattn_all.items() if k in ('Wq', 'Wkv_expand', 'Wout')}
    del _L0_xattn_all

    def _L0_attn_setup():
        import jax, jax.numpy as jnp
        import numpy as np
        H = 512
        NH = 16
        NOPE = 128
        ROPE = 64
        VD = 128
        QR = 256
        KVR = 128
        ROPE_BASE = 10000.0
        EPS = 1e-06

        def rmsnorm(x, scale):
            var = jnp.mean(jnp.square(x), axis=-1, keepdims=True)
            return x * jax.lax.rsqrt(var + EPS) * scale

        def rope_cos_sin(seq_len, dim, offset=0):
            half = dim // 2
            inv_freq = 1.0 / ROPE_BASE ** (jnp.arange(half, dtype=jnp.float32) * 2.0 / dim)
            pos = jnp.arange(offset, offset + seq_len, dtype=jnp.float32)
            ang = pos[:, None] * inv_freq[None, :]
            return (jnp.cos(ang), jnp.sin(ang))

        def apply_rope_single(x, cos, sin):
            x1 = x[..., ::2]
            x2 = x[..., 1::2]
            c = cos[None, None, :, :]
            s = sin[None, None, :, :]
            rotated = jnp.stack([x1 * c - x2 * s, x1 * s + x2 * c], axis=-1)
            return rotated.reshape(x.shape)
        key = jax.random.key(seed)
        ks = jax.random.split(key, 12)
        B, S = (2, 512)
        w = lambda k, shp: jax.random.normal(k, shp, dtype=jnp.float32) * 0.02
        return {'x': jax.random.normal(ks[0], (B, S, H), dtype=jnp.float32), 'W_cq': w(ks[1], (H, QR)), 'q_scale': jnp.ones((QR,), dtype=jnp.float32), 'W_dq_nope': w(ks[2], (QR, NH * NOPE)), 'W_dq_rope': w(ks[3], (QR, NH * ROPE)), 'W_ckv': w(ks[4], (H, KVR)), 'kv_scale': jnp.ones((KVR,), dtype=jnp.float32), 'W_dk_nope': w(ks[5], (KVR, NH * NOPE)), 'W_dv': w(ks[6], (KVR, NH * VD)), 'W_krope': w(ks[7], (H, ROPE)), 'W_o': w(ks[8], (NH * VD, H))}
    _L0_attn_all = _L0_attn_setup()
    _L0_attn_in = {k: v for k, v in _L0_attn_all.items() if k in ('W_cq', 'q_scale', 'W_dq_nope', 'W_dq_rope', 'W_ckv', 'kv_scale', 'W_dk_nope', 'W_dv', 'W_krope', 'W_o')}
    del _L0_attn_all

    def _L0_ffn_setup():
        import jax, jax.numpy as jnp
        import numpy as np
        B, S, D = (4, 512, 512)
        E, F, K = (8, 256, 2)
        SF = 256
        EPS = 1e-06

        def _rmsnorm(x, w, eps=EPS):
            var = jnp.mean(x * x, axis=-1, keepdims=True)
            return x * jax.lax.rsqrt(var + eps) * w
        key = jax.random.key(seed)
        ks = jax.random.split(key, 9)
        g = lambda k, shape, scale: jax.random.normal(k, shape, jnp.float32) * scale
        return {'x': g(ks[0], (B, S, D), 1.0), 'rms_weight': jnp.ones((D,), jnp.float32), 'router_w': g(ks[1], (D, E), 0.02), 'w_gate': g(ks[2], (E, D, F), 0.02), 'w_up': g(ks[3], (E, D, F), 0.02), 'w_down': g(ks[4], (E, F, D), 0.02), 'sw_gate': g(ks[5], (D, SF), 0.02), 'sw_up': g(ks[6], (D, SF), 0.02), 'sw_down': g(ks[7], (SF, D), 0.02)}
    _L0_ffn_all = _L0_ffn_setup()
    _L0_ffn_in = {k: v for k, v in _L0_ffn_all.items() if k in ('rms_weight', 'router_w', 'w_gate', 'w_up', 'w_down', 'sw_gate', 'sw_up', 'sw_down')}
    del _L0_ffn_all
    return {'x': x, 'ctx_512': ctx_512, 'L0_xattn_Wq': _L0_xattn_in['Wq'], 'L0_xattn_Wkv_expand': _L0_xattn_in['Wkv_expand'], 'L0_xattn_Wout': _L0_xattn_in['Wout'], 'L0_attn_W_cq': _L0_attn_in['W_cq'], 'L0_attn_q_scale': _L0_attn_in['q_scale'], 'L0_attn_W_dq_nope': _L0_attn_in['W_dq_nope'], 'L0_attn_W_dq_rope': _L0_attn_in['W_dq_rope'], 'L0_attn_W_ckv': _L0_attn_in['W_ckv'], 'L0_attn_kv_scale': _L0_attn_in['kv_scale'], 'L0_attn_W_dk_nope': _L0_attn_in['W_dk_nope'], 'L0_attn_W_dv': _L0_attn_in['W_dv'], 'L0_attn_W_krope': _L0_attn_in['W_krope'], 'L0_attn_W_o': _L0_attn_in['W_o'], 'L0_ffn_rms_weight': _L0_ffn_in['rms_weight'], 'L0_ffn_router_w': _L0_ffn_in['router_w'], 'L0_ffn_w_gate': _L0_ffn_in['w_gate'], 'L0_ffn_w_up': _L0_ffn_in['w_up'], 'L0_ffn_w_down': _L0_ffn_in['w_down'], 'L0_ffn_sw_gate': _L0_ffn_in['sw_gate'], 'L0_ffn_sw_up': _L0_ffn_in['sw_up'], 'L0_ffn_sw_down': _L0_ffn_in['sw_down']}

def reference(x, ctx_512, L0_xattn_Wq, L0_xattn_Wkv_expand, L0_xattn_Wout, L0_attn_W_cq, L0_attn_q_scale, L0_attn_W_dq_nope, L0_attn_W_dq_rope, L0_attn_W_ckv, L0_attn_kv_scale, L0_attn_W_dk_nope, L0_attn_W_dv, L0_attn_W_krope, L0_attn_W_o, L0_ffn_rms_weight, L0_ffn_router_w, L0_ffn_w_gate, L0_ffn_w_up, L0_ffn_w_down, L0_ffn_sw_gate, L0_ffn_sw_up, L0_ffn_sw_down):
    import jax
    import jax.numpy as jnp

    def _L0_xattn_ref(q, latent_kv, Wq, Wkv_expand, Wout):
        import jax, jax.numpy as jnp
        import numpy as np
        B, S, H, NH, L = (2, 512, 512, 16, 128)
        HD = H // NH
        b, sq, _ = q.shape
        sk = latent_kv.shape[1]
        qp = q @ Wq.T
        kv = latent_kv @ Wkv_expand.T
        k, v = jnp.split(kv, 2, axis=-1)
        qh = qp.reshape(b, sq, NH, HD).transpose(0, 2, 1, 3)
        kh = k.reshape(b, sk, NH, HD).transpose(0, 2, 1, 3)
        vh = v.reshape(b, sk, NH, HD).transpose(0, 2, 1, 3)
        inv_sqrt_d = 1.0 / jnp.sqrt(jnp.float32(HD))
        scores = jnp.einsum('bhqd,bhkd->bhqk', qh, kh) * inv_sqrt_d
        causal = jnp.tril(jnp.ones((sq, sk), dtype=bool))
        scores = jnp.where(causal, scores, jnp.finfo(scores.dtype).min)
        attn = jax.nn.softmax(scores, axis=-1)
        out = jnp.einsum('bhqk,bhkd->bhqd', attn, vh)
        out = out.transpose(0, 2, 1, 3).reshape(b, sq, H)
        return out @ Wout.T

    def _L0_attn_ref(x, W_cq, q_scale, W_dq_nope, W_dq_rope, W_ckv, kv_scale, W_dk_nope, W_dv, W_krope, W_o):
        import jax, jax.numpy as jnp
        import numpy as np
        H = 512
        NH = 16
        NOPE = 128
        ROPE = 64
        VD = 128
        QR = 256
        KVR = 128
        ROPE_BASE = 10000.0
        EPS = 1e-06

        def rmsnorm(x, scale):
            var = jnp.mean(jnp.square(x), axis=-1, keepdims=True)
            return x * jax.lax.rsqrt(var + EPS) * scale

        def rope_cos_sin(seq_len, dim, offset=0):
            half = dim // 2
            inv_freq = 1.0 / ROPE_BASE ** (jnp.arange(half, dtype=jnp.float32) * 2.0 / dim)
            pos = jnp.arange(offset, offset + seq_len, dtype=jnp.float32)
            ang = pos[:, None] * inv_freq[None, :]
            return (jnp.cos(ang), jnp.sin(ang))

        def apply_rope_single(x, cos, sin):
            x1 = x[..., ::2]
            x2 = x[..., 1::2]
            c = cos[None, None, :, :]
            s = sin[None, None, :, :]
            rotated = jnp.stack([x1 * c - x2 * s, x1 * s + x2 * c], axis=-1)
            return rotated.reshape(x.shape)
        B, S, _ = x.shape
        norm_q = rmsnorm(x @ W_cq, q_scale)
        q_nope = (norm_q @ W_dq_nope).reshape(B, S, NH, NOPE)
        q_rope = (norm_q @ W_dq_rope).reshape(B, S, NH, ROPE)
        norm_kv = rmsnorm(x @ W_ckv, kv_scale)
        k_nope = (norm_kv @ W_dk_nope).reshape(B, S, NH, NOPE)
        value = (norm_kv @ W_dv).reshape(B, S, NH, VD)
        k_rope = (x @ W_krope).reshape(B, S, 1, ROPE)
        q_nope = q_nope.transpose(0, 2, 1, 3)
        q_rope = q_rope.transpose(0, 2, 1, 3)
        k_nope = k_nope.transpose(0, 2, 1, 3)
        k_rope = k_rope.transpose(0, 2, 1, 3)
        value = value.transpose(0, 2, 1, 3)
        cos, sin = rope_cos_sin(S, ROPE, offset=0)
        q_rope = apply_rope_single(q_rope, cos, sin)
        k_rope = apply_rope_single(k_rope, cos, sin) / NH
        full_head_dim = NOPE + ROPE
        query = jnp.concatenate([q_nope, q_rope], axis=-1)
        key = jnp.concatenate([k_nope, jnp.broadcast_to(k_rope, k_nope.shape[:-1] + (ROPE,))], axis=-1)
        scale = 1.0 / jnp.sqrt(jnp.asarray(full_head_dim, dtype=x.dtype))
        scores = jnp.einsum('bhqd,bhkd->bhqk', query, key) * scale
        causal = jnp.tril(jnp.ones((S, S), dtype=jnp.bool_))
        scores = jnp.where(causal[None, None, :, :], scores, -1000000000.0)
        attn = jax.nn.softmax(scores, axis=-1)
        out = jnp.einsum('bhqk,bhkd->bhqd', attn, value)
        out = out.transpose(0, 2, 1, 3).reshape(B, S, NH * VD)
        return out @ W_o

    def _L0_ffn_ref(x, rms_weight, router_w, w_gate, w_up, w_down, sw_gate, sw_up, sw_down):
        import jax, jax.numpy as jnp
        import numpy as np
        B, S, D = (4, 512, 512)
        E, F, K = (8, 256, 2)
        SF = 256
        EPS = 1e-06

        def _rmsnorm(x, w, eps=EPS):
            var = jnp.mean(x * x, axis=-1, keepdims=True)
            return x * jax.lax.rsqrt(var + eps) * w
        b, s, d = x.shape
        e = router_w.shape[1]
        h = _rmsnorm(x, rms_weight)
        ht = h.reshape(-1, d)
        t = ht.shape[0]
        logits = ht @ router_w
        probs = jax.nn.softmax(logits, axis=-1)
        topv, topi = jax.lax.top_k(probs, K)
        topv = topv / jnp.sum(topv, axis=-1, keepdims=True)
        w_dense = jnp.zeros((t, e), ht.dtype).at[jnp.arange(t)[:, None], topi].set(topv)
        g = jnp.einsum('td,edf->tef', ht, w_gate)
        u = jnp.einsum('td,edf->tef', ht, w_up)
        eo = jnp.einsum('tef,efd->ted', jax.nn.silu(g) * u, w_down)
        moe = jnp.einsum('te,ted->td', w_dense, eo)
        sh = jax.nn.silu(ht @ sw_gate) * (ht @ sw_up) @ sw_down
        return (moe + sh).reshape(b, s, d)
    x = x + _L0_xattn_ref(_layernorm(x, axis=-1), ctx_512, L0_xattn_Wq, L0_xattn_Wkv_expand, L0_xattn_Wout)
    x = x + _L0_attn_ref(_layernorm(x, axis=-1), L0_attn_W_cq, L0_attn_q_scale, L0_attn_W_dq_nope, L0_attn_W_dq_rope, L0_attn_W_ckv, L0_attn_kv_scale, L0_attn_W_dk_nope, L0_attn_W_dv, L0_attn_W_krope, L0_attn_W_o)
    x = x + _L0_ffn_ref(_layernorm(x, axis=-1), L0_ffn_rms_weight, L0_ffn_router_w, L0_ffn_w_gate, L0_ffn_w_up, L0_ffn_w_down, L0_ffn_sw_gate, L0_ffn_sw_up, L0_ffn_sw_down)
    return x

_drawn_inputs = setup_inputs


def setup_inputs(seed=0):
    import zlib

    import numpy as np

    out = dict(_drawn_inputs(seed))
    spreads = {'L0_attn_q_scale': (1.0, 0.6),
     'L0_attn_kv_scale': (1.0, 0.6),
     'L0_ffn_rms_weight': (1.0, 0.6)}
    factors = {'L0_xattn_Wq': 8.0,
     'L0_attn_W_cq': 8.0,
     'L0_attn_W_dq_nope': 8.0,
     'L0_attn_W_dq_rope': 8.0,
     'L0_attn_W_dk_nope': 8.0,
     'L0_attn_W_krope': 8.0}
    for name, (base, spread) in spreads.items():
        noise = np.random.default_rng([zlib.crc32(name.encode()), seed]).standard_normal(out[name].shape)
        drawn = base * np.exp(spread * noise) if base else spread * noise
        out[name] = jnp.asarray(drawn.astype(out[name].dtype))
    for name, factor in factors.items():
        out[name] = (out[name] * factor).astype(out[name].dtype)
    return out
```

```python
from contextlib import ExitStack

import numpy as np

import concourse.bass as bass
from concourse import mybir

F32 = mybir.dt.float32
F32R = mybir.dt.float32r
I32 = mybir.dt.int32
U32 = mybir.dt.uint32
ALU = mybir.AluOpType
ACT = mybir.ActivationFunctionType
AX = mybir.AxisListType

B, S, H = 128, 32, 512
T = B * S
P = 128
HC = H // P
NT = T // P
TG = 4
G = NT // TG
GW = TG * P
BT = P // S
NH = 16
HD = H // NH
L = 128
QR, KVR, NOPE, ROPE, VD = 256, 128, 128, 64, 128
QC = QR // P
RH = ROPE // 2
CW = QR + KVR + ROPE
HJ = P // HD
E, F = 8, 256
FC = F // P
TOPK = 2
NTE = T * TOPK // P + E
SLOTS = NTE * P
LN_EPS = 1e-5
RMS_EPS = 1e-6
MASKED = -1e30
XA_SCALE = float(np.float32(1.0) / np.sqrt(np.float32(HD)))
MLA_SCALE = float(np.float32(1.0) / np.sqrt(np.float32(NOPE + ROPE)))
RSQRT_MAGIC = float(0x5F3759DF)

C_IDENT, C_TRI, C_MASK = 0, P, 2 * P
C_COS_D = C_MASK + S
C_SIN_D = C_COS_D + S
C_COS_P = C_SIN_D + S
C_SIN_P = C_COS_P + RH
C_TILE = C_SIN_P + RH
C_TOKEN = C_TILE + NTE
C_FIRST = C_TOKEN + NT
C_END = C_FIRST + E


def constants():
    c = np.zeros((P, C_END), np.float32)
    row = np.arange(P)
    pos = row % S
    c[:, C_IDENT:C_IDENT + P] = np.eye(P)
    c[:, C_TRI:C_TRI + P] = row[:, None] < row[None, :]
    c[:, C_MASK:C_MASK + S] = np.where(np.arange(S)[None, :] <= pos[:, None], 0.0, MASKED)
    freq = (np.float32(1.0) / np.power(np.float32(10000.0), np.arange(RH, dtype=np.float32) * np.float32(2.0) / np.float32(ROPE))).astype(np.float32)
    angle = np.arange(S, dtype=np.float32)[:, None] * freq[None, :]
    cos, sin = np.cos(angle).astype(np.float32), np.sin(angle).astype(np.float32)
    c[:, C_COS_D:C_COS_D + S] = cos.T[row % RH]
    c[:, C_SIN_D:C_SIN_D + S] = sin.T[row % RH]
    c[:, C_COS_P:C_COS_P + RH] = cos[pos] / NH
    c[:, C_SIN_P:C_SIN_P + RH] = sin[pos] / NH
    c[:, C_TILE:C_TILE + NTE] = np.arange(NTE)[None, :]
    c[:, C_TOKEN:C_TOKEN + NT] = np.arange(NT)[None, :] * P + row[:, None]
    c[:, C_FIRST:C_FIRST + E] = E - np.arange(E)[None, :]
    return c


class Steps:

    def __init__(self, engine, semaphore, done_before):
        self.engine, self.semaphore, self.value = engine, semaphore, done_before

    def __call__(self, instruction):
        self.value = self.value + 1
        instruction.then_inc(self.semaphore, 1)
        self.engine.wait_ge(self.semaphore, self.value)


def settle(engine, semaphore):
    engine.nop().then_inc(semaphore, 1)


RSQRT_STEPS = 10


def rsqrt(nc, step, y, u, v):
    step(nc.vector.tensor_scalar(y.bitcast(I32), v.bitcast(I32), -0.5, RSQRT_MAGIC, ALU.mult, ALU.add))
    for _ in range(3):
        step(nc.vector.tensor_tensor(u, y, y, ALU.mult))
        step(nc.vector.scalar_tensor_tensor(u, u, -0.5, v, ALU.mult, ALU.mult))
        step(nc.vector.scalar_tensor_tensor(y, u, 1.5, y, ALU.add, ALU.mult))


def product(nc, out, a, b, first=True, last=True):
    nc.tensor.matmul(out, a[0], b[0], start=first, stop=False)
    nc.tensor.matmul(out, a[0], b[1], start=False, stop=False)
    return nc.tensor.matmul(out, a[1], b[0], start=False, stop=last)


def both(pair, *index):
    return pair[0][index], pair[1][index]


def dyn(g):
    return g if isinstance(g, int) else bass.ds(g, 1)


def group_of(view, g):
    if isinstance(g, int):
        return view[g]
    return view[bass.ds(g, 1)].rearrange("a p t d -> p (a t) d")


def columns_of(view, g):
    return view[:, g * GW:(g + 1) * GW] if isinstance(g, int) else view[:, bass.ds(g * GW, GW)]


def cross_attention(nc, sb, pb, sem, d, x1_dram):
    x_v = d["x"].rearrange("(g t p) d -> g p t d", t=TG, p=P)
    x1_v = x1_dram.rearrange("(g t p) d -> g p t d", t=TG, p=P)

    const = sb("xa_const", [P, C_END], F32)
    ident = const[:, C_IDENT:C_IDENT + P]
    mask = const[:, C_MASK:C_MASK + S]
    stage = sb("xa_stage", [P, HC, H], F32)
    wq = [sb(f"xa_wq{i}", [P, HC, H], F32R) for i in range(2)]
    wkv = [sb(f"xa_wkv{i}", [P, 2 * H], F32R) for i in range(2)]
    wo = [sb(f"xa_wo{i}", [P, HC, H], F32R) for i in range(2)]
    x_in = sb("xa_x", [P, TG, H], F32)
    xres = sb("xa_xres", [P, TG, H], F32)
    xn = sb("xa_xn", [P, TG, H], F32)
    xT = [sb(f"xa_xT{i}", [P, HC, GW], F32R) for i in range(2)]
    cin = sb("xa_ctx", [P, GW], F32)
    cT = [sb(f"xa_cT{i}", [P, GW], F32R) for i in range(2)]
    qT = sb("xa_qT", [P, HC, GW], F32)
    kbd = sb("xa_kbd", [P, TG * BT, HC, P], F32)
    val = sb("xa_v", [P, TG, H], F32)
    sc = sb("xa_sc", [P, NH, S], F32)
    ex = sb("xa_ex", [P, NH, S], F32)
    pr = sb("xa_pr", [P, NH, S], F32)
    smx = sb("xa_max", [P, NH], F32)
    ssum = sb("xa_sum", [P, NH], F32)
    srec = sb("xa_rec", [P, NH], F32)
    pT = sb("xa_pT", [P, TG, NH, P], F32)
    oT = [sb(f"xa_oT{i}", [P, HC, P], F32R) for i in range(2)]
    st = sb("xa_st", [P, TG, 6], F32)
    mv = sb("xa_mv", [P, TG, 2], F32)
    var = sb("xa_var", [P, TG], F32)
    rstd = sb("xa_rstd", [P, TG], F32)
    tmp = sb("xa_tmp", [P, TG], F32)
    nbias = sb("xa_nb", [P, TG], F32)

    ring = [pb(f"xa_ring{i}", [P, H], F32) for i in range(4)]
    s_ps = [pb(f"xa_s{i}", [P, H], F32) for i in range(2)]
    pv_ps = pb("xa_pv", [P, H], F32)
    out_ps = pb("xa_out", [P, H], F32)

    names = """const_in w_in x_in ctx_in xres_in x1_out zeroed w_hi w_lo stats xn ctx_hi ctx_lo xT_mm
        xT_hi xT_lo q_mm q_sb k_mm k_bd v_mm v_sb s_mm s_read s_sub s_exp pT pv_mm o_hi o_lo out_mm x1
        ln_step sm_step settled settled_pool""".split()
    s = {n: sem("xa_" + n) for n in names}
    weights = [("xa_WqT", wq[0][:, :, :], wq[1][:, :, :], stage[:, :, :]),
               ("xa_WkvT", wkv[0][:, :], wkv[1][:, :], stage[:, 0:2, :].rearrange("p a b -> p (a b)")),
               ("xa_WoutT", wo[0][:, :, :], wo[1][:, :, :], stage[:, :, :])]

    block = nc.Block()
    with block:

        @block.sync
        def _(sp):
            sp.dma_start(const[:, :], d["const"]).then_inc(s["const_in"], 16)

            def loads(g):
                if not (isinstance(g, int) and g == 0):
                    sp.wait_ge(s["xn"], g * TG)
                sp.dma_start(x_in[:, :, :], group_of(x_v, g)).then_inc(s["x_in"], 16)
                if not (isinstance(g, int) and g == 0):
                    sp.wait_ge(s["ctx_lo"], g)
                sp.dma_start(cin[:, :], columns_of(d["ctxT"], g)).then_inc(s["ctx_in"], 16)

            def stores(g):
                sp.wait_ge(s["x1"], g * TG + TG)
                sp.dma_start(group_of(x1_v, g), xres[:, :, :]).then_inc(s["x1_out"], 16)

            def residual(g):
                if not (isinstance(g, int) and g == 0):
                    sp.wait_ge(s["x1_out"], g * 16)
                sp.dma_start(xres[:, :, :], group_of(x_v, g)).then_inc(s["xres_in"], 16)

            loads(0)
            for n, (name, _, _, dst) in enumerate(weights):
                if n:
                    sp.wait_ge(s["w_lo"], n)
                sp.dma_start(dst, d[name]).then_inc(s["w_in"], 16)
            residual(0)
            loads(1)
            with sp.Fori(1, G - 1) as g:
                loads(g + 1)
                stores(g - 1)
                residual(g)
            stores(G - 2)
            residual(G - 1)
            stores(G - 1)
            sp.wait_ge(s["x1_out"], G * 16)

        @block.gpsimd
        def _(pool):
            nc.gpsimd.memset(kbd[:, :, :, :], 0.0).then_inc(s["zeroed"], 1)
            nc.gpsimd.memset(pT[:, :, :, :], 0.0).then_inc(s["zeroed"], 1)

            def split_context(g):
                pool.wait_ge(s["ctx_in"], g * 16 + 16)
                if not (isinstance(g, int) and g == 0):
                    pool.wait_ge(s["v_mm"], g * TG)
                settle(pool, s["settled_pool"])
                nc.gpsimd.tensor_copy(cT[0][:, :], cin[:, :]).then_inc(s["ctx_hi"], 1)
                pool.wait_ge(s["ctx_hi"], g + 1)
                nc.gpsimd.tensor_tensor(cT[1][:, :], cin[:, :], cT[0][:, :].bitcast(F32),
                                        ALU.subtract).then_inc(s["ctx_lo"], 1)

            split_context(0)
            with pool.Fori(1, G) as g:
                split_context(g)

        @block.scalar
        def _(act):
            for n, (_, hi, _, src) in enumerate(weights):
                act.wait_ge(s["w_in"], 16 * (n + 1))
                nc.scalar.copy(hi, src).then_inc(s["w_hi"], 1)

            def normalise(g):
                act.wait_ge(s["stats"], g + 1)
                if not (isinstance(g, int) and g == 0):
                    act.wait_ge(s["xT_mm"], g * TG)
                for t in range(TG):
                    nc.scalar.activation(xn[:, t, :], x_in[:, t, :], ACT.Identity, bias=nbias[:, t:t + 1],
                                         scale=rstd[:, t:t + 1]).then_inc(s["xn"], 1)

            def front(g, ahead):
                for t in range(TG):
                    act.wait_ge(s["xT_mm"], g * TG + t + 1)
                    nc.scalar.copy(xT[0][:, :, t * P:(t + 1) * P],
                                   ring[t][:, :].rearrange("p (c q) -> p c q", c=HC)).then_inc(s["xT_hi"], 1)
                if ahead:
                    normalise(g + 1)
                for m in range(HC):
                    act.wait_ge(s["q_mm"], g * HC + m + 1)
                    nc.scalar.copy(qT[:, m, :], ring[m][:, :]).then_inc(s["q_sb"], 1)
                if isinstance(g, int) and g == 0:
                    act.wait_ge(s["zeroed"], 1)
                for m in range(HC):
                    act.wait_ge(s["k_mm"], g * HC + m + 1)
                    for j in range(HJ):
                        rows = slice(j * HD, (j + 1) * HD)
                        last = nc.scalar.copy(kbd[rows, :, m, j * S:(j + 1) * S],
                                              ring[m][rows, :].rearrange("p (b k) -> p b k", k=S))
                    last.then_inc(s["k_bd"], 1)

            def exponent(g, t):
                act.wait_ge(s["s_sub"], g * TG + t + 1)
                nc.scalar.activation(ex[:, :, :], sc[:, :, :], ACT.Exp, scale=XA_SCALE).then_inc(s["s_exp"], 1)

            def out_hi(g, t):
                act.wait_ge(s["pv_mm"], g * TG + t + 1)
                nc.scalar.copy(oT[0][:, :, :], pv_ps[:, :].rearrange("p (c q) -> p c q", c=HC)).then_inc(s["o_hi"], 1)

            def body(g, back, ahead):
                front(g, ahead)
                for t in range(TG):
                    if back:
                        out_hi(g - 1, t)
                    exponent(g, t)

            normalise(0)
            body(0, False, True)
            with act.Fori(1, G - 1) as g:
                body(g, True, True)
            body(G - 1, True, False)
            for t in range(TG):
                out_hi(G - 1, t)

        @block.vector
        def _(dve):
            def statistics(g):
                step = Steps(dve, s["ln_step"], g * (RSQRT_STEPS + 4))
                dve.wait_ge(s["x_in"], g * 16 + 16)
                if not (isinstance(g, int) and g == 0):
                    dve.wait_ge(s["xn"], g * TG)
                for t in range(TG):
                    last = nc.vector.bn_stats(st[:, t, :], x_in[:, t, :])
                step(last)
                settle(dve, s["settled"])
                for t in range(TG):
                    last = nc.vector.bn_aggr(mv[:, t, :], st[:, t, :])
                step(last)
                step(nc.vector.tensor_scalar(var[:, :], mv[:, :, 1], LN_EPS, None, ALU.add))
                rsqrt(nc, step, rstd[:, :], tmp[:, :], var[:, :])
                step(nc.vector.scalar_tensor_tensor(nbias[:, :], mv[:, :, 0], -1.0, rstd[:, :], ALU.mult, ALU.mult))
                dve.nop().then_inc(s["stats"], 1)

            statistics(0)
            for n, (_, hi, lo, src) in enumerate(weights):
                dve.wait_ge(s["w_hi"], n + 1)
                nc.vector.tensor_tensor(lo, src, hi.bitcast(F32), ALU.subtract).then_inc(s["w_lo"], 1)

            def front(g, ahead):
                for t in range(TG):
                    dve.wait_ge(s["xT_hi"], g * TG + t + 1)
                    part = (slice(None), slice(None), slice(t * P, (t + 1) * P))
                    nc.vector.tensor_tensor(xT[1][part], ring[t][:, :].rearrange("p (c q) -> p c q", c=HC),
                                            xT[0][part].bitcast(F32), ALU.subtract).then_inc(s["xT_lo"], 1)
                if ahead:
                    statistics(g + 1)

            def softmax(g, t):
                step = Steps(dve, s["sm_step"], (g * TG + t) * 4)
                dve.wait_ge(s["s_mm"], g * TG + t + 1)
                nc.vector.tensor_tensor(sc[:, :, :], s_ps[t % 2][:, :].rearrange("p (h k) -> p h k", h=NH),
                                        mask.unsqueeze(1).broadcast_to([P, NH, S]), ALU.add).then_inc(s["s_read"], 1)
                dve.wait_ge(s["s_read"], g * TG + t + 1)
                step(nc.vector.tensor_reduce(smx[:, :], sc[:, :, :], AX.X, ALU.max))
                nc.vector.tensor_tensor(sc[:, :, :], sc[:, :, :], smx[:, :].unsqueeze(2).broadcast_to([P, NH, S]),
                                        ALU.subtract).then_inc(s["s_sub"], 1)
                dve.wait_ge(s["s_exp"], g * TG + t + 1)
                step(nc.vector.tensor_reduce(ssum[:, :], ex[:, :, :], AX.X, ALU.add))
                step(nc.vector.reciprocal(srec[:, :], ssum[:, :]))
                step(nc.vector.tensor_tensor(pr[:, :, :], ex[:, :, :], srec[:, :].unsqueeze(2).broadcast_to([P, NH, S]),
                                             ALU.mult))
                for b in range(BT):
                    rows = slice(b * S, (b + 1) * S)
                    last = nc.vector.transpose(pT[rows, t, :, b * S:(b + 1) * S], pr[rows, :, :])
                last.then_inc(s["pT"], 1)

            def out_lo(g, t):
                dve.wait_ge(s["o_hi"], g * TG + t + 1)
                nc.vector.tensor_tensor(oT[1][:, :, :], pv_ps[:, :].rearrange("p (c q) -> p c q", c=HC),
                                        oT[0][:, :, :].bitcast(F32), ALU.subtract).then_inc(s["o_lo"], 1)

            def value(g, t):
                dve.wait_ge(s["v_mm"], g * TG + t + 1)
                nc.vector.tensor_copy(val[:, t, :], ring[t][:, :]).then_inc(s["v_sb"], 1)

            def add(g, t):
                if t == 0:
                    dve.wait_ge(s["xres_in"], g * 16 + 16)
                dve.wait_ge(s["out_mm"], g * TG + t + 1)
                nc.vector.tensor_tensor(xres[:, t, :], out_ps[:, :], xres[:, t, :], ALU.add).then_inc(s["x1"], 1)

            def body(g, back, ahead):
                front(g, ahead)
                for t in range(TG):
                    if back:
                        out_lo(g - 1, t)
                    value(g, t)
                    if isinstance(g, int) and g == 0 and t == 0:
                        dve.wait_ge(s["zeroed"], 2)
                    softmax(g, t)
                    if back:
                        add(g - 1, t)

            body(0, False, True)
            with dve.Fori(1, G - 1) as g:
                body(g, True, True)
            body(G - 1, True, False)
            for t in range(TG):
                out_lo(G - 1, t)
                add(G - 1, t)

        @block.tensor
        def _(pe):
            pe.wait_ge(s["const_in"], 16)

            def front(g):
                for t in range(TG):
                    pe.wait_ge(s["xn"], g * TG + t + 1)
                    if not (isinstance(g, int) and g == 0):
                        pe.wait_ge(s["v_sb"], (g - 1) * TG + t + 1)
                    for c in range(HC):
                        last = nc.tensor.transpose(ring[t][:, c * P:(c + 1) * P], xn[:, t, c * P:(c + 1) * P], ident)
                    last.then_inc(s["xT_mm"], 1)
                if isinstance(g, int) and g == 0:
                    pe.wait_ge(s["w_lo"], 1)
                for m in range(HC):
                    pe.wait_ge(s["xT_lo"], g * TG + TG)
                    for c in range(HC):
                        last = product(nc, ring[m][:, :], both(wq, slice(None), c, slice(m * P, (m + 1) * P)),
                                       both(xT, slice(None), c, slice(None)), c == 0, c == HC - 1)
                    last.then_inc(s["q_mm"], 1)
                pe.wait_ge(s["ctx_lo"], g + 1)
                if isinstance(g, int) and g == 0:
                    pe.wait_ge(s["w_lo"], 2)
                for m in range(HC):
                    pe.wait_ge(s["q_sb"], g * HC + m + 1)
                    product(nc, ring[m][:, :], both(wkv, slice(None), slice(m * P, (m + 1) * P)),
                            both(cT, slice(None), slice(None))).then_inc(s["k_mm"], 1)

            def values(g, t):
                pe.wait_ge(s["k_bd"], g * HC + t + 1)
                product(nc, ring[t][:, :], both(cT, slice(None), slice(t * P, (t + 1) * P)),
                        both(wkv, slice(None), slice(H, 2 * H))).then_inc(s["v_mm"], 1)

            def scores(g, t):
                if t == 0:
                    pe.wait_ge(s["k_bd"], g * HC + HC)
                if t >= 2:
                    pe.wait_ge(s["s_read"], g * TG + t - 1)
                elif not (isinstance(g, int) and g == 0):
                    pe.wait_ge(s["s_read"], (g - 1) * TG + t + 3)
                for b in range(BT):
                    token = t * P + b * S
                    for m in range(HC):
                        last = nc.tensor.matmul(s_ps[t % 2][b * S:(b + 1) * S, m * P:(m + 1) * P],
                                                qT[:, m, token:token + S], kbd[:, t * BT + b, m, :],
                                                start=True, stop=True)
                last.then_inc(s["s_mm"], 1)

            def weighted(g, t):
                pe.wait_ge(s["pT"], g * TG + t + 1)
                if t == 0:
                    pe.wait_ge(s["v_sb"], g * TG + TG)
                if not (isinstance(g, int) and g == 0 and t == 0):
                    pe.wait_ge(s["o_lo"], g * TG + t)
                for m in range(HC):
                    for j in range(HJ):
                        h = m * HJ + j
                        last = nc.tensor.matmul(pv_ps[j * HD:(j + 1) * HD, m * P:(m + 1) * P],
                                                val[:, t, h * HD:(h + 1) * HD], pT[:, t, h, :],
                                                start=True, stop=True)
                last.then_inc(s["pv_mm"], 1)

            def outputs(g, t):
                pe.wait_ge(s["o_lo"], g * TG + t + 1)
                if isinstance(g, int) and g == 0 and t == 0:
                    pe.wait_ge(s["w_lo"], 3)
                if not (isinstance(g, int) and g == 0 and t == 0):
                    pe.wait_ge(s["x1"], g * TG + t)
                for m in range(HC):
                    last = product(nc, out_ps[:, :], both(oT, slice(None), m, slice(None)),
                                   both(wo, slice(None), m, slice(None)), m == 0, m == HC - 1)
                last.then_inc(s["out_mm"], 1)

            def body(g, back):
                front(g)
                for t in range(TG):
                    if back:
                        weighted(g - 1, t)
                    values(g, t)
                    scores(g, t)
                    if back:
                        outputs(g - 1, t)

            body(0, False)
            with pe.Fori(1, G) as g:
                body(g, True)
            for t in range(TG):
                weighted(G - 1, t)
                outputs(G - 1, t)


RMS_STEPS = RSQRT_STEPS


def latent_scores(nc, sb, pb, sem, d, x1_dram, probs_dram, nkv_dram):
    x_v = x1_dram.rearrange("(g t p) d -> g p t d", t=TG, p=P)
    nkv_v = nkv_dram.rearrange("(g t p) d -> g p t d", t=TG, p=P)
    probs_v = probs_dram.rearrange("(g t) p n -> g p t n", t=TG)

    const = sb("ls_const", [P, C_END], F32)
    ident = const[:, C_IDENT:C_IDENT + P]
    mask = const[:, C_MASK:C_MASK + S]
    cos_d, sin_d = (const[:, c:c + S].unsqueeze(1).broadcast_to([P, GW // S, S]) for c in (C_COS_D, C_SIN_D))
    cos_p, sin_p = (const[:, c:c + RH].unsqueeze(1).broadcast_to([P, TG, RH]) for c in (C_COS_P, C_SIN_P))
    qscale = sb("ls_qscale", [P, QC], F32)
    kvscale = sb("ls_kvscale", [P, 1], F32)
    wc = [sb(f"ls_wc{i}", [P, HC, CW], F32R) for i in range(2)]
    wabs = [sb(f"ls_wabs{i}", [P, QC, NH * KVR], F32R) for i in range(2)]
    wrope = [sb(f"ls_wrope{i}", [P, QC, NH * ROPE], F32R) for i in range(2)]
    x_in = sb("ls_x", [P, TG, H], F32)
    xn = sb("ls_xn", [P, TG, H], F32)
    xT = [sb(f"ls_xT{i}", [P, HC, GW], F32R) for i in range(2)]
    craw = sb("ls_craw", [P, TG, CW], F32)
    krep = [sb(f"ls_krep{i}", [P, TG, HJ, RH], F32) for i in range(2)]
    kprod = [sb(f"ls_kprod{i}", [P, TG, RH], F32) for i in range(4)]
    cqT = [sb(f"ls_cqT{i}", [P, QC, GW], F32R) for i in range(2)]
    nkvT = sb("ls_nkvT", [P, GW], F32)
    krz = [sb(f"ls_krz{i}", [P, HJ, GW], F32) for i in range(2)]
    qr = [sb(f"ls_qr{i}", [P, NH // HJ, GW], F32) for i in range(2)]
    rot = [sb(f"ls_rot{i}", [P, GW], F32) for i in range(4)]
    qa = sb("ls_qa", [P, NH, GW], F32)
    sc = sb("ls_sc", [P, NH, S], F32)
    ex = sb("ls_ex", [P, NH, S], F32)
    smx = sb("ls_max", [P, NH], F32)
    ssum = sb("ls_sum", [P, NH], F32)
    srec = sb("ls_rec", [P, NH], F32)
    pT = sb("ls_pT", [P, TG, NH * S], F32)
    st = sb("ls_st", [P, TG, 6], F32)
    mv = sb("ls_mv", [P, TG, 2], F32)
    var = sb("ls_var", [P, TG], F32)
    rstd = sb("ls_rstd", [P, TG], F32)
    tmp = sb("ls_tmp", [P, TG], F32)
    nbias = sb("ls_nb", [P, TG], F32)
    squares = sb("ls_squares", [P, QR], F32)
    sumsq = sb("ls_sumsq", [P, 2, TG], F32)
    rvar = sb("ls_rvar", [P, 2, TG], F32)
    rrms = sb("ls_rrms", [P, 2, TG], F32)
    rtmp = sb("ls_rtmp", [P, 2, TG], F32)

    wdq_st, wdk_st = qa[:, :, 0:QR], qa[:, :, QR:QR + KVR]
    wrope_st = qr[0][:, :, :].rearrange("p a b -> p (a b)").rearrange("p (c n) -> p c n", c=QC)
    wc_st = qr[1][:, :, 0:CW]

    ring = [pb(f"ls_ring{i}", [P, H], F32) for i in range(4)]
    s_ps = [pb(f"ls_s{i}", [P, H], F32) for i in range(2)]
    spare = [pb(f"ls_spare{i}", [P, H], F32) for i in range(2)]
    qa_ps = [ring[3], ring[0], spare[0], spare[1]]

    names = """const_in wc_in wdq_in wrope_in x_in nkv_out probs_out zeroed wc_hi wc_lo wrope_hi wrope_lo
        wabs_mm wabs_hi wabs_lo stats xn xT_mm xT_hi xT_lo c_mm c_sq c_raw c_ready cq_T nkv_T kr_T cq_hi cq_lo
        nkv_sb kr_sb rope_mm rope_prod rope_sb qa_mm qa_sb s_mm s_masked s_max s_sub s_exp s_rec s_prob pT
        ln_step rms_step key_step sm_step settled""".split()
    s = {n: sem("ls_" + n) for n in names}
    every = slice(None)

    block = nc.Block()
    with block:

        @block.sync
        def _(sp):
            sp.dma_start(const[:, :], d["const"]).then_inc(s["const_in"], 16)
            sp.dma_start(qscale[:, :], d["q_scale"]).then_inc(s["const_in"], 16)
            sp.dma_start(kvscale[:, :], d["kv_scale"]).then_inc(s["const_in"], 16)
            sp.dma_start(wc_st, d["ls_Wc"]).then_inc(s["wc_in"], 16)
            sp.dma_start(wdq_st, d["ls_WdqT"]).then_inc(s["wdq_in"], 16)
            sp.dma_start(wdk_st, d["ls_WdkT"]).then_inc(s["wdq_in"], 16)
            sp.dma_start(wrope_st, d["ls_Wrope"]).then_inc(s["wrope_in"], 16)

            def loads(g):
                if not (isinstance(g, int) and g == 0):
                    sp.wait_ge(s["xn"], g * TG)
                sp.dma_start(x_in[:, :, :], group_of(x_v, g)).then_inc(s["x_in"], 16)

            def stores(g):
                sp.wait_ge(s["c_ready"], g + 1)
                sp.dma_start(group_of(nkv_v, g), craw[:, :, QR:QR + KVR]).then_inc(s["nkv_out"], 16)

            def probs(g):
                sp.wait_ge(s["pT"], g * TG + TG)
                sp.dma_start(group_of(probs_v, g), pT[:, :, :]).then_inc(s["probs_out"], 16)

            loads(0)
            loads(1)
            stores(0)
            with sp.Fori(1, G - 1) as g:
                loads(g + 1)
                stores(g)
                probs(g - 1)
            stores(G - 1)
            probs(G - 2)
            probs(G - 1)
            sp.wait_ge(s["nkv_out"], G * 16)
            sp.wait_ge(s["probs_out"], G * 16)

        @block.gpsimd
        def _(pool):
            for i in range(2):
                nc.gpsimd.memset(krz[i][:, :, :], 0.0).then_inc(s["zeroed"], 1)

            def rotate(g, i):
                pool.wait_ge(s["rope_prod"], g * 4 + i + 1)
                nc.gpsimd.tensor_tensor(qr[0][:, i, :], rot[0][:, :], rot[1][:, :], ALU.subtract)
                nc.gpsimd.tensor_tensor(qr[1][:, i, :], rot[2][:, :], rot[3][:, :], ALU.add).then_inc(s["rope_sb"], 1)

            def subtract(g, t):
                pool.wait_ge(s["s_max"], g * TG + t + 1)
                nc.gpsimd.tensor_tensor(sc[:, :, :], sc[:, :, :], smx[:, :].unsqueeze(2).broadcast_to([P, NH, S]),
                                        ALU.subtract).then_inc(s["s_sub"], 1)

            def normalise(g, t):
                pool.wait_ge(s["s_rec"], g * TG + t + 1)
                nc.gpsimd.tensor_tensor(ex[:, :, :], ex[:, :, :], srec[:, :].unsqueeze(2).broadcast_to([P, NH, S]),
                                        ALU.mult).then_inc(s["s_prob"], 1)

            def softmax(g, t):
                subtract(g, t)
                normalise(g, t)

            def body(g, back):
                if back:
                    softmax(g - 1, 0)
                    softmax(g - 1, 1)
                for i in range(NH // HJ):
                    rotate(g, i)
                    if back and i < 2:
                        softmax(g - 1, 2 + i)

            body(0, False)
            with pool.Fori(1, G) as g:
                body(g, True)
            for t in range(TG):
                softmax(G - 1, t)

        @block.scalar
        def _(act):
            act.wait_ge(s["const_in"], 48)
            act.wait_ge(s["wc_in"], 16)
            nc.scalar.copy(wc[0][:, :, :], wc_st).then_inc(s["wc_hi"], 1)
            act.wait_ge(s["wrope_in"], 16)
            for c in range(QC):
                nc.scalar.activation(wrope[0][:, c, :], wrope_st[:, c, :], ACT.Copy,
                                     scale=qscale[:, c:c + 1]).then_inc(s["wrope_hi"], 1)
            for n in range(QC * 4):
                c, q = divmod(n, 4)
                act.wait_ge(s["wabs_mm"], n + 1)
                nc.scalar.activation(wabs[0][:, c, q * H:(q + 1) * H], ring[n % 4][:, :], ACT.Copy,
                                     scale=qscale[:, c:c + 1]).then_inc(s["wabs_hi"], 1)

            def normalise(g):
                act.wait_ge(s["stats"], g + 1)
                if not (isinstance(g, int) and g == 0):
                    act.wait_ge(s["xT_mm"], g * TG)
                for t in range(TG):
                    nc.scalar.activation(xn[:, t, :], x_in[:, t, :], ACT.Identity, bias=nbias[:, t:t + 1],
                                         scale=rstd[:, t:t + 1]).then_inc(s["xn"], 1)

            def exponent(g, t):
                act.wait_ge(s["s_sub"], g * TG + t + 1)
                if not (isinstance(g, int) and g == 0 and t == 0):
                    act.wait_ge(s["pT"], g * TG + t)
                nc.scalar.activation(ex[:, :, :], sc[:, :, :], ACT.Exp, scale=MLA_SCALE).then_inc(s["s_exp"], 1)

            def body(g, back, ahead):
                for t in range(TG):
                    act.wait_ge(s["xT_mm"], g * TG + t + 1)
                    nc.scalar.copy(xT[0][:, :, t * P:(t + 1) * P],
                                   ring[t][:, :].rearrange("p (c q) -> p c q", c=HC)).then_inc(s["xT_hi"], 1)
                if back:
                    exponent(g - 1, 0)
                for t in range(TG):
                    act.wait_ge(s["c_mm"], g * TG + t + 1)
                    if t == 0 and not (isinstance(g, int) and g == 0):
                        act.wait_ge(s["kr_T"], g * 2)
                        act.wait_ge(s["nkv_out"], g * 16)
                    for n, (a, z) in enumerate(((0, QR), (QR, QR + KVR))):
                        if not (isinstance(g, int) and g == 0 and t == 0 and n == 0):
                            act.wait_ge(s["c_sq"], (g * TG + t) * 2 + n)
                        nc.scalar.activation(squares[:, 0:z - a], ring[t][:, a:z], ACT.Square,
                                             accum_out=sumsq[:, n, t:t + 1]).then_inc(s["c_sq"], 1)
                    nc.scalar.copy(craw[:, t, :], ring[t][:, 0:CW]).then_inc(s["c_raw"], 1)
                if back:
                    exponent(g - 1, 1)
                for n in range(2):
                    act.wait_ge(s["cq_T"], g * 2 + n + 1)
                    tok = slice(n * 2 * P, (n + 1) * 2 * P)
                    nc.scalar.copy(cqT[0][:, :, tok],
                                   ring[n][:, :].rearrange("p (t c q) -> p c t q", t=2, c=QC)
                                   ).then_inc(s["cq_hi"], 1)
                act.wait_ge(s["nkv_T"], g + 1)
                nc.scalar.activation(nkvT[:, :], ring[2][:, :], ACT.Copy, scale=kvscale[:, 0:1]).then_inc(s["nkv_sb"], 1)
                if isinstance(g, int) and g == 0:
                    act.wait_ge(s["zeroed"], 2)
                for n in range(2):
                    act.wait_ge(s["kr_T"], g * 2 + n + 1)
                    for j in range(HJ):
                        rows = slice(j * RH, (j + 1) * RH)
                        last = nc.scalar.copy(krz[n][rows, j, :], ring[(3, 0)[n]][rows, :])
                    last.then_inc(s["kr_sb"], 1)
                for h in range(NH):
                    act.wait_ge(s["qa_mm"], g * NH + h + 1)
                    nc.scalar.copy(qa[:, h, :], qa_ps[h % 4][:, :]).then_inc(s["qa_sb"], 1)
                    if back and h in (3, 7):
                        exponent(g - 1, 2 + h // 4)
                    if h == 11 and ahead:
                        normalise(g + 1)

            normalise(0)
            body(0, False, True)
            with act.Fori(1, G - 1) as g:
                body(g, True, True)
            body(G - 1, True, False)
            for t in range(TG):
                exponent(G - 1, t)

        @block.vector
        def _(dve):
            def statistics(g):
                step = Steps(dve, s["ln_step"], g * (RSQRT_STEPS + 4))
                dve.wait_ge(s["x_in"], g * 16 + 16)
                if not (isinstance(g, int) and g == 0):
                    dve.wait_ge(s["xn"], g * TG)
                for t in range(TG):
                    last = nc.vector.bn_stats(st[:, t, :], x_in[:, t, :])
                step(last)
                settle(dve, s["settled"])
                for t in range(TG):
                    last = nc.vector.bn_aggr(mv[:, t, :], st[:, t, :])
                step(last)
                step(nc.vector.tensor_scalar(var[:, :], mv[:, :, 1], LN_EPS, None, ALU.add))
                rsqrt(nc, step, rstd[:, :], tmp[:, :], var[:, :])
                step(nc.vector.scalar_tensor_tensor(nbias[:, :], mv[:, :, 0], -1.0, rstd[:, :], ALU.mult, ALU.mult))
                dve.nop().then_inc(s["stats"], 1)

            dve.nop().then_inc(s["s_masked"], 2)
            statistics(0)
            dve.wait_ge(s["wc_hi"], 1)
            nc.vector.tensor_tensor(wc[1][:, :, :], wc_st, wc[0][:, :, :].bitcast(F32), ALU.subtract).then_inc(s["wc_lo"], 1)
            for c in range(QC):
                dve.wait_ge(s["wrope_hi"], c + 1)
                nc.vector.scalar_tensor_tensor(wrope[1][:, c, :], wrope_st[:, c, :], qscale[:, c:c + 1],
                                               wrope[0][:, c, :].bitcast(F32), ALU.mult,
                                               ALU.subtract).then_inc(s["wrope_lo"], 1)
            for n in range(QC * 4):
                c, q = divmod(n, 4)
                dve.wait_ge(s["wabs_hi"], n + 1)
                nc.vector.scalar_tensor_tensor(wabs[1][:, c, q * H:(q + 1) * H], ring[n % 4][:, :],
                                               qscale[:, c:c + 1], wabs[0][:, c, q * H:(q + 1) * H].bitcast(F32),
                                               ALU.mult, ALU.subtract).then_inc(s["wabs_lo"], 1)

            def xT_low(g):
                for t in range(TG):
                    dve.wait_ge(s["xT_hi"], g * TG + t + 1)
                    part = (every, every, slice(t * P, (t + 1) * P))
                    nc.vector.tensor_tensor(xT[1][part], ring[t][:, :].rearrange("p (c q) -> p c q", c=HC),
                                            xT[0][part].bitcast(F32), ALU.subtract).then_inc(s["xT_lo"], 1)

            def latents(g):
                step = Steps(dve, s["rms_step"], g * (RMS_STEPS + 2))
                dve.wait_ge(s["c_raw"], g * TG + TG)
                for n, width in enumerate((QR, KVR)):
                    last = nc.vector.tensor_scalar(rvar[:, n, :], sumsq[:, n, :], 1.0 / width, RMS_EPS, ALU.mult, ALU.add)
                    step(last)
                rsqrt(nc, step, rrms[:, :, :], rtmp[:, :, :], rvar[:, :, :])
                for t in range(TG):
                    for n, (a, z) in enumerate(((0, QR), (QR, QR + KVR))):
                        last = nc.vector.tensor_scalar(craw[:, t, a:z], craw[:, t, a:z], rrms[:, n, t:t + 1], None, ALU.mult)
                last.then_inc(s["c_ready"], 1)
                step = Steps(dve, s["key_step"], g * 2)
                k1, k2 = (craw[:, :, a:a + RH] for a in (QR + KVR, QR + KVR + RH))
                nc.vector.tensor_tensor(kprod[0][:, :, :], k1, cos_p, ALU.mult)
                nc.vector.tensor_tensor(kprod[1][:, :, :], k2, sin_p, ALU.mult)
                nc.vector.tensor_tensor(kprod[2][:, :, :], k1, sin_p, ALU.mult)
                step(nc.vector.tensor_tensor(kprod[3][:, :, :], k2, cos_p, ALU.mult))
                for n, op in enumerate((ALU.subtract, ALU.add)):
                    a, b = (kprod[2 * n + i][:, :, :].unsqueeze(2).broadcast_to([P, TG, HJ, RH]) for i in range(2))
                    last = nc.vector.tensor_tensor(krep[n][:, :, :, :], a, b, op)
                step(last)

            def masked(g, t):
                dve.wait_ge(s["s_mm"], g * TG + t + 1)
                nc.vector.transpose(sc[:, :, :].rearrange("p h k -> p (h k)"), s_ps[t % 2][:, :]).then_inc(s["s_masked"], 1)
                step = Steps(dve, s["sm_step"], (g * TG + t) * 2)
                dve.wait_ge(s["s_masked"], g * TG + t + 3)
                step(nc.vector.tensor_tensor(sc[:, :, :], sc[:, :, :], mask.unsqueeze(1).broadcast_to([P, NH, S]), ALU.add))
                nc.vector.tensor_reduce(smx[:, :], sc[:, :, :], AX.X, ALU.max).then_inc(s["s_max"], 1)
                dve.wait_ge(s["s_exp"], g * TG + t + 1)
                step(nc.vector.tensor_reduce(ssum[:, :], ex[:, :, :], AX.X, ALU.add))
                nc.vector.reciprocal(srec[:, :], ssum[:, :]).then_inc(s["s_rec"], 1)
                dve.wait_ge(s["s_prob"], g * TG + t + 1)
                if t == 0 and not (isinstance(g, int) and g == 0):
                    dve.wait_ge(s["probs_out"], g * 16)
                nc.vector.transpose(pT[:, t, :], ex[:, :, :].rearrange("p h k -> p (h k)")).then_inc(s["pT"], 1)

            def rotary(g, i):
                dve.wait_ge(s["rope_mm"], g * 8 + 2 * i + 2)
                if not (isinstance(g, int) and g == 0 and i == 0):
                    dve.wait_ge(s["rope_sb"], g * 4 + i)
                for n, (half, table) in enumerate(((0, cos_d), (1, sin_d), (0, sin_d), (1, cos_d))):
                    last = nc.vector.tensor_tensor(rot[n][:, :].rearrange("p (b q) -> p b q", q=S),
                                                   ring[1 + half][:, :].rearrange("p (b q) -> p b q", q=S), table, ALU.mult)
                last.then_inc(s["rope_prod"], 1)

            def body(g, back, ahead):
                xT_low(g)
                if back:
                    masked(g - 1, 0)
                latents(g)
                if back:
                    masked(g - 1, 1)
                for n in range(2):
                    dve.wait_ge(s["cq_hi"], g * 2 + n + 1)
                    tok = slice(n * 2 * P, (n + 1) * 2 * P)
                    nc.vector.tensor_tensor(cqT[1][:, :, tok],
                                            ring[n][:, :].rearrange("p (t c q) -> p c t q", t=2, c=QC),
                                            cqT[0][:, :, tok].bitcast(F32).rearrange("p c (t q) -> p c t q", t=2), ALU.subtract).then_inc(s["cq_lo"], 1)
                for i in range(NH // HJ):
                    rotary(g, i)
                    if back and i < 2:
                        masked(g - 1, 2 + i)
                    if ahead and i == 2:
                        statistics(g + 1)

            body(0, False, True)
            with dve.Fori(1, G - 1) as g:
                body(g, True, True)
            body(G - 1, True, False)
            for t in range(TG):
                masked(G - 1, t)

        @block.tensor
        def _(pe):
            pe.wait_ge(s["const_in"], 48)
            pe.wait_ge(s["wdq_in"], 32)
            for n in range(QC * 4):
                c, q = divmod(n, 4)
                if n >= 4:
                    pe.wait_ge(s["wabs_lo"], n - 3)
                for i in range(4):
                    h = q * 4 + i
                    last = nc.tensor.matmul(ring[n % 4][:, i * KVR:(i + 1) * KVR], wdq_st[:, h, c * P:(c + 1) * P],
                                            wdk_st[:, h, :], start=True, stop=True)
                last.then_inc(s["wabs_mm"], 1)

            def scores(g, t):
                if t == 0:
                    pe.wait_ge(s["qa_sb"], g * NH + NH)
                    pe.wait_ge(s["rope_sb"], g * 4 + 4)
                    pe.wait_ge(s["kr_sb"], g * 2 + 2)
                pe.wait_ge(s["s_masked"], g * TG + t + 1)
                for b in range(BT):
                    tok = slice(t * P + b * S, t * P + (b + 1) * S)
                    out = s_ps[t % 2][b * S:(b + 1) * S, :]
                    nc.tensor.matmul(out, nkvT[:, tok], qa[:, :, tok], start=True, stop=False)
                    for n in range(2):
                        for j in range(HJ):
                            last = nc.tensor.matmul(out.rearrange("p (i j q) -> p i j q", j=HJ, q=S)[:, :, j, :],
                                                    krz[n][:, j, tok], qr[n][:, :, tok], start=False,
                                                    stop=n == 1 and j == HJ - 1)
                last.then_inc(s["s_mm"], 1)

            def body(g, back):
                for t in range(TG):
                    pe.wait_ge(s["xn"], g * TG + t + 1)
                    if isinstance(g, int) and g == 0:
                        pe.wait_ge(s["wabs_lo"], QC * 4 - 3 + t)
                    elif t in (1, 2):
                        pe.wait_ge(s["rope_prod"], g * 4)
                    else:
                        pe.wait_ge(s["qa_sb"], g * NH)
                    for c in range(HC):
                        last = nc.tensor.transpose(ring[t][:, c * P:(c + 1) * P], xn[:, t, c * P:(c + 1) * P], ident)
                    last.then_inc(s["xT_mm"], 1)
                if back:
                    scores(g - 1, 0)
                if isinstance(g, int) and g == 0:
                    pe.wait_ge(s["wc_lo"], 1)
                for t in range(TG):
                    pe.wait_ge(s["xT_lo"], g * TG + t + 1)
                    for c in range(HC):
                        last = product(nc, ring[t][:, 0:CW], both(xT, every, c, slice(t * P, (t + 1) * P)),
                                       both(wc, every, c, every), c == 0, c == HC - 1)
                    last.then_inc(s["c_mm"], 1)
                if back:
                    for t in range(1, TG):
                        scores(g - 1, t)
                pe.wait_ge(s["c_ready"], g + 1)
                for n in range(2):
                    for i in range(2):
                        for c in range(QC):
                            last = nc.tensor.transpose(ring[n][:, (i * QC + c) * P:(i * QC + c + 1) * P],
                                                       craw[:, 2 * n + i, c * P:(c + 1) * P], ident)
                    last.then_inc(s["cq_T"], 1)
                for t in range(TG):
                    last = nc.tensor.transpose(ring[2][:, t * P:(t + 1) * P], craw[:, t, QR:QR + KVR], ident)
                last.then_inc(s["nkv_T"], 1)
                pe.wait_ge(s["key_step"], g * 2 + 2)
                for n in range(2):
                    if n:
                        pe.wait_ge(s["cq_lo"], g * 2 + 1)
                    for t in range(TG):
                        last = nc.tensor.transpose(ring[(3, 0)[n]][:, t * P:(t + 1) * P],
                                                   krep[n][:, t, :, :].rearrange("p j r -> p (j r)"), ident)
                    last.then_inc(s["kr_T"], 1)
                if isinstance(g, int) and g == 0:
                    pe.wait_ge(s["wrope_lo"], QC)
                for i in range(NH // HJ):
                    if i == 0:
                        pe.wait_ge(s["cq_lo"], g * 2 + 2)
                        pe.wait_ge(s["nkv_sb"], g + 1)
                    else:
                        pe.wait_ge(s["rope_prod"], g * 4 + i)
                    for half in range(2):
                        m = 2 * i + half
                        for c in range(QC):
                            last = product(nc, ring[1 + half][:, :], both(wrope, every, c, slice(m * P, (m + 1) * P)),
                                           both(cqT, every, c, every), c == 0, c == QC - 1)
                        last.then_inc(s["rope_mm"], 1)
                    for h in range(4 * i, 4 * i + 4):
                        if h < 2:
                            pe.wait_ge(s["kr_sb"], g * 2 + h + 1)
                        elif h >= 4 or not (isinstance(g, int) and g == 0):
                            pe.wait_ge(s["qa_sb"], g * NH + h - 3)
                        for c in range(QC):
                            last = product(nc, qa_ps[h % 4][:, :], both(wabs, every, c, slice(h * KVR, (h + 1) * KVR)),
                                           both(cqT, every, c, every), c == 0, c == QC - 1)
                        last.then_inc(s["qa_mm"], 1)

            body(0, False)
            with pe.Fori(1, G) as g:
                body(g, True)
            for t in range(TG):
                scores(G - 1, t)


FFN_STEPS = 2 * RSQRT_STEPS + 8


def latent_values(nc, sb, pb, sem, d, x1_dram, probs_dram, nkv_dram, x2_dram, h_dram, base_dram, logits):
    x1_v, x2_v, h_v, base_v = (a.rearrange("(g t p) d -> g p t d", t=TG, p=P)
                               for a in (x1_dram, x2_dram, h_dram, base_dram))
    nkv_v = nkv_dram.rearrange("(n p) d -> n p d", p=P)

    ident = sb("lv_ident", [P, P], F32)
    kvscale = sb("lv_kvscale", [P, 1], F32)
    rms_w = sb("lv_rms_w", [P, H], F32)
    wvo = [sb(f"lv_wvo{i}", [P, NH, H], F32R) for i in range(2)]
    wgu = [sb(f"lv_wgu{i}", [P, HC, 2 * F], F32R) for i in range(2)]
    wd = [sb(f"lv_wd{i}", [P, FC, H], F32R) for i in range(2)]
    wr = [sb(f"lv_wr{i}", [P, HC, P], F32R) for i in range(2)]
    pf = sb("lv_pf", [P, 2, H], F32)
    pT = [sb(f"lv_pT{i}", [P, 2, H], F32R) for i in range(2)]
    nf = sb("lv_nf", [P, 2, KVR], F32)
    nkv = [sb(f"lv_nkv{i}", [P, 2, KVR], F32R) for i in range(2)]
    oT = [sb(f"lv_oT{i}", [P, 2, NH, P], F32R) for i in range(2)]
    xres = sb("lv_xres", [P, TG, H], F32)
    xb = sb("lv_xb", [P, TG, H], F32)
    h = sb("lv_h", [P, TG, H], F32)
    hT = [sb(f"lv_hT{i}", [P, HC, GW], F32R) for i in range(2)]
    act_f = sb("lv_act", [P, FC, GW], F32)
    aT = [sb(f"lv_aT{i}", [P, FC, GW], F32R) for i in range(2)]
    lgT = sb("lv_lgT", [E, GW], F32)
    st = sb("lv_st", [P, TG, 6], F32)
    mv = sb("lv_mv", [P, TG, 2], F32)
    var = sb("lv_var", [P, TG], F32)
    rstd = sb("lv_rstd", [P, TG], F32)
    tmp = sb("lv_tmp", [P, TG], F32)
    rvar = sb("lv_rvar", [P, TG], F32)
    rrms = sb("lv_rrms", [P, TG], F32)
    nbias = sb("lv_nb", [P, TG], F32)

    wo_st = h
    wdv_st = xb[:, :, :].rearrange("p a b -> p (a b)").rearrange("p (h k) -> p h k", h=NH)
    wr_st = xres[:, 0, :].rearrange("p (c e) -> p c e", c=HC)

    ring = [pb(f"lv_ring{i}", [P, H], F32) for i in range(4)]
    pv_ps = [pb(f"lv_pv{i}", [P, H], F32) for i in range(2)]
    out_ps = pb("lv_out", [P, H], F32)
    lg_ps = pb("lv_lg", [P, H], F32)

    names = """const_in wdv_in wo_in wr_in wgu_in wd_in x1_in p_in0 p_in1 xb_in x2_out h_out base_out zeroed
        wvo_mm wvo_hi wvo_lo wgu_hi wgu_lo p_hi p_lo pv_mm o_hi o_lo out_mm x2 stats hn h_sb hT_mm hT_hi hT_lo
        lg_mm lg_sb lgT_mm logits gu_mm silu gated a_hi a_lo down_mm base ln_step settled
        settled_pe settled_pool""".split()
    s = {n: sem("lv_" + n) for n in names}
    every = slice(None)
    WO_PART = TG
    WO_PARTS = NH // WO_PART
    first = lambda g: isinstance(g, int) and g == 0

    block = nc.Block()
    with block:

        @block.sync
        def _(sp):
            sp.dma_start(ident[:, :], d["const"][:, C_IDENT:C_IDENT + P]).then_inc(s["const_in"], 16)
            sp.dma_start(kvscale[:, :], d["kv_scale"]).then_inc(s["const_in"], 16)
            sp.dma_start(rms_w[:, :], d["rms_weight"].broadcast_to([P, H])).then_inc(s["const_in"], 16)
            sp.dma_start(wdv_st, d["lv_WdvT"]).then_inc(s["wdv_in"], 16)

            def tile_loads(g, t):
                n = g * TG + t
                if not (first(g) and t < 2):
                    sp.wait_ge(s["p_lo"], 2 * n - 2)
                src = probs_dram[n] if isinstance(n, int) else probs_dram[bass.ds(n, 1)].rearrange("a p n -> p (a n)")
                sp.dma_start(pf[:, t % 2, :], src).then_inc(s[f"p_in{t % 2}"], 16)
                src = nkv_v[n] if isinstance(n, int) else nkv_v[bass.ds(n, 1)].rearrange("a p n -> p (a n)")
                sp.dma_start(nf[:, t % 2, :], src).then_inc(s[f"p_in{t % 2}"], 16)

            tile_loads(0, 0)
            tile_loads(0, 1)
            for n in range(WO_PARTS):
                if n:
                    sp.wait_ge(s["wvo_mm"], n * WO_PART)
                sp.dma_start(wo_st[:, :, :], d["lv_Wo"][:, n * WO_PART:(n + 1) * WO_PART, :]).then_inc(s["wo_in"], 16)
            sp.wait_ge(s["wvo_mm"], NH)
            sp.dma_start(h[:, :, :], d["lv_Wgu"]).then_inc(s["wgu_in"], 16)
            sp.dma_start(xb[:, 0:FC, :], d["lv_Wd"]).then_inc(s["wd_in"], 16)
            sp.dma_start(xb[:, FC, 0:HC * E].rearrange("p (c e) -> p c e", c=HC), d["lv_Wr"]).then_inc(s["wr_in"], 16)
            sp.dma_start(xres[:, :, :], x1_v[0]).then_inc(s["x1_in"], 16)

            def after_sum(g):
                sp.wait_ge(s["x2"], g * TG + TG)
                sp.dma_start(group_of(x2_v, g), xres[:, :, :]).then_inc(s["x2_out"], 16)

            def base_load(g):
                sp.wait_ge(s["x2_out"], g * 16 + 16)
                sp.wait_ge(s["base_out"], g * 16)
                sp.dma_start(xb[:, :, :], group_of(x2_v, g)).then_inc(s["xb_in"], 16)

            def residual(g):
                sp.wait_ge(s["hn"], g * TG)
                sp.dma_start(xres[:, :, :], group_of(x1_v, g)).then_inc(s["x1_in"], 16)

            def h_store(g):
                sp.wait_ge(s["h_sb"], g * TG + TG)
                sp.dma_start(group_of(h_v, g), h[:, :, :]).then_inc(s["h_out"], 16)

            def base_store(g):
                sp.wait_ge(s["base"], g * TG + 2 * TG)
                sp.dma_start(group_of(base_v, g), xb[:, :, :]).then_inc(s["base_out"], 16)

            def body(g, back, ahead):
                if back:
                    after_sum(g - 1)
                tile_loads(g, 2)
                tile_loads(g, 3)
                if back:
                    base_load(g - 1)
                    residual(g)
                    h_store(g - 1)
                if ahead:
                    tile_loads(g + 1, 0)
                    tile_loads(g + 1, 1)
                if back:
                    base_store(g - 1)

            body(0, False, True)
            sp.wait_ge(s["wgu_lo"], 3)
            with sp.Fori(1, G - 1) as g:
                body(g, True, True)
            body(G - 1, True, False)
            after_sum(G - 1)
            base_load(G - 1)
            h_store(G - 1)
            base_store(G - 1)
            for n in ("x2_out", "h_out", "base_out"):
                sp.wait_ge(s[n], G * 16)

        @block.gpsimd
        def _(pool):
            for i in range(2):
                nc.gpsimd.memset(wr[i][:, :, :].bitcast(F32), 0.0).then_inc(s["zeroed"], 1)

            def split(g, t):
                n = g * TG + t
                pool.wait_ge(s[f"p_in{t % 2}"], (g * 2 + t // 2) * 32 + 32)
                if not (first(g) and t < 2):
                    pool.wait_ge(s["pv_mm"], n * BT - BT)
                settle(pool, s["settled_pool"])
                nc.gpsimd.tensor_copy(pT[0][:, t % 2, :], pf[:, t % 2, :])
                nc.gpsimd.tensor_copy(nkv[0][:, t % 2, :], nf[:, t % 2, :]).then_inc(s["p_hi"], 1)
                pool.wait_ge(s["p_hi"], n + 1)
                nc.gpsimd.tensor_tensor(pT[1][:, t % 2, :], pf[:, t % 2, :], pT[0][:, t % 2, :].bitcast(F32),
                                        ALU.subtract).then_inc(s["p_lo"], 1)
                nc.gpsimd.tensor_tensor(nkv[1][:, t % 2, :], nf[:, t % 2, :], nkv[0][:, t % 2, :].bitcast(F32),
                                        ALU.subtract).then_inc(s["p_lo"], 1)

            def weigh(g):
                for t in range(TG):
                    pool.wait_ge(s["hn"], g * TG + t + 1)
                    nc.gpsimd.tensor_tensor(h[:, t, :], h[:, t, :], rms_w[:, :], ALU.mult).then_inc(s["h_sb"], 1)

            def body(g, back, ahead):
                if back:
                    weigh(g - 1)
                split(g, 2)
                split(g, 3)
                if ahead:
                    split(g + 1, 0)
                    split(g + 1, 1)

            split(0, 0)
            split(0, 1)
            pool.wait_ge(s["const_in"], 48)
            body(0, False, True)
            with pool.Fori(1, G - 1) as g:
                body(g, True, True)
            body(G - 1, True, False)
            weigh(G - 1)

        @block.scalar
        def _(act):
            act.wait_ge(s["const_in"], 48)
            for n in range(NH):
                act.wait_ge(s["wvo_mm"], n + 1)
                nc.scalar.activation(wvo[0][:, n, :], ring[n % 4][:, :], ACT.Copy,
                                     scale=kvscale[:, 0:1]).then_inc(s["wvo_hi"], 1)
            act.wait_ge(s["wgu_in"], 16)
            nc.scalar.copy(wgu[0][:, :, :], h[:, :, :]).then_inc(s["wgu_hi"], 1)
            act.wait_ge(s["wd_in"], 16)
            nc.scalar.copy(wd[0][:, :, :], xb[:, 0:FC, :]).then_inc(s["wgu_hi"], 1)
            act.wait_ge(s["wr_in"], 16)
            act.wait_ge(s["zeroed"], 2)
            nc.scalar.copy(wr[0][:, :, 0:E],
                           xb[:, FC, 0:HC * E].rearrange("p (c e) -> p c e", c=HC)).then_inc(s["wgu_hi"], 1)

            def sum_hi(g, t):
                for b in range(BT):
                    act.wait_ge(s["pv_mm"], (g * TG + t) * BT + b + 1)
                    nc.scalar.copy(oT[0][:, t % 2, :, b * S:(b + 1) * S],
                                   pv_ps[b % 2][:, :].rearrange("p (h q) -> p h q", h=NH)).then_inc(s["o_hi"], 1)

            def normalise(g):
                act.wait_ge(s["stats"], g + 1)
                act.wait_ge(s["h_out"], g * 16)
                act.wait_ge(s["hT_mm"], g * TG)
                for t in range(TG):
                    nc.scalar.activation(h[:, t, :], xres[:, t, :], ACT.Identity, bias=nbias[:, t:t + 1],
                                         scale=rstd[:, t:t + 1]).then_inc(s["hn"], 1)

            def h_hi(g):
                for t in range(TG):
                    act.wait_ge(s["hT_mm"], g * TG + t + 1)
                    nc.scalar.copy(hT[0][:, :, t * P:(t + 1) * P],
                                   ring[t][:, :].rearrange("p (c q) -> p c q", c=HC)).then_inc(s["hT_hi"], 1)

            def shared(g):
                act.wait_ge(s["lg_mm"], g + 1)
                nc.scalar.copy(lgT[:, :], lg_ps[0:E, :]).then_inc(s["lg_sb"], 1)
                for m in range(FC):
                    act.wait_ge(s["gu_mm"], g * 2 * FC + m + 1)
                    nc.scalar.activation(act_f[:, m, :], ring[m][:, :], ACT.Silu).then_inc(s["silu"], 1)
                for m in range(FC):
                    act.wait_ge(s["gated"], g * FC + m + 1)
                    nc.scalar.copy(aT[0][:, m, :], act_f[:, m, :]).then_inc(s["a_hi"], 1)

            def body(g, back):
                sum_hi(g, 0)
                if back:
                    normalise(g - 1)
                sum_hi(g, 1)
                if back:
                    h_hi(g - 1)
                    shared(g - 1)
                sum_hi(g, 2)
                sum_hi(g, 3)

            body(0, False)
            act.wait_ge(s["wgu_lo"], 1)
            with act.Fori(1, G) as g:
                body(g, True)
            normalise(G - 1)
            h_hi(G - 1)
            shared(G - 1)

        @block.vector
        def _(dve):
            dve.wait_ge(s["const_in"], 48)
            dve.nop().then_inc(s["base"], TG)
            for n in range(NH):
                dve.wait_ge(s["wvo_hi"], n + 1)
                nc.vector.scalar_tensor_tensor(wvo[1][:, n, :], ring[n % 4][:, :], kvscale[:, 0:1],
                                               wvo[0][:, n, :].bitcast(F32), ALU.mult, ALU.subtract).then_inc(s["wvo_lo"], 1)
            dve.wait_ge(s["wgu_hi"], 1)
            nc.vector.tensor_tensor(wgu[1][:, :, :], h[:, :, :], wgu[0][:, :, :].bitcast(F32),
                                    ALU.subtract).then_inc(s["wgu_lo"], 1)
            dve.wait_ge(s["wgu_hi"], 2)
            nc.vector.tensor_tensor(wd[1][:, :, :], xb[:, 0:FC, :], wd[0][:, :, :].bitcast(F32),
                                    ALU.subtract).then_inc(s["wgu_lo"], 1)
            dve.wait_ge(s["wgu_hi"], 3)
            nc.vector.tensor_tensor(wr[1][:, :, 0:E], xb[:, FC, 0:HC * E].rearrange("p (c e) -> p c e", c=HC),
                                    wr[0][:, :, 0:E].bitcast(F32), ALU.subtract).then_inc(s["wgu_lo"], 1)

            def sum_lo(g, t):
                for b in range(BT):
                    dve.wait_ge(s["o_hi"], (g * TG + t) * BT + b + 1)
                    part = (every, t % 2, every, slice(b * S, (b + 1) * S))
                    nc.vector.tensor_tensor(oT[1][part], pv_ps[b % 2][:, :].rearrange("p (h q) -> p h q", h=NH),
                                            oT[0][part].bitcast(F32), ALU.subtract).then_inc(s["o_lo"], 1)

            def statistics(g):
                step = Steps(dve, s["ln_step"], g * FFN_STEPS)
                dve.wait_ge(s["x2"], g * TG + TG)
                if not first(g):
                    dve.wait_ge(s["hn"], g * TG)
                for t in range(TG):
                    last = nc.vector.bn_stats(st[:, t, :], xres[:, t, :])
                step(last)
                settle(dve, s["settled"])
                for t in range(TG):
                    last = nc.vector.bn_aggr(mv[:, t, :], st[:, t, :])
                step(last)
                step(nc.vector.tensor_scalar(var[:, :], mv[:, :, 1], LN_EPS, None, ALU.add))
                rsqrt(nc, step, rstd[:, :], tmp[:, :], var[:, :])
                step(nc.vector.tensor_tensor(rvar[:, :], rstd[:, :], rstd[:, :], ALU.mult))
                step(nc.vector.tensor_tensor(rvar[:, :], rvar[:, :], mv[:, :, 1], ALU.mult))
                step(nc.vector.tensor_scalar(rvar[:, :], rvar[:, :], RMS_EPS, None, ALU.add))
                rsqrt(nc, step, rrms[:, :], tmp[:, :], rvar[:, :])
                step(nc.vector.tensor_tensor(rstd[:, :], rstd[:, :], rrms[:, :], ALU.mult))
                step(nc.vector.scalar_tensor_tensor(nbias[:, :], mv[:, :, 0], -1.0, rstd[:, :], ALU.mult, ALU.mult))
                dve.nop().then_inc(s["stats"], 1)

            def add(g, t):
                if t == 0:
                    dve.wait_ge(s["x1_in"], g * 16 + 16)
                dve.wait_ge(s["out_mm"], g * TG + t + 1)
                nc.vector.tensor_tensor(xres[:, t, :], out_ps[:, :], xres[:, t, :], ALU.add).then_inc(s["x2"], 1)

            def h_lo(g):
                for t in range(TG):
                    dve.wait_ge(s["hT_hi"], g * TG + t + 1)
                    part = (every, every, slice(t * P, (t + 1) * P))
                    nc.vector.tensor_tensor(hT[1][part], ring[t][:, :].rearrange("p (c q) -> p c q", c=HC),
                                            hT[0][part].bitcast(F32), ALU.subtract).then_inc(s["hT_lo"], 1)

            def gate(g):
                for m in range(FC):
                    dve.wait_ge(s["silu"], g * FC + m + 1)
                    dve.wait_ge(s["gu_mm"], g * 2 * FC + FC + m + 1)
                    nc.vector.tensor_tensor(act_f[:, m, :], ring[FC + m][:, :], act_f[:, m, :], ALU.mult).then_inc(s["gated"], 1)
                for m in range(FC):
                    dve.wait_ge(s["a_hi"], g * FC + m + 1)
                    nc.vector.tensor_tensor(aT[1][:, m, :], act_f[:, m, :], aT[0][:, m, :].bitcast(F32),
                                            ALU.subtract).then_inc(s["a_lo"], 1)

            def router(g):
                dve.wait_ge(s["lgT_mm"], g + 1)
                dst = logits[:, g * TG:(g + 1) * TG, :] if isinstance(g, int) else logits[:, bass.ds(g * TG, TG), :]
                nc.vector.tensor_copy(dst, lg_ps[:, 0:TG * E].rearrange("p (t e) -> p t e", t=TG)).then_inc(s["logits"], 1)

            def base(g, t):
                if t == 0:
                    dve.wait_ge(s["xb_in"], g * 16 + 16)
                dve.wait_ge(s["down_mm"], g * TG + t + 1)
                nc.vector.tensor_tensor(xb[:, t, :], ring[t][:, :], xb[:, t, :], ALU.add).then_inc(s["base"], 1)

            def body(g, back):
                sum_lo(g, 0)
                if back:
                    statistics(g - 1)
                add(g, 0)
                sum_lo(g, 1)
                if back:
                    h_lo(g - 1)
                add(g, 1)
                if back:
                    gate(g - 1)
                sum_lo(g, 2)
                if back:
                    router(g - 1)
                    base(g - 1, 0)
                    base(g - 1, 1)
                add(g, 2)
                sum_lo(g, 3)
                if back:
                    base(g - 1, 2)
                    base(g - 1, 3)
                add(g, 3)

            body(0, False)
            with dve.Fori(1, G) as g:
                body(g, True)
            statistics(G - 1)
            h_lo(G - 1)
            gate(G - 1)
            router(G - 1)
            for t in range(TG):
                base(G - 1, t)

        @block.tensor
        def _(pe):
            pe.wait_ge(s["const_in"], 48)
            pe.wait_ge(s["wdv_in"], 16)
            for n in range(NH):
                if n % WO_PART == 0:
                    pe.wait_ge(s["wo_in"], 16 * (n // WO_PART + 1))
                if n >= 4:
                    pe.wait_ge(s["wvo_lo"], n - 3)
                nc.tensor.matmul(ring[n % 4][:, :], wdv_st[:, n, :], wo_st[:, n % WO_PART, :],
                                 start=True, stop=True).then_inc(s["wvo_mm"], 1)

            def weighted(g, t):
                n = g * TG + t
                pe.wait_ge(s["p_lo"], 2 * n + 2)
                for b in range(BT):
                    if not (first(g) and t == 0 and b < 2):
                        pe.wait_ge(s["o_lo"], n * BT + b - 1)
                    rows = slice(b * S, (b + 1) * S)
                    product(nc, pv_ps[b % 2][:, :], both(nkv, rows, t % 2, every),
                            both(pT, rows, t % 2, every)).then_inc(s["pv_mm"], 1)

            def outputs(g, t):
                n = g * TG + t
                pe.wait_ge(s["o_lo"], n * BT + BT)
                if first(g) and t == 0:
                    pe.wait_ge(s["wvo_lo"], NH)
                else:
                    pe.wait_ge(s["x2"], n)
                for i in range(NH):
                    last = product(nc, out_ps[:, :], both(oT, every, t % 2, i, every), both(wvo, every, i, every),
                                   i == 0, i == NH - 1)
                last.then_inc(s["out_mm"], 1)

            def transposes(g):
                for t in range(TG):
                    pe.wait_ge(s["h_sb"], g * TG + t + 1)
                    pe.wait_ge(s["base"], g * TG + t + 1)
                    for c in range(HC):
                        last = nc.tensor.transpose(ring[t][:, c * P:(c + 1) * P], h[:, t, c * P:(c + 1) * P], ident[:, :])
                    last.then_inc(s["hT_mm"], 1)

            def shared_up(g):
                pe.wait_ge(s["hT_lo"], g * TG + TG)
                pe.wait_ge(s["logits"], g)
                for c in range(HC):
                    last = product(nc, lg_ps[:, :], both(wr, every, c, every), both(hT, every, c, every), c == 0, c == HC - 1)
                last.then_inc(s["lg_mm"], 1)
                for m in range(2 * FC):
                    for c in range(HC):
                        last = product(nc, ring[m][:, :], both(wgu, every, c, slice(m * P, (m + 1) * P)),
                                       both(hT, every, c, every), c == 0, c == HC - 1)
                    last.then_inc(s["gu_mm"], 1)

            def logit_transposes(g):
                pe.wait_ge(s["lg_sb"], g + 1)
                settle(pe, s["settled_pe"])
                for t in range(TG):
                    last = nc.tensor.transpose(lg_ps[:, t * E:(t + 1) * E], lgT[:, t * P:(t + 1) * P], ident[0:E, 0:E])
                last.then_inc(s["lgT_mm"], 1)

            def shared_down(g, t):
                pe.wait_ge(s["a_lo"], g * FC + FC)
                for m in range(FC):
                    last = product(nc, ring[t][:, :], both(aT, every, m, slice(t * P, (t + 1) * P)),
                                   both(wd, every, m, every), m == 0, m == FC - 1)
                last.then_inc(s["down_mm"], 1)

            def body(g, back):
                weighted(g, 0)
                outputs(g, 0)
                weighted(g, 1)
                if back:
                    transposes(g - 1)
                outputs(g, 1)
                if back:
                    shared_up(g - 1)
                weighted(g, 2)
                if back:
                    logit_transposes(g - 1)
                    shared_down(g - 1, 0)
                    shared_down(g - 1, 1)
                outputs(g, 2)
                weighted(g, 3)
                if back:
                    shared_down(g - 1, 2)
                    shared_down(g - 1, 3)
                outputs(g, 3)

            body(0, False)
            pe.wait_ge(s["wgu_lo"], 3)
            with pe.Fori(1, G) as g:
                body(g, True)
            transposes(G - 1)
            shared_up(G - 1)
            logit_transposes(G - 1)
            for t in range(TG):
                shared_down(G - 1, t)


UE = 4
UF = 4


def experts(nc, sb, pb, sem, d, h_dram, table_dram, y_dram, logits, slots, weights):
    const = sb("ex_const", [P, C_END], F32)
    ident = const[:, C_IDENT:C_IDENT + P]
    ones = sb("ex_ones", [P, P], F32)
    wgu = [sb(f"ex_wgu{i}", [P, E * HC, 2 * F], F32R) for i in range(2)]
    wd = sb("ex_wd", [P, E * FC, H], F32)
    hs = sb("ex_hs", [P, UE, H], F32)
    hT = [sb(f"ex_hT{i}", [P, 2, HC, P], F32R) for i in range(2)]
    gated = sb("ex_gated", [P, 2, F], F32)
    aT = sb("ex_aT", [P, 2, FC, P], F32)
    y = sb("ex_y", [P, 2, H], F32)
    route = [sb(f"ex_route{i}", [P, NT, E], F32) for i in range(3)]
    hot = [sb(f"ex_hot{i}", [P, NT, E], F32) for i in range(2)]
    row = [sb(f"ex_row{i}", [P, NT], F32) for i in range(4)]
    per = [sb(f"ex_per{i}", [P, E], F32) for i in range(4)]
    count = sb("ex_count", [P, E], I32)
    slot_i = sb("ex_slot_i", [P, TOPK, NT], I32)
    part = [sb(f"ex_part{i}", [P, TOPK, NT], I32) for i in range(2)]
    part_f = [sb(f"ex_part_f{i}", [P, TOPK, NT], F32) for i in range(2)]
    cell = sb("ex_cell", [P, TOPK, NT], U32)
    token = sb("ex_token", [P, NT], U32)
    zero = sb("ex_zero", [P, NTE], U32)
    reached = gated[:, :, :].rearrange("p a b -> p (a b)")
    expert_f = sb("ex_expert_f", [P, NTE], F32)
    expert = sb("ex_expert", [P, NTE], I32)
    source = sb("ex_source", [P, NTE], U32)
    index = sb("ex_index", [P, UE], U32)

    hT_ps = [pb(f"ex_hT_ps{i}", [P, H], F32) for i in range(2)]
    gu_ps = [pb(f"ex_gu_ps{i}", [P, H], F32) for i in range(2)]
    aT_ps = pb("ex_aT_ps", [P, H], F32)
    y_ps = [pb(f"ex_y_ps{i}", [P, H], F32) for i in range(2)]
    count_ps = pb("ex_count_ps", [P, H], F32)

    names = """const_in wd_in wgu_in0 wgu_in1 ones zeros wgu_hi wgu_lo route delta gap ranked count_mm slots_ready
        table_zero table_out source_in indexed gather0 gather1 gather2 gather3 hT_mm hT_hi hT_lo gu_mm silu gated
        aT_mm aT y_mm y_sb y_out0 y_out1 settled""".split()
    s = {n: sem("ex_" + n) for n in names}
    every = slice(None)
    STAGES = UE * H // (2 * F * 2)
    every = slice(None)
    HALF = HC // 2
    stage = [hs[:, 2 * i:2 * i + HALF, :] for i in range(2)]
    first = lambda g: isinstance(g, int) and g == 0
    assert STAGES == 2

    block = nc.Block()
    with block:

        @block.sync
        def _(sp):
            sp.dma_start(const[:, :], d["const"]).then_inc(s["const_in"], 16)
            sp.wait_ge(s["zeros"], 1)
            sp.dma_start(table_dram, zero[:, :]).then_inc(s["table_zero"], 16)
            for n in range(E * 2):
                if n >= 2:
                    sp.wait_ge(s["wgu_lo"], n - 1)
                sp.dma_start(stage[n % 2], d["ex_Wgu"][:, n * HALF:(n + 1) * HALF, :]).then_inc(s[f"wgu_in{n % 2}"], 16)
            sp.dma_start(wd[:, :, :], d["ex_Wd"]).then_inc(s["wd_in"], 16)
            sp.wait_ge(s["table_out"], TOPK * NT * 16)
            sp.dma_start(source[:, :], table_dram).then_inc(s["source_in"], 16)

            def store(k, i):
                n = k * UE + i
                sp.wait_ge(s["y_sb"], n + 1)
                dst = y_dram[n * P:(n + 1) * P, :] if isinstance(k, int) else y_dram[bass.ds(n * P, P), :]
                sp.dma_start(dst, y[:, i % 2, :]).then_inc(s[f"y_out{i % 2}"], 16)

            with sp.Fori(0, NTE // UE) as k:
                for i in range(UE):
                    store(k, i)
            for i in range(2):
                sp.wait_ge(s[f"y_out{i}"], NTE // 2 * 16)

        @block.gpsimd
        def _(pool):
            nc.gpsimd.memset(zero[:, :], 0).then_inc(s["zeros"], 1)
            nc.gpsimd.memset(ones[:, :], 1.0).then_inc(s["ones"], 1)
            pool.wait_ge(s["table_zero"], 16)
            pool.wait_ge(s["slots_ready"], 1)
            for k in range(TOPK):
                for t in range(NT):
                    nc.gpsimd.indirect_dma_start(
                        table_dram.rearrange("p (n a) -> (p n) a", a=1),
                        bass.IndirectOffsetOnAxis(ap=cell[:, k, t:t + 1], axis=0), token[:, t:t + 1], None
                    ).then_inc(s["table_out"], 16)
            pool.wait_ge(s["source_in"], 16)
            pool.wait_ge(s["wgu_lo"], 2 * E)

            def gathers(k):
                nc.gpsimd.tensor_copy(index[:, :], source[:, k * UE:(k + 1) * UE] if isinstance(k, int)
                                      else source[:, bass.ds(k * UE, UE)]).then_inc(s["indexed"], 1)
                for i in range(UE):
                    pool.wait_ge(s["indexed"], k + 1)
                    if not first(k):
                        pool.wait_ge(s["hT_mm"], (k - 1) * UE + i + 1)
                    settle(pool, s["settled"])
                    nc.gpsimd.indirect_dma_start(
                        hs[:, i, :], None, h_dram, bass.IndirectOffsetOnAxis(ap=index[:, i:i + 1], axis=0)
                    ).then_inc(s[f"gather{i}"], 16)

            gathers(0)
            with pool.Fori(1, NTE // UE) as k:
                for i in range(UE):
                    pool.wait_ge(s[f"gather{i}"], k * 16)
                settle(pool, s["settled"])
                gathers(k)

        @block.scalar
        def _(act):
            act.wait_ge(s["delta"], 1)
            nc.scalar.activation(row[3][:, :], row[2][:, :], ACT.Exp).then_inc(s["gap"], 1)
            for n in range(E * 2):
                act.wait_ge(s[f"wgu_in{n % 2}"], 16 * (n // 2 + 1))
                nc.scalar.copy(wgu[0][:, n * HALF:(n + 1) * HALF, :], stage[n % 2]).then_inc(s["wgu_hi"], 1)

            def hT_high(n, i):
                act.wait_ge(s["hT_mm"], n + 1)
                if not isinstance(n, int) or n >= 2:
                    act.wait_ge(s["gu_mm"], n - 1)
                nc.scalar.copy(hT[0][:, i % 2, :, :], hT_ps[i % 2][:, :].rearrange("p (c q) -> p c q", c=HC)).then_inc(s["hT_hi"], 1)

            def silu(n, i):
                act.wait_ge(s["gu_mm"], n + 1)
                if not isinstance(n, int) or n >= 2:
                    act.wait_ge(s["aT_mm"], n - 1)
                nc.scalar.activation(gated[:, i % 2, :], gu_ps[i % 2][:, 0:F], ACT.Silu).then_inc(s["silu"], 1)

            def result(n, i):
                act.wait_ge(s["y_mm"], n + 1)
                if not isinstance(n, int) or n >= 2:
                    act.wait_ge(s[f"y_out{i % 2}"], n // 2 * 16 if isinstance(n, int) else out_before(n, i))
                nc.scalar.copy(y[:, i % 2, :], y_ps[i % 2][:, :]).then_inc(s["y_sb"], 1)

            def out_before(n, i):
                return (turn[0] * (UE // 2) + i // 2) * 16 if i >= 0 else turn[0] * (UE // 2) * 16 - 16

            turn = [None]

            def tile(k, i):
                n = k * UE + i
                if i < UE - 1 or not isinstance(k, int) or k < NTE // UE - 1:
                    hT_high(n + 1, i + 1)
                silu(n, i)
                if not (first(k) and i == 0):
                    result(n - 1, i - 1)

            hT_high(0, 0)
            for k in (0,):
                for i in range(UE):
                    tile(k, i)
            with act.Fori(1, NTE // UE - 1) as k:
                turn[0] = k
                for i in range(UE):
                    tile(k, i)
            for i in range(UE):
                tile(NTE // UE - 1, i)
            result(NTE - 1, UE - 1)

        @block.vector
        def _(dve):
            step = Steps(dve, s["route"], 0)
            dve.wait_ge(s["const_in"], 16)
            order = const[:, C_FIRST:C_FIRST + E].unsqueeze(1).broadcast_to([P, NT, E])

            def spread(a):
                return a[:, :].unsqueeze(2).broadcast_to([P, NT, E])

            score, scratch, base = route
            for k in range(TOPK):
                src = logits if k == 0 else score
                step(nc.vector.tensor_reduce(row[k][:, :], src[:, :, :], AX.X, ALU.max))
                step(nc.vector.tensor_tensor(scratch[:, :, :], src[:, :, :], spread(row[k]), ALU.is_equal))
                step(nc.vector.tensor_tensor(scratch[:, :, :], scratch[:, :, :], order, ALU.mult))
                step(nc.vector.tensor_reduce(row[2][:, :], scratch[:, :, :], AX.X, ALU.max))
                step(nc.vector.tensor_tensor(hot[k][:, :, :], order, spread(row[2]), ALU.is_equal))
                if k == 0:
                    step(nc.vector.scalar_tensor_tensor(score[:, :, :], hot[0][:, :, :], MASKED, logits[:, :, :],
                                                        ALU.mult, ALU.add))
            nc.vector.tensor_tensor(row[2][:, :], row[1][:, :], row[0][:, :], ALU.subtract).then_inc(s["delta"], 1)
            nc.vector.tensor_tensor(score[:, :, :], hot[0][:, :, :], hot[1][:, :, :], ALU.add).then_inc(s["ranked"], 1)
            dve.wait_ge(s["gap"], 1)
            step(nc.vector.tensor_scalar(row[0][:, :], row[3][:, :], 1.0, None, ALU.add))
            step(nc.vector.reciprocal(weights[:, 0, :], row[0][:, :]))
            step(nc.vector.tensor_tensor(weights[:, 1, :], row[3][:, :], weights[:, 0, :], ALU.mult))
            dve.wait_ge(s["count_mm"], 1)
            rank, total = (count_ps[:, a:a + NT * E].rearrange("p (t e) -> p t e", e=E) for a in (0, NT * E))
            step(nc.vector.tensor_copy(scratch[:, :, :], total))
            a, b = scratch, base
            k = 1
            while k < NT:
                nc.vector.tensor_tensor(b[:, k:, :], a[:, k:, :], a[:, :NT - k, :], ALU.add)
                step(nc.vector.tensor_copy(b[:, :k, :], a[:, :k, :]))
                a, b, k = b, a, 2 * k
            step(nc.vector.tensor_scalar(count[:, :], a[:, NT - 1, :], float(P - 1), None, ALU.add))
            step(nc.vector.tensor_scalar(count[:, :], count[:, :], P.bit_length() - 1, None, ALU.arith_shift_right))
            step(nc.vector.tensor_copy(per[0][:, :], count[:, :]))
            step(nc.vector.tensor_copy(per[1][:, :], per[0][:, :]))
            c, e = per[1], per[2]
            k = 1
            while k < E:
                nc.vector.tensor_tensor(e[:, k:], c[:, k:], c[:, :E - k], ALU.add)
                step(nc.vector.tensor_copy(e[:, :k], c[:, :k]))
                c, e, k = e, c, 2 * k
            start = per[3]
            step(nc.vector.tensor_tensor(start[:, :], c[:, :], per[0][:, :], ALU.subtract))
            step(nc.vector.tensor_tensor(a[:, :, :], a[:, :, :], total, ALU.subtract))
            step(nc.vector.tensor_tensor(a[:, :, :], a[:, :, :], rank, ALU.add))
            step(nc.vector.scalar_tensor_tensor(a[:, :, :], start[:, :].unsqueeze(1).broadcast_to([P, NT, E]),
                                                float(P), a[:, :, :], ALU.mult, ALU.add))
            for k in range(TOPK):
                step(nc.vector.tensor_tensor(b[:, :, :], hot[k][:, :, :], a[:, :, :], ALU.mult))
                step(nc.vector.tensor_reduce(part_f[0][:, k, :], b[:, :, :], AX.X, ALU.add))
            step(nc.vector.tensor_copy(slot_i[:, :, :], part_f[0][:, :, :]))
            nc.vector.tensor_copy(slots[:, :, :], part_f[0][:, :, :])
            nc.vector.tensor_scalar(part[0][:, :, :], slot_i[:, :, :], P - 1, None, ALU.bitwise_and)
            step(nc.vector.tensor_scalar(part[1][:, :, :], slot_i[:, :, :], P.bit_length() - 1, None, ALU.arith_shift_right))
            nc.vector.tensor_copy(part_f[0][:, :, :], part[0][:, :, :])
            step(nc.vector.tensor_copy(part_f[1][:, :, :], part[1][:, :, :]))
            nc.vector.tensor_copy(token[:, :], const[:, C_TOKEN:C_TOKEN + NT])
            step(nc.vector.scalar_tensor_tensor(cell[:, :, :], part_f[0][:, :, :], float(NTE), part_f[1][:, :, :],
                                                ALU.mult, ALU.add))
            dve.nop().then_inc(s["slots_ready"], 1)
            tiles = const[:, C_TILE:C_TILE + NTE]
            step(nc.vector.tensor_scalar(expert_f[:, :], tiles, start[:, 1:2], None, ALU.is_ge))
            for k in range(2, E):
                step(nc.vector.scalar_tensor_tensor(expert_f[:, :], tiles, start[:, k:k + 1], expert_f[:, :],
                                                    ALU.is_ge, ALU.add))
            step(nc.vector.tensor_copy(expert[:, :], expert_f[:, :]))
            dve.nop().then_inc(s["slots_ready"], 1)
            for n in range(E * 2):
                dve.wait_ge(s["wgu_hi"], n + 1)
                nc.vector.tensor_tensor(wgu[1][:, n * HALF:(n + 1) * HALF, :], stage[n % 2],
                                        wgu[0][:, n * HALF:(n + 1) * HALF, :].bitcast(F32),
                                        ALU.subtract).then_inc(s["wgu_lo"], 1)

            def hT_low(n, i):
                dve.wait_ge(s["hT_hi"], n + 1)
                nc.vector.tensor_tensor(hT[1][:, i % 2, :, :], hT_ps[i % 2][:, :].rearrange("p (c q) -> p c q", c=HC),
                                        hT[0][:, i % 2, :, :].bitcast(F32), ALU.subtract).then_inc(s["hT_lo"], 1)

            def gate(n, i):
                dve.wait_ge(s["silu"], n + 1)
                nc.vector.tensor_tensor(gated[:, i % 2, :], gu_ps[i % 2][:, F:2 * F], gated[:, i % 2, :],
                                        ALU.mult).then_inc(s["gated"], 1)

            def aT_copy(n, i):
                dve.wait_ge(s["aT_mm"], n + 1)
                if not isinstance(n, int) or n >= 2:
                    dve.wait_ge(s["y_mm"], n - 1)
                nc.vector.tensor_copy(aT[:, i % 2, :, :], aT_ps[:, 0:F].rearrange("p (c q) -> p c q", c=FC)).then_inc(s["aT"], 1)

            def tile(k, i):
                n = k * UE + i
                if i < UE - 1 or not isinstance(k, int) or k < NTE // UE - 1:
                    hT_low(n + 1, i + 1)
                gate(n, i)
                aT_copy(n, i)

            hT_low(0, 0)
            for i in range(UE):
                tile(0, i)
            with dve.Fori(1, NTE // UE - 1) as k:
                for i in range(UE):
                    tile(k, i)
            for i in range(UE):
                tile(NTE // UE - 1, i)

        @block.tensor
        def _(pe):
            pe.wait_ge(s["const_in"], 16)
            pe.wait_ge(s["ones"], 1)
            pe.wait_ge(s["ranked"], 1)
            chosen = route[0][:, :, :].rearrange("p t e -> p (t e)")
            nc.tensor.matmul(count_ps[:, 0:NT * E], const[:, C_TRI:C_TRI + P], chosen, start=True, stop=True)
            nc.tensor.matmul(count_ps[:, NT * E:2 * NT * E], ones[:, :], chosen, start=True, stop=True).then_inc(s["count_mm"], 1)
            pe.wait_ge(s["wgu_lo"], 2 * E)
            pe.wait_ge(s["wd_in"], 16)
            pe.wait_ge(s["slots_ready"], 2)

            def transposes(k, n, i):
                pe.wait_ge(s[f"gather{i % UE}"], (k + i // UE) * 16 + 16)
                if not isinstance(n, int) or n >= 2:
                    pe.wait_ge(s["hT_lo"], n - 1)
                for c in range(HC):
                    last = nc.tensor.transpose(hT_ps[i % 2][:, c * P:(c + 1) * P], hs[:, i % UE, c * P:(c + 1) * P], ident)
                last.then_inc(s["hT_mm"], 1)

            def up(n, i, e):
                pe.wait_ge(s["hT_lo"], n + 1)
                if not isinstance(n, int) or n >= 2:
                    pe.wait_ge(s["gated"], n - 1)
                for c in range(HC):
                    a = both(hT, every, i % 2, c, every)
                    w = [wgu[j][:, bass.ds(e * HC + c, 1), :].rearrange("p a f -> p (a f)") for j in range(2)]
                    last = product(nc, gu_ps[i % 2][:, :], a, w, c == 0, c == HC - 1)
                last.then_inc(s["gu_mm"], 1)

            def down(n, i, e):
                pe.wait_ge(s["aT"], n + 1)
                if not isinstance(n, int) or n >= 2:
                    pe.wait_ge(s["y_sb"], n - 1)
                for c in range(FC):
                    last = nc.tensor.matmul(y_ps[i % 2][:, :], aT[:, i % 2, c, :],
                                            wd[:, bass.ds(e * FC + c, 1), :].rearrange("p a f -> p (a f)"),
                                            start=c == 0, stop=c == FC - 1)
                last.then_inc(s["y_mm"], 1)

            def gated_transposes(n, i):
                pe.wait_ge(s["gated"], n + 1)
                if not isinstance(n, int) or n >= 1:
                    pe.wait_ge(s["aT"], n)
                for c in range(FC):
                    last = nc.tensor.transpose(aT_ps[:, c * P:(c + 1) * P], gated[:, i % 2, c * P:(c + 1) * P], ident)
                last.then_inc(s["aT_mm"], 1)

            def expert_of(n):
                column = expert[0:1, n:n + 1] if isinstance(n, int) else expert[0:1, bass.ds(n, 1)]
                return pe.value_load(column, min_val=0, max_val=E - 1)

            def tile(k, i):
                n = k * UE + i
                up(n, i, expert_of(n))
                if i < UE - 1 or not isinstance(k, int) or k < NTE // UE - 1:
                    transposes(k, n + 1, i + 1)
                if not (first(k) and i == 0):
                    down(n - 1, i - 1, expert_of(n - 1))
                gated_transposes(n, i)

            transposes(0, 0, 0)
            for i in range(UE):
                tile(0, i)
            with pe.Fori(1, NTE // UE - 1) as k:
                for i in range(UE):
                    tile(k, i)
            for i in range(UE):
                tile(NTE // UE - 1, i)
            down(NTE - 1, UE - 1, expert_of(NTE - 1))


def combine(nc, sb, pb, sem, d, base_dram, y_dram, out_dram, slots, weights):
    base_v, out_v = (a.rearrange("(n p) d -> p n d", p=P) for a in (base_dram, out_dram))
    acc = sb("cb_acc", [P, 2, UF, H], F32)
    ys = sb("cb_y", [P, UF, TOPK, H], F32)
    index = sb("cb_index", [P, UF, TOPK], U32)
    names = """base_in0 base_in1 indexed gather0 gather1 gather2 gather3 added summed out0 out1 settled""".split()
    s = {n: sem("cb_" + n) for n in names}
    TURNS = NT // UF
    first = lambda g: isinstance(g, int) and g == 0

    def part(view, n):
        return view[:, n * UF:(n + 1) * UF, :] if isinstance(n, int) else view[:, bass.ds(n * UF, UF), :]

    block = nc.Block()
    with block:

        @block.sync
        def _(sp):
            def load(n, half):
                if not isinstance(n, int) or n >= 2:
                    sp.wait_ge(s[f"out{half}"], (n - half) * 8)
                sp.dma_start(acc[:, half, :, :], part(base_v, n)).then_inc(s[f"base_in{half}"], 16)

            def store(n, half):
                sp.wait_ge(s["summed"], n * UF + UF)
                sp.dma_start(part(out_v, n), acc[:, half, :, :]).then_inc(s[f"out{half}"], 16)

            load(0, 0)
            load(1, 1)
            with sp.Fori(0, TURNS // 2 - 1) as k:
                for half in range(2):
                    store(2 * k + half, half)
                    load(2 * k + 2 + half, half)
            for half in range(2):
                store(TURNS - 2 + half, half)
            for half in range(2):
                sp.wait_ge(s[f"out{half}"], TURNS // 2 * 16)

        @block.gpsimd
        def _(pool):
            def gathers(n):
                src = slots[:, :, n * UF:(n + 1) * UF] if isinstance(n, int) else slots[:, :, bass.ds(n * UF, UF)]
                for k in range(TOPK):
                    last = nc.gpsimd.tensor_copy(index[:, :, k], src[:, k, :])
                last.then_inc(s["indexed"], 1)
                for i in range(UF):
                    pool.wait_ge(s["indexed"], n + 1)
                    if not first(n):
                        pool.wait_ge(s["summed"], (n - 1) * UF + i + 1)
                    settle(pool, s["settled"])
                    for k in range(TOPK):
                        nc.gpsimd.indirect_dma_start(
                            ys[:, i, k, :], None, y_dram, bass.IndirectOffsetOnAxis(ap=index[:, i, k:k + 1], axis=0)
                        ).then_inc(s[f"gather{i}"], 16)

            gathers(0)
            with pool.Fori(1, TURNS) as n:
                for i in range(UF):
                    pool.wait_ge(s[f"gather{i}"], n * 32)
                settle(pool, s["settled"])
                gathers(n)

        @block.vector
        def _(dve):
            def turn(n, half, pair):
                dve.wait_ge(s[f"base_in{half}"], pair * 16 + 16)
                for i in range(UF):
                    dve.wait_ge(s[f"gather{i}"], n * 32 + 32)
                    for k in range(TOPK):
                        w = weights[:, k, bass.ds(n * UF + i, 1)]
                        last = nc.vector.scalar_tensor_tensor(acc[:, half, i, :], ys[:, i, k, :], w, acc[:, half, i, :],
                                                              ALU.mult, ALU.add)
                        if k == 0:
                            last.then_inc(s["added"], 1)
                            dve.wait_ge(s["added"], n * UF + i + 1)
                    last.then_inc(s["summed"], 1)

            with dve.Fori(0, TURNS // 2) as k:
                for half in range(2):
                    turn(2 * k + half, half, k)


def program(nc, d, out):
    def dram(name, *shape, dt=F32):
        return nc.dram_tensor(name, shape, dt).ap()

    x1, x2, h, base = (dram(n, T, H) for n in ("x1", "x2", "h", "base"))
    probs, nkv = dram("probs", NT, P, NH * S), dram("nkv", T, KVR)
    table, y = dram("table", P, NTE, dt=U32), dram("y", SLOTS, H)

    def memory(stack):
        taken = []

        def semaphore(name):
            taken.append(nc.alloc_semaphore(name))
            return taken[-1]

        def finish():
            if taken:
                nc.clear_and_free_semaphores(taken)
                nc.all_engine_barrier()

        stack.callback(finish)
        return (lambda name, shape, dt: stack.enter_context(nc.sbuf_tensor(name, shape, dt)),
                lambda name, shape, dt: stack.enter_context(nc.psum_tensor(name, shape, dt)),
                semaphore)

    with ExitStack() as stack:
        cross_attention(nc, *memory(stack), d, x1)
    with ExitStack() as stack:
        latent_scores(nc, *memory(stack), d, x1, probs, nkv)
    with ExitStack() as outer:
        sb, _, _ = memory(outer)
        logits = sb("logits", [P, NT, E], F32)
        slots = sb("slots", [P, TOPK, NT], U32)
        weights = sb("weights", [P, TOPK, NT], F32)
        with ExitStack() as stack:
            latent_values(nc, *memory(stack), d, x1, probs, nkv, x2, h, base, logits)
        with ExitStack() as stack:
            experts(nc, *memory(stack), d, h, table, y, logits, slots, weights)
        with ExitStack() as stack:
            combine(nc, *memory(stack), d, base, y, out, slots, weights)


def prepare(a):
    def chunks(w):
        return np.ascontiguousarray(w.reshape(-1, P, w.shape[-1]).transpose(1, 0, 2))

    a = {k: np.asarray(v) for k, v in a.items()}
    halves = a["L0_attn_W_krope"].reshape(H, RH, 2).transpose(0, 2, 1).reshape(H, ROPE)
    rope = a["L0_attn_W_dq_rope"].reshape(QR, NH // HJ, HJ, RH, 2).transpose(0, 1, 4, 2, 3).reshape(QR, NH * ROPE)
    gate_up = np.concatenate([a["L0_ffn_w_gate"], a["L0_ffn_w_up"]], axis=2).reshape(E, HC, P, 2 * F)
    return {
        "x": np.ascontiguousarray(a["x"].reshape(T, H)),
        "ctxT": np.ascontiguousarray(a["ctx_512"][:, :S, :].reshape(T, L).T),
        "const": constants(),
        "xa_WqT": chunks(a["L0_xattn_Wq"].T),
        "xa_WkvT": np.ascontiguousarray(a["L0_xattn_Wkv_expand"].T),
        "xa_WoutT": chunks(a["L0_xattn_Wout"].T),
        "q_scale": np.ascontiguousarray(a["L0_attn_q_scale"].reshape(QC, P).T),
        "kv_scale": a["L0_attn_kv_scale"].reshape(P, 1),
        "ls_Wc": chunks(np.concatenate([a["L0_attn_W_cq"], a["L0_attn_W_ckv"], halves], axis=1)),
        "ls_WdqT": np.ascontiguousarray(a["L0_attn_W_dq_nope"].reshape(QR, NH, NOPE).transpose(2, 1, 0)),
        "ls_WdkT": np.ascontiguousarray(a["L0_attn_W_dk_nope"].reshape(KVR, NH, NOPE).transpose(2, 1, 0)),
        "ls_Wrope": chunks(rope),
        "lv_WdvT": np.ascontiguousarray(a["L0_attn_W_dv"].reshape(KVR, NH, VD).transpose(2, 1, 0)),
        "lv_Wo": np.ascontiguousarray(a["L0_attn_W_o"].reshape(NH, VD, H).transpose(1, 0, 2)),
        "lv_Wgu": chunks(np.concatenate([a["L0_ffn_sw_gate"], a["L0_ffn_sw_up"]], axis=1)),
        "lv_Wd": chunks(a["L0_ffn_sw_down"]),
        "lv_Wr": chunks(a["L0_ffn_router_w"]),
        "rms_weight": a["L0_ffn_rms_weight"].reshape(1, H),
        "ex_Wgu": np.ascontiguousarray(gate_up.transpose(2, 0, 1, 3).reshape(P, E * HC, 2 * F)),
        "ex_Wd": np.ascontiguousarray(a["L0_ffn_w_down"].reshape(E, FC, P, H).transpose(2, 0, 1, 3).reshape(P, E * FC, H)),
    }


def kernel(**inputs):
    import concourse.bacc as bacc
    from concourse.bass_utils import run_bass_kernel_spmd

    nc = bacc.Bacc("TRN2", target_bir_lowering=False, num_devices=1)
    arrays = {f"in_{name}": a for name, a in prepare(inputs).items()}
    d = {name[3:]: nc.dram_tensor(name, a.shape, mybir.dt.from_np(a.dtype), kind="ExternalInput").ap()
         for name, a in arrays.items()}
    out = nc.dram_tensor("out", (T, H), F32, kind="ExternalOutput").ap()
    program(nc, d, out)
    r = run_bass_kernel_spmd(nc, [arrays], core_ids=[0])
    return r.results[0]["out"].reshape(B, S, H)
```

```python
from contextlib import ExitStack

import numpy as np

import concourse.bass as bass
from concourse import mybir

F32 = mybir.dt.float32
F32R = mybir.dt.float32r
I32 = mybir.dt.int32
U32 = mybir.dt.uint32
ALU = mybir.AluOpType
ACT = mybir.ActivationFunctionType
AX = mybir.AxisListType

B, S, H = 128, 32, 512
T = B * S
P = 128
HC = H // P
NT = T // P
TG = 4
G = NT // TG
GW = TG * P
BT = P // S
NH = 16
HD = H // NH
L = 128
QR, KVR, NOPE, ROPE, VD = 256, 128, 128, 64, 128
QC = QR // P
RH = ROPE // 2
CW = QR + KVR + ROPE
HJ = P // HD
E, F = 8, 256
FC = F // P
TOPK = 2
NTE = T * TOPK // P + E
SLOTS = NTE * P
LN_EPS = 1e-5
RMS_EPS = 1e-6
MASKED = -1e30
XA_SCALE = float(np.float32(1.0) / np.sqrt(np.float32(HD)))
MLA_SCALE = float(np.float32(1.0) / np.sqrt(np.float32(NOPE + ROPE)))
RSQRT_MAGIC = float(0x5F3759DF)

C_IDENT, C_TRI, C_MASK = 0, P, 2 * P
C_COS_D = C_MASK + S
C_SIN_D = C_COS_D + S
C_COS_P = C_SIN_D + S
C_SIN_P = C_COS_P + RH
C_TILE = C_SIN_P + RH
C_TOKEN = C_TILE + NTE
C_FIRST = C_TOKEN + NT
C_PAD = C_FIRST + E
C_END = C_PAD + 1


def constants():
    c = np.zeros((P, C_END), np.float32)
    row = np.arange(P)
    pos = row % S
    c[:, C_IDENT:C_IDENT + P] = np.eye(P)
    c[:, C_TRI:C_TRI + P] = row[:, None] < row[None, :]
    c[:, C_MASK:C_MASK + S] = np.where(np.arange(S)[None, :] <= pos[:, None], 0.0, MASKED)
    freq = (np.float32(1.0) / np.power(np.float32(10000.0), np.arange(RH, dtype=np.float32) * np.float32(2.0) / np.float32(ROPE))).astype(np.float32)
    angle = np.arange(S, dtype=np.float32)[:, None] * freq[None, :]
    cos, sin = np.cos(angle).astype(np.float32), np.sin(angle).astype(np.float32)
    c[:, C_COS_D:C_COS_D + S] = cos.T[row % RH]
    c[:, C_SIN_D:C_SIN_D + S] = sin.T[row % RH]
    c[:, C_COS_P:C_COS_P + RH] = cos[pos] / NH
    c[:, C_SIN_P:C_SIN_P + RH] = sin[pos] / NH
    c[:, C_TILE:C_TILE + NTE] = np.arange(NTE)[None, :]
    c[:, C_TOKEN:C_TOKEN + NT] = np.arange(NT)[None, :] * P + row[:, None]
    c[:, C_FIRST:C_FIRST + E] = E - np.arange(E)[None, :]
    c[:, C_PAD] = T + row
    return c


class Steps:

    def __init__(self, engine, semaphore, done_before):
        self.engine, self.semaphore, self.value = engine, semaphore, done_before

    def __call__(self, instruction):
        self.value = self.value + 1
        instruction.then_inc(self.semaphore, 1)
        self.engine.wait_ge(self.semaphore, self.value)


def settle(engine, semaphore):
    engine.nop().then_inc(semaphore, 1)


RSQRT_STEPS = 10


def rsqrt(nc, step, y, u, v):
    step(nc.vector.tensor_scalar(y.bitcast(I32), v.bitcast(I32), -0.5, RSQRT_MAGIC, ALU.mult, ALU.add))
    for _ in range(3):
        step(nc.vector.tensor_tensor(u, y, y, ALU.mult))
        step(nc.vector.scalar_tensor_tensor(u, u, -0.5, v, ALU.mult, ALU.mult))
        step(nc.vector.scalar_tensor_tensor(y, u, 1.5, y, ALU.add, ALU.mult))


def product(nc, out, a, b, first=True, last=True):
    nc.tensor.matmul(out, a[0], b[0], start=first, stop=False)
    nc.tensor.matmul(out, a[0], b[1], start=False, stop=False)
    return nc.tensor.matmul(out, a[1], b[0], start=False, stop=last)


def both(pair, *index):
    return pair[0][index], pair[1][index]


def dyn(g):
    return g if isinstance(g, int) else bass.ds(g, 1)


def group_of(view, g):
    if isinstance(g, int):
        return view[g]
    return view[bass.ds(g, 1)].rearrange("a p t d -> p (a t) d")


def columns_of(view, g):
    return view[:, g * GW:(g + 1) * GW] if isinstance(g, int) else view[:, bass.ds(g * GW, GW)]


def cross_attention(nc, sb, pb, sem, d, x1_dram):
    x_v = d["x"].rearrange("(g t p) d -> g p t d", t=TG, p=P)
    x1_v = x1_dram.rearrange("(g t p) d -> g p t d", t=TG, p=P)

    const = sb("xa_const", [P, C_END], F32)
    ident = const[:, C_IDENT:C_IDENT + P]
    mask = const[:, C_MASK:C_MASK + S]
    stage = sb("xa_stage", [P, HC, H], F32)
    wq = [sb(f"xa_wq{i}", [P, HC, H], F32R) for i in range(2)]
    wkv = [sb(f"xa_wkv{i}", [P, 2 * H], F32R) for i in range(2)]
    wo = [sb(f"xa_wo{i}", [P, HC, H], F32R) for i in range(2)]
    x_in = sb("xa_x", [P, TG, H], F32)
    xres = sb("xa_xres", [P, TG, H], F32)
    xn = sb("xa_xn", [P, TG, H], F32)
    xT = [sb(f"xa_xT{i}", [P, HC, GW], F32R) for i in range(2)]
    cin = sb("xa_ctx", [P, GW], F32)
    cT = [sb(f"xa_cT{i}", [P, GW], F32R) for i in range(2)]
    qT = sb("xa_qT", [P, HC, GW], F32)
    kbd = sb("xa_kbd", [P, TG * BT, HC, P], F32)
    val = sb("xa_v", [P, TG, H], F32)
    sc = sb("xa_sc", [P, 2, NH, S], F32)
    ex = sb("xa_ex", [P, 2, NH, S], F32)
    smx = sb("xa_max", [P, 2, NH], F32)
    ssum = sb("xa_sum", [P, NH], F32)
    srec = sb("xa_rec", [P, 2, NH], F32)
    pTc = sb("xa_pTc", [P, 2, NH, S], F32)
    pT = sb("xa_pT", [P, TG, NH, P], F32)
    oT = [sb(f"xa_oT{i}", [P, HC, P], F32R) for i in range(2)]
    st = sb("xa_st", [P, TG, 6], F32)
    mv = sb("xa_mv", [P, TG, 2], F32)
    var = sb("xa_var", [P, TG], F32)
    rstd = sb("xa_rstd", [P, TG], F32)
    tmp = sb("xa_tmp", [P, TG], F32)
    nbias = sb("xa_nb", [P, TG], F32)

    ring = [pb(f"xa_ring{i}", [P, H], F32) for i in range(4)]
    s_ps = [pb(f"xa_s{i}", [P, H], F32) for i in range(2)]
    pv_ps = pb("xa_pv", [P, H], F32)
    out_ps = pb("xa_out", [P, H], F32)

    k_ps = [s_ps[0], s_ps[1], pv_ps, out_ps]

    names = """const_in wkv_in wq_in wo_in x_in ctx_in xres_in x1_out zeroed w_hi w_lo moments stats xn ctx_hi ctx_lo
        xT_mm xT_hi xT_lo q_mm q_sb k_mm k_bd v_mm v_sb s_mm s_read s_max s_sub s_exp s_rec s_prob pT expanded
        pv_mm o_hi o_lo out_mm x1 ln_step sm_step settled settled_pool""".split()
    s = {n: sem("xa_" + n) for n in names}
    weights = [("xa_WkvT", "wkv_in", wkv[0][:, :], wkv[1][:, :], xres[:, 0:2, :].rearrange("p a b -> p (a b)")),
               ("xa_WqT", "wq_in", wq[0][:, :, :], wq[1][:, :, :], stage[:, :, :]),
               ("xa_WoutT", "wo_in", wo[0][:, :, :], wo[1][:, :, :], stage[:, :, :])]

    def first(g):
        return isinstance(g, int) and g == 0

    def heads(a):
        return a.unsqueeze(2).broadcast_to([P, NH, S])

    def place_keys(copy, m, js):
        for j in js:
            rows = slice(j * HD, (j + 1) * HD)
            last = copy(kbd[rows, :, m, j * S:(j + 1) * S], k_ps[m][rows, :].rearrange("p (b k) -> p b k", k=S))
        last.then_inc(s["k_bd"], 1)

    block = nc.Block()
    with block:

        @block.sync
        def _(sp):
            def load_x(g):
                if not first(g):
                    sp.wait_ge(s["xn"], g * TG)
                sp.dma_start(x_in[:, :, :], group_of(x_v, g)).then_inc(s["x_in"], 16)

            def load_context(g):
                if not first(g):
                    sp.wait_ge(s["ctx_lo"], g)
                sp.dma_start(cin[:, :], columns_of(d["ctxT"], g)).then_inc(s["ctx_in"], 16)

            def store(g):
                sp.wait_ge(s["x1"], g * TG + TG + 1)
                sp.dma_start(group_of(x1_v, g), xres[:, :, :]).then_inc(s["x1_out"], 16)

            def residual(g):
                if not first(g):
                    sp.wait_ge(s["x1_out"], g * 16)
                sp.dma_start(xres[:, :, :], group_of(x_v, g)).then_inc(s["xres_in"], 16)

            load_x(0)
            sp.dma_start(const[:, :], d["const"]).then_inc(s["const_in"], 16)
            load_context(0)
            for n, (name, loaded, _, _, dst) in enumerate(weights):
                if n == 2:
                    sp.wait_ge(s["w_lo"], 2)
                sp.dma_start(dst, d[name]).then_inc(s[loaded], 16)
                if n == 1:
                    load_x(1)
            residual(0)
            load_context(1)
            load_x(2)
            load_context(2)
            with sp.Fori(2, G - 1) as g:
                load_x(g + 1)
                store(g - 2)
                load_context(g + 1)
                residual(g - 1)
            store(G - 3)
            residual(G - 2)
            store(G - 2)
            residual(G - 1)
            store(G - 1)
            sp.wait_ge(s["x1_out"], G * 16)

        @block.gpsimd
        def _(pool):
            nc.gpsimd.memset(kbd[:, :, :, :], 0.0).then_inc(s["zeroed"], 1)

            def split_context(g):
                pool.wait_ge(s["ctx_in"], g * 16 + 16)
                if not first(g):
                    pool.wait_ge(s["v_mm"], g * TG)
                settle(pool, s["settled_pool"])
                nc.gpsimd.tensor_copy(cT[0][:, :], cin[:, :]).then_inc(s["ctx_hi"], 1)
                pool.wait_ge(s["ctx_hi"], g + 1)
                nc.gpsimd.tensor_tensor(cT[1][:, :], cin[:, :], cT[0][:, :].bitcast(F32),
                                        ALU.subtract).then_inc(s["ctx_lo"], 1)

            def subtract(g, t):
                pool.wait_ge(s["s_max"], g * TG + t + 1)
                nc.gpsimd.tensor_tensor(sc[:, t % 2], sc[:, t % 2], heads(smx[:, t % 2]),
                                        ALU.subtract).then_inc(s["s_sub"], 1)

            def normalise(g, t):
                pool.wait_ge(s["s_rec"], g * TG + t + 1)
                nc.gpsimd.tensor_tensor(ex[:, t % 2], ex[:, t % 2], heads(srec[:, t % 2]),
                                        ALU.mult).then_inc(s["s_prob"], 1)

            def body(g, back, ahead):
                if back:
                    normalise(g - 1, 2)
                    normalise(g - 1, 3)
                subtract(g, 0)
                subtract(g, 1)
                normalise(g, 0)
                subtract(g, 2)
                normalise(g, 1)
                subtract(g, 3)
                if ahead:
                    split_context(g + 1)

            split_context(0)
            nc.gpsimd.memset(pT[:, :, :, :], 0.0).then_inc(s["zeroed"], 1)
            body(0, False, True)
            with pool.Fori(1, G - 1) as g:
                body(g, True, True)
            body(G - 1, True, False)
            normalise(G - 1, 2)
            normalise(G - 1, 3)

        @block.scalar
        def _(act):
            def normalise(g, t):
                if t == 0:
                    act.wait_ge(s["stats"], g + 1)
                    if not first(g):
                        act.wait_ge(s["xT_mm"], g * TG)
                nc.scalar.activation(xn[:, t, :], x_in[:, t, :], ACT.Identity, bias=nbias[:, t:t + 1],
                                     scale=rstd[:, t:t + 1]).then_inc(s["xn"], 1)

            def weight_high(n):
                _, loaded, hi, _, src = weights[n]
                act.wait_ge(s[loaded], 16)
                nc.scalar.copy(hi, src).then_inc(s["w_hi"], 1)

            def x_high(g, t):
                act.wait_ge(s["xT_mm"], g * TG + t + 1)
                nc.scalar.copy(xT[0][:, :, t * P:(t + 1) * P],
                               ring[t][:, :].rearrange("p (c q) -> p c q", c=HC)).then_inc(s["xT_hi"], 1)

            def keys(g, m):
                act.wait_ge(s["k_mm"], g * HC + m + 1)
                place_keys(nc.scalar.copy, m, (0, 1))

            def query(g, m):
                act.wait_ge(s["q_mm"], g * HC + m + 1)
                nc.scalar.copy(qT[:, m, :], ring[m][:, :]).then_inc(s["q_sb"], 1)

            def exponent(g, t):
                act.wait_ge(s["s_sub"], g * TG + t + 1)
                if not (first(g) and t < 2):
                    act.wait_ge(s["pT"], g * TG + t - 1)
                nc.scalar.activation(ex[:, t % 2], sc[:, t % 2], ACT.Exp, scale=XA_SCALE).then_inc(s["s_exp"], 1)

            def expand(g, t):
                act.wait_ge(s["pT"], g * TG + t + 1)
                act.wait_ge(s["pv_mm"], g * TG + t + 1)
                for b in range(BT):
                    rows = slice(b * S, (b + 1) * S)
                    last = nc.scalar.copy(pT[rows, t, :, b * S:(b + 1) * S], pTc[rows, t % 2])
                last.then_inc(s["expanded"], 1)

            def value(g, t):
                act.wait_ge(s["v_mm"], g * TG + t + 1)
                nc.scalar.copy(val[:, t, :], ring[t][:, :]).then_inc(s["v_sb"], 1)

            def out_high(g, t):
                act.wait_ge(s["pv_mm"], (g + 1) * TG + t + 1)
                nc.scalar.copy(oT[0][:, :, :], pv_ps[:, :].rearrange("p (c q) -> p c q", c=HC)).then_inc(s["o_hi"], 1)

            def body(g, back, ahead):
                x_high(g, 0)
                x_high(g, 1)
                if back:
                    exponent(g - 1, 3)
                x_high(g, 2)
                x_high(g, 3)
                if first(g):
                    act.wait_ge(s["zeroed"], 1)
                keys(g, 0)
                keys(g, 1)
                query(g, 0)
                if back:
                    expand(g - 1, 1)
                keys(g, 2)
                query(g, 1)
                keys(g, 3)
                query(g, 2)
                if back:
                    expand(g - 1, 2)
                query(g, 3)
                if first(g):
                    weight_high(2)
                for t in range(TG):
                    if back:
                        out_high(g - 1, t)
                    value(g, t)
                    if t == 0 and back:
                        expand(g - 1, 3)
                    if t > 0:
                        exponent(g, t - 1)
                    if t >= 2 and ahead:
                        normalise(g + 1, 2 * t - 4)
                        normalise(g + 1, 2 * t - 3)
                if first(g):
                    act.wait_ge(s["zeroed"], 2)
                expand(g, 0)

            for t in range(TG):
                normalise(0, t)
            weight_high(0)
            weight_high(1)
            body(0, False, True)
            with act.Fori(1, G - 1) as g:
                body(g, True, True)
            body(G - 1, True, False)
            exponent(G - 1, 3)
            for t in range(TG):
                if t > 0:
                    expand(G - 1, t)
                out_high(G - 1, t)

        @block.vector
        def _(dve):
            dve.nop().then_inc(s["o_lo"], 1)
            dve.nop().then_inc(s["x1"], 1)

            def moments(g):
                dve.wait_ge(s["x_in"], g * 16 + 16)
                for t in range(TG):
                    last = nc.vector.bn_stats(st[:, t, :], x_in[:, t, :])
                last.then_inc(s["moments"], 1)

            def statistics(g):
                step = Steps(dve, s["ln_step"], g * (RSQRT_STEPS + 3))
                dve.wait_ge(s["moments"], g + 1)
                if not first(g):
                    dve.wait_ge(s["xn"], g * TG)
                settle(dve, s["settled"])
                for t in range(TG):
                    last = nc.vector.bn_aggr(mv[:, t, :], st[:, t, :])
                step(last)
                step(nc.vector.tensor_scalar(var[:, :], mv[:, :, 1], LN_EPS, None, ALU.add))
                rsqrt(nc, step, rstd[:, :], tmp[:, :], var[:, :])
                step(nc.vector.scalar_tensor_tensor(nbias[:, :], mv[:, :, 0], -1.0, rstd[:, :], ALU.mult, ALU.mult))
                dve.nop().then_inc(s["stats"], 1)

            def weight_low(n):
                _, _, hi, lo, src = weights[n]
                dve.wait_ge(s["w_hi"], n + 1)
                nc.vector.tensor_tensor(lo, src, hi.bitcast(F32), ALU.subtract).then_inc(s["w_lo"], 1)

            def x_low(g, t):
                dve.wait_ge(s["xT_hi"], g * TG + t + 1)
                part = (slice(None), slice(None), slice(t * P, (t + 1) * P))
                nc.vector.tensor_tensor(xT[1][part], ring[t][:, :].rearrange("p (c q) -> p c q", c=HC),
                                        xT[0][part].bitcast(F32), ALU.subtract).then_inc(s["xT_lo"], 1)

            def keys(g, m):
                dve.wait_ge(s["k_mm"], g * HC + m + 1)
                place_keys(nc.vector.tensor_copy, m, (2, 3))

            def maximum(g, t):
                dve.wait_ge(s["s_mm"], g * TG + t + 1)
                if not (first(g) and t < 2):
                    dve.wait_ge(s["s_exp"], g * TG + t - 1)
                nc.vector.tensor_tensor(sc[:, t % 2], s_ps[t % 2][:, :].rearrange("p (h k) -> p h k", h=NH),
                                        mask.unsqueeze(1).broadcast_to([P, NH, S]), ALU.add).then_inc(s["s_read"], 1)
                dve.wait_ge(s["s_read"], g * TG + t + 1)
                nc.vector.tensor_reduce(smx[:, t % 2], sc[:, t % 2], AX.X, ALU.max).then_inc(s["s_max"], 1)

            def total(g, t):
                dve.wait_ge(s["s_exp"], g * TG + t + 1)
                nc.vector.tensor_reduce(ssum[:, :], ex[:, t % 2], AX.X, ALU.add).then_inc(s["sm_step"], 1)
                dve.wait_ge(s["sm_step"], g * TG + t + 1)
                nc.vector.reciprocal(srec[:, t % 2], ssum[:, :]).then_inc(s["s_rec"], 1)

            def turn(g, t):
                dve.wait_ge(s["s_prob"], g * TG + t + 1)
                if not (first(g) and t < 2):
                    dve.wait_ge(s["expanded"], g * TG + t - 1)
                nc.vector.transpose(pTc[:, t % 2], ex[:, t % 2]).then_inc(s["pT"], 1)

            def out_low(g, t):
                dve.wait_ge(s["o_hi"], g * TG + t + 1)
                nc.vector.tensor_tensor(oT[1][:, :, :], pv_ps[:, :].rearrange("p (c q) -> p c q", c=HC),
                                        oT[0][:, :, :].bitcast(F32), ALU.subtract).then_inc(s["o_lo"], 1)

            def add(g, t):
                if t == 0:
                    dve.wait_ge(s["xres_in"], g * 16 + 16)
                dve.wait_ge(s["out_mm"], g * TG + t + 1)
                nc.vector.tensor_tensor(xres[:, t, :], out_ps[:, :], xres[:, t, :], ALU.add).then_inc(s["x1"], 1)

            def body(g, back, ahead):
                if back:
                    total(g - 1, 2)
                for t in range(TG):
                    x_low(g, t)
                if back:
                    turn(g - 1, 2)
                if first(g):
                    dve.wait_ge(s["zeroed"], 1)
                keys(g, 0)
                keys(g, 1)
                if back:
                    total(g - 1, 3)
                keys(g, 2)
                keys(g, 3)
                if back:
                    turn(g - 1, 3)
                if first(g):
                    weight_low(2)
                for t in range(TG):
                    if back:
                        out_low(g - 1, t)
                    if t >= 2:
                        total(g, t - 2)
                    maximum(g, t)
                    if t >= 2:
                        turn(g, t - 2)
                    if back:
                        add(g - 1, t)
                    if t == 0 and ahead:
                        moments(g + 1)
                    if t == 1 and ahead:
                        statistics(g + 1)

            moments(0)
            statistics(0)
            weight_low(0)
            weight_low(1)
            body(0, False, True)
            with dve.Fori(1, G - 1) as g:
                body(g, True, True)
            body(G - 1, True, False)
            total(G - 1, 2)
            turn(G - 1, 2)
            total(G - 1, 3)
            turn(G - 1, 3)
            for t in range(TG):
                out_low(G - 1, t)
                add(G - 1, t)

        @block.tensor
        def _(pe):
            pe.nop().then_inc(s["pv_mm"], TG)
            pe.wait_ge(s["const_in"], 16)

            def transposes(g, t):
                pe.wait_ge(s["xn"], g * TG + t + 1)
                if not first(g):
                    pe.wait_ge(s["v_sb"], (g - 1) * TG + t + 1)
                for c in range(HC):
                    last = nc.tensor.transpose(ring[t][:, c * P:(c + 1) * P], xn[:, t, c * P:(c + 1) * P], ident)
                last.then_inc(s["xT_mm"], 1)

            def keys(g, m):
                if m == 0:
                    pe.wait_ge(s["ctx_lo"], g + 1)
                if not first(g):
                    name, value = [("s_read", g * TG - 1), ("s_read", g * TG), ("o_lo", (g - 1) * TG + 1),
                                   ("x1", (g - 1) * TG + 1)][m]
                    pe.wait_ge(s[name], value)
                product(nc, k_ps[m][:, :], both(wkv, slice(None), slice(m * P, (m + 1) * P)),
                        both(cT, slice(None), slice(None))).then_inc(s["k_mm"], 1)

            def queries(g, m):
                pe.wait_ge(s["xT_lo"], g * TG + TG)
                for c in range(HC):
                    last = product(nc, ring[m][:, :], both(wq, slice(None), c, slice(m * P, (m + 1) * P)),
                                   both(xT, slice(None), c, slice(None)), c == 0, c == HC - 1)
                last.then_inc(s["q_mm"], 1)

            def values(g, t):
                pe.wait_ge(s["q_sb"], g * HC + t + 1)
                product(nc, ring[t][:, :], both(cT, slice(None), slice(t * P, (t + 1) * P)),
                        both(wkv, slice(None), slice(H, 2 * H))).then_inc(s["v_mm"], 1)

            def scores(g, t):
                if t == 0:
                    pe.wait_ge(s["q_sb"], g * HC + HC)
                if t >= 2:
                    pe.wait_ge(s["s_read"], g * TG + t - 1)
                for b in range(BT):
                    token = t * P + b * S
                    for m in range(HC):
                        last = nc.tensor.matmul(s_ps[t % 2][b * S:(b + 1) * S, m * P:(m + 1) * P],
                                                qT[:, m, token:token + S], kbd[:, t * BT + b, m, :],
                                                start=True, stop=True)
                last.then_inc(s["s_mm"], 1)

            def weighted(g, t):
                pe.wait_ge(s["expanded"], g * TG + t + 1)
                if t == 0:
                    pe.wait_ge(s["v_sb"], g * TG + TG)
                pe.wait_ge(s["o_lo"], g * TG + t + 1)
                for m in range(HC):
                    for j in range(HJ):
                        h = m * HJ + j
                        last = nc.tensor.matmul(pv_ps[j * HD:(j + 1) * HD, m * P:(m + 1) * P],
                                                val[:, t, h * HD:(h + 1) * HD], pT[:, t, h, :],
                                                start=True, stop=True)
                last.then_inc(s["pv_mm"], 1)

            def outputs(g, t):
                pe.wait_ge(s["o_lo"], g * TG + t + 2)
                pe.wait_ge(s["x1"], g * TG + t + 1)
                for m in range(HC):
                    last = product(nc, out_ps[:, :], both(oT, slice(None), m, slice(None)),
                                   both(wo, slice(None), m, slice(None)), m == 0, m == HC - 1)
                last.then_inc(s["out_mm"], 1)

            def body(g, back):
                for t in range(TG):
                    transposes(g, t)
                if first(g):
                    pe.wait_ge(s["w_lo"], 1)
                for m in range(HC):
                    keys(g, m)
                if first(g):
                    pe.wait_ge(s["w_lo"], 2)
                for m in range(HC):
                    queries(g, m)
                pe.wait_ge(s["k_bd"], (g * HC + HC) * 2)
                for t in range(TG):
                    if back:
                        weighted(g - 1, t)
                    values(g, t)
                    scores(g, t)
                    if back:
                        outputs(g - 1, t)

            body(0, False)
            pe.wait_ge(s["w_lo"], 3)
            with pe.Fori(1, G) as g:
                body(g, True)
            for t in range(TG):
                weighted(G - 1, t)
                outputs(G - 1, t)


RMS_STEPS = RSQRT_STEPS


def latent_scores(nc, sb, pb, sem, d, x1_dram, probs_dram, nkv_dram):
    x_v = x1_dram.rearrange("(g t p) d -> g p t d", t=TG, p=P)
    nkv_v = nkv_dram.rearrange("(g t p) d -> g p t d", t=TG, p=P)
    probs_v = probs_dram.rearrange("(g t) p n -> g p t n", t=TG)

    const = sb("ls_const", [P, C_END], F32)
    ident = const[:, C_IDENT:C_IDENT + P]
    mask = const[:, C_MASK:C_MASK + S]
    cos_d, sin_d = (const[:, c:c + S].unsqueeze(1).broadcast_to([P, GW // S, S]) for c in (C_COS_D, C_SIN_D))
    cos_p, sin_p = (const[:, c:c + RH].unsqueeze(1).broadcast_to([P, TG, RH]) for c in (C_COS_P, C_SIN_P))
    qscale = sb("ls_qscale", [P, QC], F32)
    kvscale = sb("ls_kvscale", [P, 1], F32)
    wc = [sb(f"ls_wc{i}", [P, HC, CW], F32R) for i in range(2)]
    wabs = [sb(f"ls_wabs{i}", [P, QC, NH * KVR], F32R) for i in range(2)]
    wrope = [sb(f"ls_wrope{i}", [P, QC, NH * ROPE], F32R) for i in range(2)]
    x_in = sb("ls_x", [P, TG, H], F32)
    xn = sb("ls_xn", [P, TG, H], F32)
    xT = [sb(f"ls_xT{i}", [P, HC, GW], F32R) for i in range(2)]
    craw = sb("ls_craw", [P, TG, CW], F32)
    kprod = [sb(f"ls_kprod{i}", [P, TG, RH], F32) for i in range(4)]
    cqT = [sb(f"ls_cqT{i}", [P, QC, GW], F32R) for i in range(2)]
    nkvT = sb("ls_nkvT", [P, GW], F32)
    krz = [sb(f"ls_krz{i}", [P, HJ, GW], F32) for i in range(2)]
    qr = [sb(f"ls_qr{i}", [P, NH // HJ, GW], F32) for i in range(2)]
    rot = [sb(f"ls_rot{i}", [P, GW], F32) for i in range(4)]
    krep = [r[:, :].rearrange("p (t j r) -> p t j r", t=TG, j=HJ) for r in rot[0:2]]
    qa = sb("ls_qa", [P, NH, GW], F32)
    sc = sb("ls_sc", [P, 2, NH, S], F32)
    ex = sb("ls_ex", [P, 2, NH, S], F32)
    smx = sb("ls_max", [P, 2, NH], F32)
    ssum = sb("ls_sum", [P, NH], F32)
    srec = sb("ls_rec", [P, 2, NH], F32)
    pT = sb("ls_pT", [P, TG, NH * S], F32)
    st = sb("ls_st", [P, TG, 6], F32)
    mv = sb("ls_mv", [P, TG, 2], F32)
    var = sb("ls_var", [P, TG], F32)
    rstd = sb("ls_rstd", [P, TG], F32)
    tmp = sb("ls_tmp", [P, TG], F32)
    nbias = sb("ls_nb", [P, TG], F32)
    squares = sb("ls_squares", [P, QR], F32)
    sumsq = sb("ls_sumsq", [P, 2, TG], F32)
    rvar = sb("ls_rvar", [P, 2, TG], F32)
    rrms = sb("ls_rrms", [P, 2, TG], F32)
    rtmp = sb("ls_rtmp", [P, 2, TG], F32)

    wdq_st, wdk_st = qa[:, :, 0:QR], qa[:, :, QR:QR + KVR]
    wrope_st = qr[0][:, :, :].rearrange("p a b -> p (a b)").rearrange("p (c n) -> p c n", c=QC)
    wc_st = qr[1][:, :, 0:CW]

    ring = [pb(f"ls_ring{i}", [P, H], F32) for i in range(4)]
    s_ps = [pb(f"ls_s{i}", [P, H], F32) for i in range(2)]
    spare = [pb(f"ls_spare{i}", [P, H], F32) for i in range(2)]
    qa_ps = [ring[3], ring[0], spare[0], spare[1]]
    fold_ps = [spare[0], spare[1], s_ps[0], s_ps[1]]

    names = """const_in wc_in wdq_in wrope_in x_in nkv_out probs_out zeroed wc_hi wc_lo wrope_hi wrope_lo
        wabs_mm wabs_hi wabs_lo stats xn xT_mm xT_hi xT_lo c_mm c_sq c_raw c_ready cq_T nkv_T kr_T cq_hi cq_lo
        nkv_sb kr_sb rope_mm rope_prod rope_sb qa_mm qa_sb s_mm s_out s_masked s_max s_sub s_exp s_sum s_rec s_prob pT
        ln_step rms_step key_step settled""".split()
    s = {n: sem("ls_" + n) for n in names}
    every = slice(None)

    def first(g):
        return isinstance(g, int) and g == 0

    def heads(a):
        return a.unsqueeze(2).broadcast_to([P, NH, S])

    block = nc.Block()
    with block:

        @block.sync
        def _(sp):
            sp.nop().then_inc(s["probs_out"], 16)

            def loads(g):
                if not first(g):
                    sp.wait_ge(s["xn"], g * TG)
                sp.dma_start(x_in[:, :, :], group_of(x_v, g)).then_inc(s["x_in"], 16)

            def stores(g):
                sp.wait_ge(s["c_ready"], g + 1)
                sp.dma_start(group_of(nkv_v, g), craw[:, :, QR:QR + KVR]).then_inc(s["nkv_out"], 16)

            def probs(g):
                sp.wait_ge(s["pT"], g * TG + TG + 2)
                sp.dma_start(group_of(probs_v, g), pT[:, :, :]).then_inc(s["probs_out"], 16)

            loads(0)
            sp.dma_start(const[:, :], d["const"]).then_inc(s["const_in"], 16)
            sp.dma_start(qscale[:, :], d["q_scale"]).then_inc(s["const_in"], 16)
            sp.dma_start(kvscale[:, :], d["kv_scale"]).then_inc(s["const_in"], 16)
            sp.dma_start(wc_st, d["ls_Wc"]).then_inc(s["wc_in"], 16)
            sp.dma_start(wdq_st, d["ls_WdqT"]).then_inc(s["wdq_in"], 16)
            sp.dma_start(wdk_st, d["ls_WdkT"]).then_inc(s["wdq_in"], 16)
            sp.dma_start(wrope_st, d["ls_Wrope"]).then_inc(s["wrope_in"], 16)
            loads(1)
            stores(0)
            with sp.Fori(1, G - 1) as g:
                loads(g + 1)
                stores(g)
                probs(g - 1)
            stores(G - 1)
            probs(G - 2)
            probs(G - 1)
            sp.wait_ge(s["nkv_out"], G * 16)
            sp.wait_ge(s["probs_out"], G * 16 + 16)

        @block.gpsimd
        def _(pool):
            for i in range(2):
                nc.gpsimd.memset(krz[i][:, :, :], 0.0).then_inc(s["zeroed"], 1)

            def rotate(g, i):
                pool.wait_ge(s["rope_prod"], g * 4 + i + 1)
                nc.gpsimd.tensor_tensor(qr[0][:, i, :], rot[0][:, :], rot[1][:, :], ALU.subtract)
                nc.gpsimd.tensor_tensor(qr[1][:, i, :], rot[2][:, :], rot[3][:, :], ALU.add).then_inc(s["rope_sb"], 1)

            def subtract(g, t):
                pool.wait_ge(s["s_max"], g * TG + t + 1)
                nc.gpsimd.tensor_tensor(sc[:, t % 2], sc[:, t % 2], heads(smx[:, t % 2]),
                                        ALU.subtract).then_inc(s["s_sub"], 1)

            def normalise(g, t):
                pool.wait_ge(s["s_rec"], g * TG + t + 1)
                nc.gpsimd.tensor_tensor(ex[:, t % 2], ex[:, t % 2], heads(srec[:, t % 2]),
                                        ALU.mult).then_inc(s["s_prob"], 1)

            def softmax(g, t):
                subtract(g, t)
                if t:
                    normalise(g, t - 1)

            def body(g, back):
                if back:
                    for t in range(TG - 1):
                        softmax(g - 1, t)
                    subtract(g - 1, 3)
                rotate(g, 0)
                if back:
                    normalise(g - 1, 2)
                rotate(g, 1)
                if back:
                    normalise(g - 1, 3)
                rotate(g, 2)
                rotate(g, 3)

            body(0, False)
            with pool.Fori(1, G) as g:
                body(g, True)
            for t in range(TG):
                softmax(G - 1, t)
            normalise(G - 1, 3)

        @block.scalar
        def _(act):
            def normalise(g):
                act.wait_ge(s["stats"], g + 1)
                if not first(g):
                    act.wait_ge(s["xT_mm"], g * TG)
                for t in range(TG):
                    nc.scalar.activation(xn[:, t, :], x_in[:, t, :], ACT.Identity, bias=nbias[:, t:t + 1],
                                         scale=rstd[:, t:t + 1]).then_inc(s["xn"], 1)

            act.nop().then_inc(s["s_exp"], 2)

            def exponent(g, t):
                act.wait_ge(s["s_sub"], g * TG + t + 1)
                act.wait_ge(s["pT"], g * TG + t + 1)
                nc.scalar.activation(ex[:, t % 2], sc[:, t % 2], ACT.Exp, scale=MLA_SCALE).then_inc(s["s_exp"], 1)

            def weights_high():
                for n in range(QC * 4):
                    c, q = divmod(n, 4)
                    act.wait_ge(s["wabs_mm"], n + 1)
                    nc.scalar.activation(wabs[0][:, c, q * H:(q + 1) * H], fold_ps[n % 4][:, :], ACT.Copy,
                                         scale=qscale[:, c:c + 1]).then_inc(s["wabs_hi"], 1)
                act.wait_ge(s["wrope_in"], 16)
                for c in range(QC):
                    nc.scalar.activation(wrope[0][:, c, :], wrope_st[:, c, :], ACT.Copy,
                                         scale=qscale[:, c:c + 1]).then_inc(s["wrope_hi"], 1)

            def body(g, back, ahead):
                for t in range(TG):
                    act.wait_ge(s["xT_mm"], g * TG + t + 1)
                    nc.scalar.copy(xT[0][:, :, t * P:(t + 1) * P],
                                   ring[t][:, :].rearrange("p (c q) -> p c q", c=HC)).then_inc(s["xT_hi"], 1)
                if back:
                    exponent(g - 1, 0)
                for t in range(TG):
                    act.wait_ge(s["c_mm"], g * TG + t + 1)
                    if t == 0 and not first(g):
                        act.wait_ge(s["kr_T"], g * 2)
                        act.wait_ge(s["nkv_out"], g * 16)
                    for n, (a, z) in enumerate(((0, QR), (QR, QR + KVR))):
                        if not (first(g) and t == 0 and n == 0):
                            act.wait_ge(s["c_sq"], (g * TG + t) * 2 + n)
                        nc.scalar.activation(squares[:, 0:z - a], ring[t][:, a:z], ACT.Square,
                                             accum_out=sumsq[:, n, t:t + 1]).then_inc(s["c_sq"], 1)
                    nc.scalar.copy(craw[:, t, :], ring[t][:, 0:CW]).then_inc(s["c_raw"], 1)
                if first(g):
                    weights_high()
                if back:
                    exponent(g - 1, 1)
                for n in range(2):
                    act.wait_ge(s["cq_T"], g * 2 + n + 1)
                    tok = slice(n * 2 * P, (n + 1) * 2 * P)
                    nc.scalar.copy(cqT[0][:, :, tok],
                                   ring[n][:, :].rearrange("p (t c q) -> p c t q", t=2, c=QC)
                                   ).then_inc(s["cq_hi"], 1)
                act.wait_ge(s["nkv_T"], g + 1)
                nc.scalar.activation(nkvT[:, :], ring[2][:, :], ACT.Copy, scale=kvscale[:, 0:1]).then_inc(s["nkv_sb"], 1)
                if back:
                    exponent(g - 1, 2)
                if first(g):
                    act.wait_ge(s["zeroed"], 2)
                for n in range(2):
                    act.wait_ge(s["kr_T"], g * 2 + n + 1)
                    for j in range(HJ):
                        rows = slice(j * RH, (j + 1) * RH)
                        last = nc.scalar.copy(krz[n][rows, j, :], ring[(3, 0)[n]][rows, :])
                    last.then_inc(s["kr_sb"], 1)
                for h in range(NH):
                    act.wait_ge(s["qa_mm"], g * NH + h + 1)
                    nc.scalar.copy(qa[:, h, :], qa_ps[h % 4][:, :]).then_inc(s["qa_sb"], 1)
                    if back and h == 1:
                        exponent(g - 1, 3)
                    if h == 11 and ahead:
                        normalise(g + 1)

            normalise(0)
            act.wait_ge(s["const_in"], 48)
            act.wait_ge(s["wc_in"], 16)
            nc.scalar.copy(wc[0][:, :, :], wc_st).then_inc(s["wc_hi"], 1)
            body(0, False, True)
            with act.Fori(1, G - 1) as g:
                body(g, True, True)
            body(G - 1, True, False)
            for t in range(TG):
                exponent(G - 1, t)

        @block.vector
        def _(dve):
            def statistics(g):
                step = Steps(dve, s["ln_step"], g * (RSQRT_STEPS + 4))
                dve.wait_ge(s["x_in"], g * 16 + 16)
                if not first(g):
                    dve.wait_ge(s["xn"], g * TG)
                for t in range(TG):
                    last = nc.vector.bn_stats(st[:, t, :], x_in[:, t, :])
                step(last)
                settle(dve, s["settled"])
                for t in range(TG):
                    last = nc.vector.bn_aggr(mv[:, t, :], st[:, t, :])
                step(last)
                step(nc.vector.tensor_scalar(var[:, :], mv[:, :, 1], LN_EPS, None, ALU.add))
                rsqrt(nc, step, rstd[:, :], tmp[:, :], var[:, :])
                step(nc.vector.scalar_tensor_tensor(nbias[:, :], mv[:, :, 0], -1.0, rstd[:, :], ALU.mult, ALU.mult))
                dve.nop().then_inc(s["stats"], 1)

            def weights_low():
                for n in range(QC * 4):
                    c, q = divmod(n, 4)
                    dve.wait_ge(s["wabs_hi"], n + 1)
                    nc.vector.scalar_tensor_tensor(wabs[1][:, c, q * H:(q + 1) * H], fold_ps[n % 4][:, :],
                                                   qscale[:, c:c + 1], wabs[0][:, c, q * H:(q + 1) * H].bitcast(F32),
                                                   ALU.mult, ALU.subtract).then_inc(s["wabs_lo"], 1)
                for c in range(QC):
                    dve.wait_ge(s["wrope_hi"], c + 1)
                    nc.vector.scalar_tensor_tensor(wrope[1][:, c, :], wrope_st[:, c, :], qscale[:, c:c + 1],
                                                   wrope[0][:, c, :].bitcast(F32), ALU.mult,
                                                   ALU.subtract).then_inc(s["wrope_lo"], 1)

            def xT_low(g):
                for t in range(TG):
                    dve.wait_ge(s["xT_hi"], g * TG + t + 1)
                    part = (every, every, slice(t * P, (t + 1) * P))
                    nc.vector.tensor_tensor(xT[1][part], ring[t][:, :].rearrange("p (c q) -> p c q", c=HC),
                                            xT[0][part].bitcast(F32), ALU.subtract).then_inc(s["xT_lo"], 1)

            def latents(g):
                step = Steps(dve, s["rms_step"], g * (RMS_STEPS + 2))
                dve.wait_ge(s["c_raw"], g * TG + TG)
                for n, width in enumerate((QR, KVR)):
                    last = nc.vector.tensor_scalar(rvar[:, n, :], sumsq[:, n, :], 1.0 / width, RMS_EPS, ALU.mult, ALU.add)
                    step(last)
                rsqrt(nc, step, rrms[:, :, :], rtmp[:, :, :], rvar[:, :, :])
                for t in range(TG):
                    for n, (a, z) in enumerate(((0, QR), (QR, QR + KVR))):
                        last = nc.vector.tensor_scalar(craw[:, t, a:z], craw[:, t, a:z], rrms[:, n, t:t + 1], None, ALU.mult)
                last.then_inc(s["c_ready"], 1)

            def keys(g):
                if not first(g):
                    dve.wait_ge(s["rope_sb"], g * 4)
                step = Steps(dve, s["key_step"], g * 2)
                k1, k2 = (craw[:, :, a:a + RH] for a in (QR + KVR, QR + KVR + RH))
                nc.vector.tensor_tensor(kprod[0][:, :, :], k1, cos_p, ALU.mult)
                nc.vector.tensor_tensor(kprod[1][:, :, :], k2, sin_p, ALU.mult)
                nc.vector.tensor_tensor(kprod[2][:, :, :], k1, sin_p, ALU.mult)
                step(nc.vector.tensor_tensor(kprod[3][:, :, :], k2, cos_p, ALU.mult))
                for n, op in enumerate((ALU.subtract, ALU.add)):
                    a, b = (kprod[2 * n + i][:, :, :].unsqueeze(2).broadcast_to([P, TG, HJ, RH]) for i in range(2))
                    last = nc.vector.tensor_tensor(krep[n][:, :, :, :], a, b, op)
                step(last)

            def maximum(g, t):
                dve.wait_ge(s["s_exp"], g * TG + t + 1)
                dve.wait_ge(s["s_mm"], g * TG + t + 1)
                nc.vector.transpose(sc[:, t % 2].rearrange("p h k -> p (h k)"), s_ps[t % 2][:, :]).then_inc(s["s_out"], 1)
                dve.wait_ge(s["s_out"], g * TG + t + 3)
                nc.vector.tensor_tensor(sc[:, t % 2], sc[:, t % 2], mask.unsqueeze(1).broadcast_to([P, NH, S]),
                                        ALU.add).then_inc(s["s_masked"], 1)
                dve.wait_ge(s["s_masked"], g * TG + t + 1)
                nc.vector.tensor_reduce(smx[:, t % 2], sc[:, t % 2], AX.X, ALU.max).then_inc(s["s_max"], 1)

            def total(g, t):
                dve.wait_ge(s["s_exp"], g * TG + t + 3)
                nc.vector.tensor_reduce(ssum[:, :], ex[:, t % 2], AX.X, ALU.add).then_inc(s["s_sum"], 1)
                dve.wait_ge(s["s_sum"], g * TG + t + 1)
                nc.vector.reciprocal(srec[:, t % 2], ssum[:, :]).then_inc(s["s_rec"], 1)

            def turn(g, t):
                dve.wait_ge(s["s_prob"], g * TG + t + 1)
                if t == 0:
                    dve.wait_ge(s["probs_out"], g * 16 + 16)
                nc.vector.transpose(pT[:, t, :], ex[:, t % 2].rearrange("p h k -> p (h k)")).then_inc(s["pT"], 1)

            def rotary(g, i):
                dve.wait_ge(s["rope_mm"], g * 8 + 2 * i + 2)
                if not (first(g) and i == 0):
                    dve.wait_ge(s["rope_sb"], g * 4 + i)
                for n, (half, table) in enumerate(((0, cos_d), (1, sin_d), (0, sin_d), (1, cos_d))):
                    last = nc.vector.tensor_tensor(rot[n][:, :].rearrange("p (b q) -> p b q", q=S),
                                                   ring[1 + half][:, :].rearrange("p (b q) -> p b q", q=S), table, ALU.mult)
                last.then_inc(s["rope_prod"], 1)

            def query_low(g, n):
                dve.wait_ge(s["cq_hi"], g * 2 + n + 1)
                tok = slice(n * 2 * P, (n + 1) * 2 * P)
                nc.vector.tensor_tensor(cqT[1][:, :, tok],
                                        ring[n][:, :].rearrange("p (t c q) -> p c t q", t=2, c=QC),
                                        cqT[0][:, :, tok].bitcast(F32).rearrange("p c (t q) -> p c t q", t=2),
                                        ALU.subtract).then_inc(s["cq_lo"], 1)

            def body(g, back, ahead):
                xT_low(g)
                if back:
                    maximum(g - 1, 0)
                latents(g)
                if back:
                    maximum(g - 1, 1)
                    total(g - 1, 0)
                keys(g)
                if back:
                    maximum(g - 1, 2)
                    turn(g - 1, 0)
                if first(g):
                    weights_low()
                query_low(g, 0)
                query_low(g, 1)
                if back:
                    total(g - 1, 1)
                    maximum(g - 1, 3)
                    turn(g - 1, 1)
                rotary(g, 0)
                if back:
                    total(g - 1, 2)
                    turn(g - 1, 2)
                rotary(g, 1)
                if back:
                    total(g - 1, 3)
                    turn(g - 1, 3)
                rotary(g, 2)
                if ahead:
                    statistics(g + 1)
                rotary(g, 3)

            dve.nop().then_inc(s["s_out"], 2)
            dve.nop().then_inc(s["pT"], 2)
            statistics(0)
            dve.wait_ge(s["const_in"], 48)
            dve.wait_ge(s["wc_hi"], 1)
            nc.vector.tensor_tensor(wc[1][:, :, :], wc_st, wc[0][:, :, :].bitcast(F32), ALU.subtract).then_inc(s["wc_lo"], 1)
            body(0, False, True)
            with dve.Fori(1, G - 1) as g:
                body(g, True, True)
            body(G - 1, True, False)
            for t in range(TG):
                maximum(G - 1, t)
                if t:
                    total(G - 1, t - 1)
                    turn(G - 1, t - 1)
            total(G - 1, 3)
            turn(G - 1, 3)

        @block.tensor
        def _(pe):
            pe.wait_ge(s["const_in"], 48)

            def fold():
                pe.wait_ge(s["wdq_in"], 32)
                for n in range(QC * 4):
                    c, q = divmod(n, 4)
                    if n >= 4:
                        pe.wait_ge(s["wabs_lo"], n - 3)
                    for i in range(4):
                        h = q * 4 + i
                        last = nc.tensor.matmul(fold_ps[n % 4][:, i * KVR:(i + 1) * KVR], wdq_st[:, h, c * P:(c + 1) * P],
                                                wdk_st[:, h, :], start=True, stop=True)
                    last.then_inc(s["wabs_mm"], 1)

            def scores(g, t):
                if t == 0:
                    pe.wait_ge(s["qa_sb"], g * NH + NH)
                    pe.wait_ge(s["rope_sb"], g * 4 + 4)
                    pe.wait_ge(s["kr_sb"], g * 2 + 2)
                pe.wait_ge(s["s_out"], g * TG + t + 1)
                for b in range(BT):
                    tok = slice(t * P + b * S, t * P + (b + 1) * S)
                    out = s_ps[t % 2][b * S:(b + 1) * S, :]
                    nc.tensor.matmul(out, nkvT[:, tok], qa[:, :, tok], start=True, stop=False)
                    for n in range(2):
                        for j in range(HJ):
                            last = nc.tensor.matmul(out.rearrange("p (i j q) -> p i j q", j=HJ, q=S)[:, :, j, :],
                                                    krz[n][:, j, tok], qr[n][:, :, tok], start=False,
                                                    stop=n == 1 and j == HJ - 1)
                last.then_inc(s["s_mm"], 1)

            def body(g, back):
                for t in range(TG):
                    pe.wait_ge(s["xn"], g * TG + t + 1)
                    if first(g):
                        pass
                    elif t in (1, 2):
                        pe.wait_ge(s["rope_prod"], g * 4)
                    else:
                        pe.wait_ge(s["qa_sb"], g * NH)
                    for c in range(HC):
                        last = nc.tensor.transpose(ring[t][:, c * P:(c + 1) * P], xn[:, t, c * P:(c + 1) * P], ident)
                    last.then_inc(s["xT_mm"], 1)
                if back:
                    scores(g - 1, 0)
                if first(g):
                    pe.wait_ge(s["wc_lo"], 1)
                for t in range(TG):
                    pe.wait_ge(s["xT_lo"], g * TG + t + 1)
                    for c in range(HC):
                        last = product(nc, ring[t][:, 0:CW], both(xT, every, c, slice(t * P, (t + 1) * P)),
                                       both(wc, every, c, every), c == 0, c == HC - 1)
                    last.then_inc(s["c_mm"], 1)
                if first(g):
                    fold()
                if back:
                    for t in range(1, TG):
                        scores(g - 1, t)
                pe.wait_ge(s["c_ready"], g + 1)
                for n in range(2):
                    for i in range(2):
                        for c in range(QC):
                            last = nc.tensor.transpose(ring[n][:, (i * QC + c) * P:(i * QC + c + 1) * P],
                                                       craw[:, 2 * n + i, c * P:(c + 1) * P], ident)
                    last.then_inc(s["cq_T"], 1)
                for t in range(TG):
                    last = nc.tensor.transpose(ring[2][:, t * P:(t + 1) * P], craw[:, t, QR:QR + KVR], ident)
                last.then_inc(s["nkv_T"], 1)
                pe.wait_ge(s["key_step"], g * 2 + 2)
                for n in range(2):
                    if n:
                        pe.wait_ge(s["cq_lo"], g * 2 + 1)
                    for t in range(TG):
                        last = nc.tensor.transpose(ring[(3, 0)[n]][:, t * P:(t + 1) * P],
                                                   krep[n][:, t, :, :].rearrange("p j r -> p (j r)"), ident)
                    last.then_inc(s["kr_T"], 1)
                if first(g):
                    pe.wait_ge(s["wabs_lo"], QC * 4)
                    pe.wait_ge(s["wrope_lo"], QC)
                for i in range(NH // HJ):
                    if i == 0:
                        pe.wait_ge(s["cq_lo"], g * 2 + 2)
                        pe.wait_ge(s["nkv_sb"], g + 1)
                    else:
                        pe.wait_ge(s["rope_prod"], g * 4 + i)
                    for half in range(2):
                        m = 2 * i + half
                        for c in range(QC):
                            last = product(nc, ring[1 + half][:, :], both(wrope, every, c, slice(m * P, (m + 1) * P)),
                                           both(cqT, every, c, every), c == 0, c == QC - 1)
                        last.then_inc(s["rope_mm"], 1)
                    for h in range(4 * i, 4 * i + 4):
                        if h < 2:
                            pe.wait_ge(s["kr_sb"], g * 2 + h + 1)
                        elif h >= 4 or not first(g):
                            pe.wait_ge(s["qa_sb"], g * NH + h - 3)
                        for c in range(QC):
                            last = product(nc, qa_ps[h % 4][:, :], both(wabs, every, c, slice(h * KVR, (h + 1) * KVR)),
                                           both(cqT, every, c, every), c == 0, c == QC - 1)
                        last.then_inc(s["qa_mm"], 1)

            body(0, False)
            with pe.Fori(1, G) as g:
                body(g, True)
            for t in range(TG):
                scores(G - 1, t)


FFN_STEPS = 2 * RSQRT_STEPS + 7


def latent_values(nc, sb, pb, sem, d, x1_dram, probs_dram, nkv_dram, h_dram, base_dram, logits):
    x1_v, h_v, base_v = (a.rearrange("(g t p) d -> g p t d", t=TG, p=P) for a in (x1_dram, h_dram, base_dram))
    nkv_v = nkv_dram.rearrange("(n p) d -> n p d", p=P)

    ident = sb("lv_ident", [P, P], F32)
    kvscale = sb("lv_kvscale", [P, 1], F32)
    rms_w = sb("lv_rms_w", [P, HC], F32)
    wvo = [sb(f"lv_wvo{i}", [P, NH, H], F32R) for i in range(2)]
    wgu = [sb(f"lv_wgu{i}", [P, HC, 2 * F], F32R) for i in range(2)]
    wd = [sb(f"lv_wd{i}", [P, FC, H], F32R) for i in range(2)]
    wr = [sb(f"lv_wr{i}", [P, HC, P], F32R) for i in range(2)]
    pf = sb("lv_pf", [P, 2, H], F32)
    pT = [sb(f"lv_pT{i}", [P, 2, H], F32R) for i in range(2)]
    nf = sb("lv_nf", [P, 2, KVR], F32)
    nkv = [sb(f"lv_nkv{i}", [P, 2, KVR], F32R) for i in range(2)]
    oT = [sb(f"lv_oT{i}", [P, 2, NH, P], F32R) for i in range(2)]
    xres = sb("lv_xres", [P, TG, H], F32)
    x2 = sb("lv_x2", [P, TG, H], F32)
    xb = sb("lv_xb", [P, TG, H], F32)
    h = sb("lv_h", [P, TG, H], F32)
    hT = [sb(f"lv_hT{i}", [P, HC, GW], F32R) for i in range(2)]
    act_f = sb("lv_act", [P, FC, GW], F32)
    aT = [sb(f"lv_aT{i}", [P, FC, GW], F32R) for i in range(2)]
    lgT = sb("lv_lgT", [E, GW], F32)
    st = sb("lv_st", [P, TG, 6], F32)
    mv = sb("lv_mv", [P, TG, 2], F32)
    var = sb("lv_var", [P, TG], F32)
    rstd = sb("lv_rstd", [P, TG], F32)
    tmp = sb("lv_tmp", [P, TG], F32)
    rvar = sb("lv_rvar", [P, TG], F32)
    rrms = sb("lv_rrms", [P, TG], F32)
    nbias = sb("lv_nb", [P, TG], F32)

    wo_st = h
    wo_stages = [wo_st, x2]
    wdv_st = xb[:, :, :].rearrange("p a b -> p (a b)").rearrange("p (h k) -> p h k", h=NH)
    wr_st = xb[:, FC, 0:HC * E].rearrange("p (c e) -> p c e", c=HC)

    ring = [pb(f"lv_ring{i}", [P, H], F32) for i in range(4)]
    pv_ps = [pb(f"lv_pv{i}", [P, H], F32) for i in range(2)]
    out_ps = pb("lv_out", [P, H], F32)
    lg_ps = pb("lv_lg", [P, H], F32)

    names = """const_in wdv_in wo_in0 wo_in1 wr_in wgu_in wd_in x1_in p_in0 p_in1 h_out base_out zeroed
        wvo_mm wvo_hi wvo_lo w_hi w_lo p_hi p_lo pv_mm o_hi o_lo out_mm x2 moments copied stats hn hT_mm hT_hi
        hT_lo lg_mm lg_sb lgT_mm logits gu_mm silu gated a_hi a_lo down_mm base ln_step settled settled_pe
        settled_pool""".split()
    s = {n: sem("lv_" + n) for n in names}
    every = slice(None)
    WO_PART = TG
    WO_PARTS = NH // WO_PART
    HP = NH // BT
    W_PARTS = 2 * HC + 1

    def first(g):
        return isinstance(g, int) and g == 0

    def after(g, t):
        return (g, t + 1) if t < TG - 1 else (g + 1, 0)

    def at_end(g, t):
        return isinstance(g, int) and g == G - 1 and t == TG - 1

    block = nc.Block()
    with block:

        @block.sync
        def _(sp):
            sp.nop().then_inc(s["h_out"], 16)
            sp.nop().then_inc(s["base_out"], 16)
            sp.dma_start(wdv_st, d["lv_WdvT"]).then_inc(s["wdv_in"], 16)
            sp.dma_start(wo_st[:, :, :], d["lv_Wo"][:, 0:WO_PART, :]).then_inc(s["wo_in0"], 16)
            sp.dma_start(ident[:, :], d["const"][:, C_IDENT:C_IDENT + P]).then_inc(s["const_in"], 16)
            sp.dma_start(kvscale[:, :], d["kv_scale"]).then_inc(s["const_in"], 16)
            sp.dma_start(rms_w[:, :], d["rms_weight"]).then_inc(s["const_in"], 16)

            def tile_loads(g, t):
                n = g * TG + t
                if not (first(g) and t < 2):
                    sp.wait_ge(s["p_lo"], 2 * n - 2)
                src = probs_dram[n] if isinstance(n, int) else probs_dram[bass.ds(n, 1)].rearrange("a p n -> p (a n)")
                sp.dma_start(pf[:, t % 2, :], src).then_inc(s[f"p_in{t % 2}"], 16)
                src = nkv_v[n] if isinstance(n, int) else nkv_v[bass.ds(n, 1)].rearrange("a p n -> p (a n)")
                sp.dma_start(nf[:, t % 2, :], src).then_inc(s[f"p_in{t % 2}"], 16)

            for n in range(1, WO_PARTS):
                if n >= 2:
                    sp.wait_ge(s["wvo_mm"], (n - 1) * WO_PART)
                sp.dma_start(wo_stages[n % 2][:, :, :], d["lv_Wo"][:, n * WO_PART:(n + 1) * WO_PART, :]).then_inc(s[f"wo_in{n % 2}"], 16)
            tile_loads(0, 0)
            tile_loads(0, 1)
            sp.dma_start(xres[:, :, :], x1_v[0]).then_inc(s["x1_in"], 16)
            sp.wait_ge(s["wvo_mm"], NH)
            sp.dma_start(h[:, :, :], d["lv_Wgu"]).then_inc(s["wgu_in"], 16)
            sp.dma_start(xb[:, 0:FC, :], d["lv_Wd"]).then_inc(s["wd_in"], 16)
            sp.dma_start(wr_st, d["lv_Wr"]).then_inc(s["wr_in"], 16)

            def residual(g):
                sp.wait_ge(s["x2"], g * TG)
                sp.dma_start(xres[:, :, :], group_of(x1_v, g)).then_inc(s["x1_in"], 16)

            def h_store(g):
                sp.wait_ge(s["hn"], (g + 2) * TG)
                sp.dma_start(group_of(h_v, g), h[:, :, :]).then_inc(s["h_out"], 16)

            def base_store(g):
                sp.wait_ge(s["base"], g * TG + 2 * TG)
                sp.dma_start(group_of(base_v, g), xb[:, :, :]).then_inc(s["base_out"], 16)

            def body(g, back, ahead):
                if back:
                    residual(g)
                tile_loads(g, 2)
                tile_loads(g, 3)
                if back:
                    h_store(g - 1)
                if ahead:
                    tile_loads(g + 1, 0)
                    tile_loads(g + 1, 1)
                if back:
                    base_store(g - 1)

            body(0, False, True)
            with sp.Fori(1, G - 1) as g:
                body(g, True, True)
            body(G - 1, True, False)
            h_store(G - 1)
            base_store(G - 1)
            for n in ("h_out", "base_out"):
                sp.wait_ge(s[n], G * 16 + 16)

        @block.gpsimd
        def _(pool):
            pool.nop().then_inc(s["copied"], TG)
            for i in range(2):
                nc.gpsimd.memset(wr[i][:, :, :].bitcast(F32), 0.0).then_inc(s["zeroed"], 1)

            def split(g, t):
                n = g * TG + t
                pool.wait_ge(s[f"p_in{t % 2}"], (g * 2 + t // 2) * 32 + 32)
                if not (first(g) and t < 2):
                    pool.wait_ge(s["pv_mm"], n * BT - BT)
                settle(pool, s["settled_pool"])
                nc.gpsimd.tensor_copy(pT[0][:, t % 2, :], pf[:, t % 2, :])
                nc.gpsimd.tensor_copy(nkv[0][:, t % 2, :], nf[:, t % 2, :]).then_inc(s["p_hi"], 1)
                pool.wait_ge(s["p_hi"], n + 1)
                nc.gpsimd.tensor_tensor(pT[1][:, t % 2, :], pf[:, t % 2, :], pT[0][:, t % 2, :].bitcast(F32),
                                        ALU.subtract).then_inc(s["p_lo"], 1)
                nc.gpsimd.tensor_tensor(nkv[1][:, t % 2, :], nf[:, t % 2, :], nkv[0][:, t % 2, :].bitcast(F32),
                                        ALU.subtract).then_inc(s["p_lo"], 1)

            def copy(g):
                pool.wait_ge(s["base_out"], g * 16 + 16)
                for t in range(TG):
                    pool.wait_ge(s["x2"], g * TG + t + 1)
                    settle(pool, s["settled_pool"])
                    nc.gpsimd.tensor_copy(xb[:, t, :], x2[:, t, :]).then_inc(s["copied"], 1)

            def body(g, back, ahead):
                if back:
                    copy(g - 1)
                split(g, 2)
                split(g, 3)
                if ahead:
                    split(g + 1, 0)
                    split(g + 1, 1)

            split(0, 0)
            split(0, 1)
            body(0, False, True)
            pool.wait_ge(s["w_lo"], W_PARTS)
            with pool.Fori(1, G - 1) as g:
                body(g, True, True)
            body(G - 1, True, False)
            copy(G - 1)

        @block.scalar
        def _(act):
            act.nop().then_inc(s["hn"], TG)
            act.wait_ge(s["const_in"], 48)
            for n in range(NH):
                act.wait_ge(s["wvo_mm"], n + 1)
                nc.scalar.activation(wvo[0][:, n, :], ring[n % 4][:, :], ACT.Copy,
                                     scale=kvscale[:, 0:1]).then_inc(s["wvo_hi"], 1)

            def later_weights():
                act.wait_ge(s["wgu_in"], 16)
                for c in range(HC):
                    nc.scalar.activation(wgu[0][:, c, :], h[:, c, :], ACT.Copy, scale=rms_w[:, c:c + 1]).then_inc(s["w_hi"], 1)
                act.wait_ge(s["wd_in"], 16)
                nc.scalar.copy(wd[0][:, :, :], xb[:, 0:FC, :]).then_inc(s["w_hi"], 1)
                act.wait_ge(s["wr_in"], 16)
                act.wait_ge(s["zeroed"], 2)
                for c in range(HC):
                    nc.scalar.activation(wr[0][:, c, 0:E], wr_st[:, c, :], ACT.Copy, scale=rms_w[:, c:c + 1]).then_inc(s["w_hi"], 1)

            def sum_high(g, t, b):
                act.wait_ge(s["pv_mm"], (g * TG + t) * BT + b + 1)
                nc.scalar.copy(oT[0][:, t % 2, :, b * S:(b + 1) * S],
                               pv_ps[b % 2][:, :].rearrange("p (h q) -> p h q", h=NH)).then_inc(s["o_hi"], 1)

            def normalise(g):
                act.wait_ge(s["stats"], g + 1)
                act.wait_ge(s["h_out"], g * 16 + 16)
                act.wait_ge(s["hT_mm"], g * TG + TG)
                for t in range(TG):
                    nc.scalar.activation(h[:, t, :], x2[:, t, :], ACT.Identity, bias=nbias[:, t:t + 1],
                                         scale=rstd[:, t:t + 1]).then_inc(s["hn"], 1)

            def h_high(g):
                for t in range(TG):
                    act.wait_ge(s["hT_mm"], (g + 1) * TG + t + 1)
                    nc.scalar.copy(hT[0][:, :, t * P:(t + 1) * P],
                                   ring[t][:, :].rearrange("p (c q) -> p c q", c=HC)).then_inc(s["hT_hi"], 1)

            def logit_copy(g):
                act.wait_ge(s["lg_mm"], g + 1)
                nc.scalar.copy(lgT[:, :], lg_ps[0:E, :]).then_inc(s["lg_sb"], 1)

            def silu(g, m):
                act.wait_ge(s["gu_mm"], g * 2 * FC + m + 1)
                nc.scalar.activation(act_f[:, m, :], ring[m][:, :], ACT.Silu).then_inc(s["silu"], 1)

            def gated_high(g, m):
                act.wait_ge(s["gated"], g * FC + m + 1)
                nc.scalar.copy(aT[0][:, m, :], act_f[:, m, :]).then_inc(s["a_hi"], 1)

            def shared(g, t, q):
                if (t, q) == (0, 3):
                    normalise(g)
                elif (t, q) == (1, 0):
                    h_high(g)
                elif (t, q) == (1, 2):
                    logit_copy(g)
                    silu(g, 0)
                elif (t, q) == (1, 3):
                    silu(g, 1)
                elif (t, q) == (2, 1):
                    gated_high(g, 0)
                elif (t, q) == (2, 2):
                    gated_high(g, 1)

            def body(g, back):
                for t in range(TG):
                    for q in range(BT):
                        if not at_end(g, t):
                            sum_high(*after(g, t), q)
                        if back:
                            shared(g - 1, t, q)

            for b in range(BT):
                sum_high(0, 0, b)
            later_weights()
            body(0, False)
            with act.Fori(1, G - 1) as g:
                body(g, True)
            body(G - 1, True)
            for t in range(TG):
                for q in range(BT):
                    shared(G - 1, t, q)

        @block.vector
        def _(dve):
            dve.wait_ge(s["const_in"], 48)
            dve.nop().then_inc(s["base"], TG)
            dve.nop().then_inc(s["logits"], 1)
            for n in range(NH):
                dve.wait_ge(s["wvo_hi"], n + 1)
                nc.vector.scalar_tensor_tensor(wvo[1][:, n, :], ring[n % 4][:, :], kvscale[:, 0:1],
                                               wvo[0][:, n, :].bitcast(F32), ALU.mult, ALU.subtract).then_inc(s["wvo_lo"], 1)

            def later_weights():
                for c in range(HC):
                    dve.wait_ge(s["w_hi"], c + 1)
                    nc.vector.scalar_tensor_tensor(wgu[1][:, c, :], h[:, c, :], rms_w[:, c:c + 1],
                                                   wgu[0][:, c, :].bitcast(F32), ALU.mult,
                                                   ALU.subtract).then_inc(s["w_lo"], 1)
                dve.wait_ge(s["w_hi"], HC + 1)
                nc.vector.tensor_tensor(wd[1][:, :, :], xb[:, 0:FC, :], wd[0][:, :, :].bitcast(F32),
                                        ALU.subtract).then_inc(s["w_lo"], 1)
                for c in range(HC):
                    dve.wait_ge(s["w_hi"], HC + c + 2)
                    nc.vector.scalar_tensor_tensor(wr[1][:, c, 0:E], wr_st[:, c, :], rms_w[:, c:c + 1],
                                                   wr[0][:, c, 0:E].bitcast(F32), ALU.mult,
                                                   ALU.subtract).then_inc(s["w_lo"], 1)

            def sum_low(g, t, b):
                dve.wait_ge(s["o_hi"], (g * TG + t) * BT + b + 1)
                part = (every, t % 2, every, slice(b * S, (b + 1) * S))
                nc.vector.tensor_tensor(oT[1][part], pv_ps[b % 2][:, :].rearrange("p (h q) -> p h q", h=NH),
                                        oT[0][part].bitcast(F32), ALU.subtract).then_inc(s["o_lo"], 1)

            def add(g, t):
                if t == 0:
                    dve.wait_ge(s["x1_in"], g * 16 + 16)
                dve.wait_ge(s["hn"], g * TG + t + 1)
                dve.wait_ge(s["copied"], g * TG + t + 1)
                dve.wait_ge(s["out_mm"], g * TG + t + 1)
                nc.vector.tensor_tensor(x2[:, t, :], out_ps[:, :], xres[:, t, :], ALU.add).then_inc(s["x2"], 1)

            def moments(g, t):
                dve.wait_ge(s["x2"], g * TG + t + 1)
                nc.vector.bn_stats(st[:, t, :], x2[:, t, :]).then_inc(s["moments"], 1)

            def chain(g, done):
                return Steps(dve, s["ln_step"], g * FFN_STEPS + done)

            def variance(g):
                dve.wait_ge(s["moments"], g * TG + TG)
                settle(dve, s["settled"])
                step = chain(g, 0)
                for t in range(TG):
                    last = nc.vector.bn_aggr(mv[:, t, :], st[:, t, :])
                step(last)
                step(nc.vector.tensor_scalar(var[:, :], mv[:, :, 1], LN_EPS, None, ALU.add))

            def layer_scale(g):
                step = chain(g, 2)
                rsqrt(nc, step, rstd[:, :], tmp[:, :], var[:, :])
                step(nc.vector.tensor_tensor(rvar[:, :], rstd[:, :], rstd[:, :], ALU.mult))
                step(nc.vector.tensor_tensor(rvar[:, :], rvar[:, :], mv[:, :, 1], ALU.mult))
                step(nc.vector.tensor_scalar(rvar[:, :], rvar[:, :], RMS_EPS, None, ALU.add))

            def both_scales(g):
                step = chain(g, RSQRT_STEPS + 5)
                rsqrt(nc, step, rrms[:, :], tmp[:, :], rvar[:, :])
                step(nc.vector.tensor_tensor(rstd[:, :], rstd[:, :], rrms[:, :], ALU.mult))
                step(nc.vector.scalar_tensor_tensor(nbias[:, :], mv[:, :, 0], -1.0, rstd[:, :], ALU.mult, ALU.mult))
                dve.nop().then_inc(s["stats"], 1)

            def h_low(g):
                for t in range(TG):
                    dve.wait_ge(s["hT_hi"], g * TG + t + 1)
                    part = (every, every, slice(t * P, (t + 1) * P))
                    nc.vector.tensor_tensor(hT[1][part], ring[t][:, :].rearrange("p (c q) -> p c q", c=HC),
                                            hT[0][part].bitcast(F32), ALU.subtract).then_inc(s["hT_lo"], 1)

            def gate(g, m):
                dve.wait_ge(s["silu"], g * FC + m + 1)
                dve.wait_ge(s["gu_mm"], g * 2 * FC + FC + m + 1)
                nc.vector.tensor_tensor(act_f[:, m, :], ring[FC + m][:, :], act_f[:, m, :], ALU.mult).then_inc(s["gated"], 1)

            def gated_low(g, m):
                dve.wait_ge(s["a_hi"], g * FC + m + 1)
                nc.vector.tensor_tensor(aT[1][:, m, :], act_f[:, m, :], aT[0][:, m, :].bitcast(F32),
                                        ALU.subtract).then_inc(s["a_lo"], 1)

            def router(g):
                dve.wait_ge(s["lgT_mm"], g + 1)
                dst = logits[:, g * TG:(g + 1) * TG, :] if isinstance(g, int) else logits[:, bass.ds(g * TG, TG), :]
                nc.vector.tensor_copy(dst, lg_ps[:, 0:TG * E].rearrange("p (t e) -> p t e", t=TG)).then_inc(s["logits"], 1)

            def base(g, t):
                if t == 0:
                    dve.wait_ge(s["copied"], (g + 2) * TG)
                dve.wait_ge(s["down_mm"], g * TG + t + 1)
                nc.vector.tensor_tensor(xb[:, t, :], ring[t][:, :], xb[:, t, :], ALU.add).then_inc(s["base"], 1)

            def shared(g, t, q):
                if (t, q) == (0, 0):
                    moments(g, TG - 1)
                    variance(g)
                elif (t, q) == (0, 1):
                    layer_scale(g)
                elif (t, q) == (0, 2):
                    both_scales(g)
                elif (t, q) == (1, 0):
                    h_low(g)
                elif (t, q) == (2, 0):
                    gate(g, 0)
                elif (t, q) == (2, 1):
                    gate(g, 1)
                    gated_low(g, 0)
                elif (t, q) == (2, 2):
                    router(g)
                    gated_low(g, 1)
                elif (t, q) == (3, 0):
                    base(g, 0)
                elif (t, q) == (3, 1):
                    base(g, 1)
                elif (t, q) == (3, 2):
                    base(g, 2)
                elif (t, q) == (3, 3):
                    base(g, 3)

            def body(g, back):
                for t in range(TG):
                    for q in range(BT):
                        if q == 0 and t > 0:
                            add(g, t - 1)
                        if q == 0 and t == 0 and back:
                            add(g - 1, TG - 1)
                        if not at_end(g, t):
                            sum_low(*after(g, t), q)
                        if q == 0 and t > 0:
                            moments(g, t - 1)
                        if back:
                            shared(g - 1, t, q)

            for b in range(BT):
                sum_low(0, 0, b)
            later_weights()
            body(0, False)
            with dve.Fori(1, G - 1) as g:
                body(g, True)
            body(G - 1, True)
            add(G - 1, TG - 1)
            for t in range(TG):
                for q in range(BT):
                    shared(G - 1, t, q)

        @block.tensor
        def _(pe):
            pe.nop().then_inc(s["hT_mm"], TG)
            pe.wait_ge(s["const_in"], 48)
            pe.wait_ge(s["wdv_in"], 16)
            for n in range(NH):
                if n % WO_PART == 0:
                    part = n // WO_PART
                    pe.wait_ge(s[f"wo_in{part % 2}"], 16 * (part // 2 + 1))
                if n >= 4:
                    pe.wait_ge(s["wvo_lo"], n - 3)
                nc.tensor.matmul(ring[n % 4][:, :], wdv_st[:, n, :], wo_stages[n // WO_PART % 2][:, n % WO_PART, :],
                                 start=True, stop=True).then_inc(s["wvo_mm"], 1)

            def weighted(g, t, b):
                n = g * TG + t
                if b == 0:
                    pe.wait_ge(s["p_lo"], 2 * n + 2)
                if not (first(g) and t == 0 and b < 2):
                    pe.wait_ge(s["o_lo"], n * BT + b - 1)
                rows = slice(b * S, (b + 1) * S)
                product(nc, pv_ps[b % 2][:, :], both(nkv, rows, t % 2, every),
                        both(pT, rows, t % 2, every)).then_inc(s["pv_mm"], 1)

            def outputs(g, t, q):
                n = g * TG + t
                if q == 0:
                    pe.wait_ge(s["o_lo"], n * BT + BT)
                    if not (first(g) and t == 0):
                        pe.wait_ge(s["x2"], n)
                for i in range(q * HP, (q + 1) * HP):
                    last = product(nc, out_ps[:, :], both(oT, every, t % 2, i, every), both(wvo, every, i, every),
                                   i == 0, i == NH - 1)
                if q == BT - 1:
                    last.then_inc(s["out_mm"], 1)

            def transposes(g):
                for t in range(TG):
                    pe.wait_ge(s["hn"], (g + 1) * TG + t + 1)
                    pe.wait_ge(s["base"], g * TG + t + 1)
                    for c in range(HC):
                        last = nc.tensor.transpose(ring[t][:, c * P:(c + 1) * P], h[:, t, c * P:(c + 1) * P], ident[:, :])
                    last.then_inc(s["hT_mm"], 1)

            def router(g):
                pe.wait_ge(s["hT_lo"], g * TG + TG)
                pe.wait_ge(s["logits"], g + 1)
                for c in range(HC):
                    last = product(nc, lg_ps[:, :], both(wr, every, c, every), both(hT, every, c, every), c == 0, c == HC - 1)
                last.then_inc(s["lg_mm"], 1)

            def shared_up(g, m):
                for c in range(HC):
                    last = product(nc, ring[m][:, :], both(wgu, every, c, slice(m * P, (m + 1) * P)),
                                   both(hT, every, c, every), c == 0, c == HC - 1)
                last.then_inc(s["gu_mm"], 1)

            def logit_transposes(g):
                pe.wait_ge(s["lg_sb"], g + 1)
                settle(pe, s["settled_pe"])
                for t in range(TG):
                    last = nc.tensor.transpose(lg_ps[:, t * E:(t + 1) * E], lgT[:, t * P:(t + 1) * P], ident[0:E, 0:E])
                last.then_inc(s["lgT_mm"], 1)

            def shared_down(g, t):
                pe.wait_ge(s["a_lo"], g * FC + FC)
                for m in range(FC):
                    last = product(nc, ring[t][:, :], both(aT, every, m, slice(t * P, (t + 1) * P)),
                                   both(wd, every, m, every), m == 0, m == FC - 1)
                last.then_inc(s["down_mm"], 1)

            def shared(g, t, q):
                if (t, q) == (1, 0):
                    transposes(g)
                elif (t, q) == (1, 1):
                    router(g)
                    shared_up(g, 0)
                elif (t, q) == (1, 2):
                    shared_up(g, 1)
                elif (t, q) == (1, 3):
                    shared_up(g, 2)
                elif (t, q) == (2, 0):
                    shared_up(g, 3)
                elif (t, q) == (2, 1):
                    logit_transposes(g)
                elif (t, q) == (2, 3):
                    shared_down(g, 0)
                elif (t, q) == (3, 0):
                    shared_down(g, 1)
                elif (t, q) == (3, 1):
                    shared_down(g, 2)
                elif (t, q) == (3, 2):
                    shared_down(g, 3)

            def body(g, back):
                for t in range(TG):
                    for q in range(BT):
                        if not at_end(g, t):
                            weighted(*after(g, t), q)
                        outputs(g, t, q)
                        if back:
                            shared(g - 1, t, q)

            pe.wait_ge(s["wvo_lo"], NH)
            for b in range(BT):
                weighted(0, 0, b)
            body(0, False)
            pe.wait_ge(s["w_lo"], W_PARTS)
            with pe.Fori(1, G - 1) as g:
                body(g, True)
            body(G - 1, True)
            for t in range(TG):
                for q in range(BT):
                    shared(G - 1, t, q)


UE = 4


def experts(nc, sb, pb, sem, d, h_dram, table_dram, out_dram, logits):
    const = sb("ex_const", [P, C_END], F32)
    ident = const[:, C_IDENT:C_IDENT + P]
    ones = sb("ex_ones", [P, P], F32)
    rms_w = sb("ex_rms_w", [P, HC], F32)
    wgu = [sb(f"ex_wgu{i}", [P, E * HC, 2 * F], F32R) for i in range(2)]
    wd = sb("ex_wd", [P, E * FC, H], F32)
    hs = sb("ex_hs", [P, UE, H], F32)
    hT = [sb(f"ex_hT{i}", [P, 2, HC, P], F32R) for i in range(2)]
    gated = sb("ex_gated", [P, 2, F], F32)
    aT = sb("ex_aT", [P, 2, FC, P], F32)
    y = sb("ex_y", [P, 2, H], F32)
    route = [sb(f"ex_route{i}", [P, NT, E], F32) for i in range(3)]
    hot = [sb(f"ex_hot{i}", [P, NT, E], F32) for i in range(2)]
    row = [sb(f"ex_row{i}", [P, NT], F32) for i in range(4)]
    per = [sb(f"ex_per{i}", [P, E], F32) for i in range(4)]
    count = sb("ex_count", [P, E], I32)
    weights = sb("ex_weights", [P, TOPK, NT], F32)
    slot_i = sb("ex_slot_i", [P, TOPK, NT], I32)
    part = [sb(f"ex_part{i}", [P, TOPK, NT], I32) for i in range(2)]
    part_f = [sb(f"ex_part_f{i}", [P, TOPK, NT], F32) for i in range(2)]
    cell = sb("ex_cell", [P, TOPK, NT], U32)
    entry = sb("ex_entry", [P, TOPK, NT, 2], U32)
    padding = sb("ex_padding", [P, NTE, 2], U32)
    reached = gated[:, :, :].rearrange("p a b -> p (a b)")
    expert_f = sb("ex_expert_f", [P, NTE], F32)
    expert = sb("ex_expert", [P, NTE], I32)
    source = sb("ex_source", [P, NTE, 2], U32)
    from_row = sb("ex_from_row", [P, UE], U32)
    to_row = sb("ex_to_row", [P, UE], U32)

    hT_ps = [pb(f"ex_hT_ps{i}", [P, H], F32) for i in range(2)]
    gu_ps = [pb(f"ex_gu_ps{i}", [P, H], F32) for i in range(2)]
    aT_ps = pb("ex_aT_ps", [P, H], F32)
    y_ps = [pb(f"ex_y_ps{i}", [P, H], F32) for i in range(2)]
    count_ps = pb("ex_count_ps", [P, H], F32)

    names = """const_in rms_in wd_in wgu_in0 wgu_in1 ones padded pad_rows wgu_hi wgu_lo route delta gap ranked count_mm
        slots_ready table_zero table_out source_in indexed to_rows gather0 gather1 gather2 gather3 hT_mm hT_hi hT_lo
        gu_mm silu gated aT_mm aT y_mm y_sb summed settled""".split()
    s = {n: sem("ex_" + n) for n in names}
    every = slice(None)
    STAGES = UE * H // (2 * F * 2)
    every = slice(None)
    HALF = HC // 2
    stage = [hs[:, 2 * i:2 * i + HALF, :] for i in range(2)]
    first = lambda g: isinstance(g, int) and g == 0
    assert STAGES == 2

    block = nc.Block()
    with block:

        @block.sync
        def _(sp):
            sp.dma_start(const[:, :], d["const"]).then_inc(s["const_in"], 16)
            sp.dma_start(rms_w[:, :], d["rms_weight"]).then_inc(s["rms_in"], 16)
            sp.wait_ge(s["padded"], 2)
            sp.dma_start(table_dram, padding[:, :, :].rearrange("p n a -> p (n a)")).then_inc(s["table_zero"], 16)
            sp.dma_start(h_dram[T:T + P, :], y[:, 0, :]).then_inc(s["pad_rows"], 16)
            sp.dma_start(out_dram[T:T + P, :], y[:, 0, :]).then_inc(s["pad_rows"], 16)
            for n in range(E * 2):
                if n >= 2:
                    sp.wait_ge(s["wgu_lo"], n - 1)
                sp.dma_start(stage[n % 2], d["ex_Wgu"][:, n * HALF:(n + 1) * HALF, :]).then_inc(s[f"wgu_in{n % 2}"], 16)
            sp.dma_start(wd[:, :, :], d["ex_Wd"]).then_inc(s["wd_in"], 16)
            sp.wait_ge(s["table_out"], TOPK * NT * 16)
            sp.dma_start(source[:, :, :].rearrange("p n a -> p (n a)"), table_dram).then_inc(s["source_in"], 16)

        @block.gpsimd
        def _(pool):
            nc.gpsimd.memset(y[:, 0, :], 0.0).then_inc(s["padded"], 1)
            nc.gpsimd.memset(ones[:, :], 1.0).then_inc(s["ones"], 1)
            pool.wait_ge(s["table_zero"], 16)
            pool.wait_ge(s["slots_ready"], 1)
            for k in range(TOPK):
                for t in range(NT):
                    nc.gpsimd.indirect_dma_start(
                        table_dram.rearrange("p (n a) -> (p n) a", a=2),
                        bass.IndirectOffsetOnAxis(ap=cell[:, k, t:t + 1], axis=0), entry[:, k, t, :], None
                    ).then_inc(s["table_out"], 16)
            pool.wait_ge(s["source_in"], 16)
            pool.wait_ge(s["pad_rows"], 32)
            pool.wait_ge(s["wgu_lo"], 2 * E)

            def tokens(k):
                return source[:, k * UE:(k + 1) * UE, 0] if isinstance(k, int) else source[:, bass.ds(k * UE, UE), 0]

            def gather(k, i):
                pool.wait_ge(s["indexed"], k + 1)
                if not first(k):
                    pool.wait_ge(s["hT_mm"], (k - 1) * UE + i + 1)
                settle(pool, s["settled"])
                nc.gpsimd.indirect_dma_start(
                    hs[:, i, :], None, h_dram, bass.IndirectOffsetOnAxis(ap=from_row[:, i:i + 1], axis=0)
                ).then_inc(s[f"gather{i}"], 16)

            def add(k, i):
                n = k * UE + i
                pool.wait_ge(s["to_rows"], k + 1)
                pool.wait_ge(s["y_sb"], n + 1)
                if not (first(k) and i == 0):
                    pool.wait_ge(s["summed"], n * 16)
                settle(pool, s["settled"])
                nc.gpsimd.indirect_dma_start(
                    out_dram, bass.IndirectOffsetOnAxis(ap=to_row[:, i:i + 1], axis=0), y[:, i % 2, :], None,
                    compute_op=ALU.add).then_inc(s["summed"], 16)

            def turn(k, ahead):
                if ahead:
                    for i in range(UE):
                        pool.wait_ge(s[f"gather{i}"], k * 16 + 16)
                    settle(pool, s["settled"])
                    nc.gpsimd.tensor_copy(from_row[:, :], tokens(k + 1)).then_inc(s["indexed"], 1)
                if not first(k):
                    pool.wait_ge(s["summed"], k * UE * 16)
                settle(pool, s["settled"])
                nc.gpsimd.tensor_copy(to_row[:, :], tokens(k)).then_inc(s["to_rows"], 1)
                for i in range(UE):
                    if ahead:
                        gather(k + 1, i)
                    add(k, i)

            nc.gpsimd.tensor_copy(from_row[:, :], tokens(0)).then_inc(s["indexed"], 1)
            for i in range(UE):
                gather(0, i)
            turn(0, True)
            with pool.Fori(1, NTE // UE - 1) as k:
                turn(k, True)
            turn(NTE // UE - 1, False)
            pool.wait_ge(s["summed"], NTE * 16)

        @block.scalar
        def _(act):
            act.wait_ge(s["rms_in"], 16)
            act.wait_ge(s["delta"], 1)
            nc.scalar.activation(row[3][:, :], row[2][:, :], ACT.Exp).then_inc(s["gap"], 1)
            for n in range(E * 2):
                act.wait_ge(s[f"wgu_in{n % 2}"], 16 * (n // 2 + 1))
                for c in range(HALF):
                    row_of = n % 2 * HALF + c
                    last = nc.scalar.activation(wgu[0][:, n * HALF + c, :], stage[n % 2][:, c, :], ACT.Copy,
                                                scale=rms_w[:, row_of:row_of + 1])
                last.then_inc(s["wgu_hi"], 1)

            def hT_high(n, i):
                act.wait_ge(s["hT_mm"], n + 1)
                if not isinstance(n, int) or n >= 2:
                    act.wait_ge(s["gu_mm"], n - 1)
                nc.scalar.copy(hT[0][:, i % 2, :, :], hT_ps[i % 2][:, :].rearrange("p (c q) -> p c q", c=HC)).then_inc(s["hT_hi"], 1)

            def silu(n, i):
                act.wait_ge(s["gu_mm"], n + 1)
                if not isinstance(n, int) or n >= 2:
                    act.wait_ge(s["aT_mm"], n - 1)
                nc.scalar.activation(gated[:, i % 2, :], gu_ps[i % 2][:, 0:F], ACT.Silu).then_inc(s["silu"], 1)

            weight = source[:, :, 1].bitcast(F32)

            def result(n, i):
                act.wait_ge(s["y_mm"], n + 1)
                if not isinstance(n, int) or n >= 2:
                    act.wait_ge(s["summed"], (n - 1) * 16)
                nc.scalar.activation(y[:, i % 2, :], y_ps[i % 2][:, :], ACT.Copy,
                                     scale=weight[:, n:n + 1] if isinstance(n, int) else weight[:, bass.ds(n, 1)]
                                     ).then_inc(s["y_sb"], 1)

            def tile(k, i):
                n = k * UE + i
                if i < UE - 1 or not isinstance(k, int) or k < NTE // UE - 1:
                    hT_high(n + 1, i + 1)
                silu(n, i)
                if not (first(k) and i == 0):
                    result(n - 1, i - 1)

            hT_high(0, 0)
            for k in (0,):
                for i in range(UE):
                    tile(k, i)
            with act.Fori(1, NTE // UE - 1) as k:
                for i in range(UE):
                    tile(k, i)
            for i in range(UE):
                tile(NTE // UE - 1, i)
            result(NTE - 1, UE - 1)

        @block.vector
        def _(dve):
            step = Steps(dve, s["route"], 0)
            dve.wait_ge(s["rms_in"], 16)
            dve.wait_ge(s["const_in"], 16)
            nc.vector.memset(padding[:, :, 1], 0)
            nc.vector.tensor_copy(padding[:, :, 0], const[:, C_PAD:C_PAD + 1].broadcast_to([P, NTE])).then_inc(s["padded"], 1)
            order = const[:, C_FIRST:C_FIRST + E].unsqueeze(1).broadcast_to([P, NT, E])

            def spread(a):
                return a[:, :].unsqueeze(2).broadcast_to([P, NT, E])

            score, scratch, base = route
            for k in range(TOPK):
                src = logits if k == 0 else score
                step(nc.vector.tensor_reduce(row[k][:, :], src[:, :, :], AX.X, ALU.max))
                step(nc.vector.tensor_tensor(scratch[:, :, :], src[:, :, :], spread(row[k]), ALU.is_equal))
                step(nc.vector.tensor_tensor(scratch[:, :, :], scratch[:, :, :], order, ALU.mult))
                step(nc.vector.tensor_reduce(row[2][:, :], scratch[:, :, :], AX.X, ALU.max))
                step(nc.vector.tensor_tensor(hot[k][:, :, :], order, spread(row[2]), ALU.is_equal))
                if k == 0:
                    step(nc.vector.scalar_tensor_tensor(score[:, :, :], hot[0][:, :, :], MASKED, logits[:, :, :],
                                                        ALU.mult, ALU.add))
            nc.vector.tensor_tensor(row[2][:, :], row[1][:, :], row[0][:, :], ALU.subtract).then_inc(s["delta"], 1)
            nc.vector.tensor_tensor(score[:, :, :], hot[0][:, :, :], hot[1][:, :, :], ALU.add).then_inc(s["ranked"], 1)
            dve.wait_ge(s["gap"], 1)
            step(nc.vector.tensor_scalar(row[0][:, :], row[3][:, :], 1.0, None, ALU.add))
            step(nc.vector.reciprocal(weights[:, 0, :], row[0][:, :]))
            step(nc.vector.tensor_tensor(weights[:, 1, :], row[3][:, :], weights[:, 0, :], ALU.mult))
            dve.wait_ge(s["count_mm"], 1)
            rank, total = (count_ps[:, a:a + NT * E].rearrange("p (t e) -> p t e", e=E) for a in (0, NT * E))
            step(nc.vector.tensor_copy(scratch[:, :, :], total))
            a, b = scratch, base
            k = 1
            while k < NT:
                nc.vector.tensor_tensor(b[:, k:, :], a[:, k:, :], a[:, :NT - k, :], ALU.add)
                step(nc.vector.tensor_copy(b[:, :k, :], a[:, :k, :]))
                a, b, k = b, a, 2 * k
            step(nc.vector.tensor_scalar(count[:, :], a[:, NT - 1, :], float(P - 1), None, ALU.add))
            step(nc.vector.tensor_scalar(count[:, :], count[:, :], P.bit_length() - 1, None, ALU.arith_shift_right))
            step(nc.vector.tensor_copy(per[0][:, :], count[:, :]))
            step(nc.vector.tensor_copy(per[1][:, :], per[0][:, :]))
            c, e = per[1], per[2]
            k = 1
            while k < E:
                nc.vector.tensor_tensor(e[:, k:], c[:, k:], c[:, :E - k], ALU.add)
                step(nc.vector.tensor_copy(e[:, :k], c[:, :k]))
                c, e, k = e, c, 2 * k
            start = per[3]
            step(nc.vector.tensor_tensor(start[:, :], c[:, :], per[0][:, :], ALU.subtract))
            step(nc.vector.tensor_tensor(a[:, :, :], a[:, :, :], total, ALU.subtract))
            step(nc.vector.tensor_tensor(a[:, :, :], a[:, :, :], rank, ALU.add))
            step(nc.vector.scalar_tensor_tensor(a[:, :, :], start[:, :].unsqueeze(1).broadcast_to([P, NT, E]),
                                                float(P), a[:, :, :], ALU.mult, ALU.add))
            for k in range(TOPK):
                step(nc.vector.tensor_tensor(b[:, :, :], hot[k][:, :, :], a[:, :, :], ALU.mult))
                step(nc.vector.tensor_reduce(part_f[0][:, k, :], b[:, :, :], AX.X, ALU.add))
            step(nc.vector.tensor_copy(slot_i[:, :, :], part_f[0][:, :, :]))
            nc.vector.tensor_scalar(part[0][:, :, :], slot_i[:, :, :], P - 1, None, ALU.bitwise_and)
            step(nc.vector.tensor_scalar(part[1][:, :, :], slot_i[:, :, :], P.bit_length() - 1, None, ALU.arith_shift_right))
            nc.vector.tensor_copy(part_f[0][:, :, :], part[0][:, :, :])
            step(nc.vector.tensor_copy(part_f[1][:, :, :], part[1][:, :, :]))
            nc.vector.tensor_copy(entry[:, :, :, 0], const[:, C_TOKEN:C_TOKEN + NT].unsqueeze(1).broadcast_to([P, TOPK, NT]))
            nc.vector.tensor_copy(entry[:, :, :, 1], weights[:, :, :].bitcast(U32))
            step(nc.vector.scalar_tensor_tensor(cell[:, :, :], part_f[0][:, :, :], float(NTE), part_f[1][:, :, :],
                                                ALU.mult, ALU.add))
            dve.nop().then_inc(s["slots_ready"], 1)
            tiles = const[:, C_TILE:C_TILE + NTE]
            step(nc.vector.tensor_scalar(expert_f[:, :], tiles, start[:, 1:2], None, ALU.is_ge))
            for k in range(2, E):
                step(nc.vector.scalar_tensor_tensor(expert_f[:, :], tiles, start[:, k:k + 1], expert_f[:, :],
                                                    ALU.is_ge, ALU.add))
            step(nc.vector.tensor_copy(expert[:, :], expert_f[:, :]))
            dve.nop().then_inc(s["slots_ready"], 1)
            for n in range(E * 2):
                dve.wait_ge(s["wgu_hi"], n + 1)
                for c in range(HALF):
                    row_of = n % 2 * HALF + c
                    last = nc.vector.scalar_tensor_tensor(wgu[1][:, n * HALF + c, :], stage[n % 2][:, c, :],
                                                          rms_w[:, row_of:row_of + 1],
                                                          wgu[0][:, n * HALF + c, :].bitcast(F32), ALU.mult, ALU.subtract)
                last.then_inc(s["wgu_lo"], 1)

            def hT_low(n, i):
                dve.wait_ge(s["hT_hi"], n + 1)
                nc.vector.tensor_tensor(hT[1][:, i % 2, :, :], hT_ps[i % 2][:, :].rearrange("p (c q) -> p c q", c=HC),
                                        hT[0][:, i % 2, :, :].bitcast(F32), ALU.subtract).then_inc(s["hT_lo"], 1)

            def gate(n, i):
                dve.wait_ge(s["silu"], n + 1)
                nc.vector.tensor_tensor(gated[:, i % 2, :], gu_ps[i % 2][:, F:2 * F], gated[:, i % 2, :],
                                        ALU.mult).then_inc(s["gated"], 1)

            def aT_copy(n, i):
                dve.wait_ge(s["aT_mm"], n + 1)
                if not isinstance(n, int) or n >= 2:
                    dve.wait_ge(s["y_mm"], n - 1)
                nc.vector.tensor_copy(aT[:, i % 2, :, :], aT_ps[:, 0:F].rearrange("p (c q) -> p c q", c=FC)).then_inc(s["aT"], 1)

            def tile(k, i):
                n = k * UE + i
                if i < UE - 1 or not isinstance(k, int) or k < NTE // UE - 1:
                    hT_low(n + 1, i + 1)
                gate(n, i)
                aT_copy(n, i)

            hT_low(0, 0)
            for i in range(UE):
                tile(0, i)
            with dve.Fori(1, NTE // UE - 1) as k:
                for i in range(UE):
                    tile(k, i)
            for i in range(UE):
                tile(NTE // UE - 1, i)

        @block.tensor
        def _(pe):
            pe.wait_ge(s["const_in"], 16)
            pe.wait_ge(s["ones"], 1)
            pe.wait_ge(s["ranked"], 1)
            chosen = route[0][:, :, :].rearrange("p t e -> p (t e)")
            nc.tensor.matmul(count_ps[:, 0:NT * E], const[:, C_TRI:C_TRI + P], chosen, start=True, stop=True)
            nc.tensor.matmul(count_ps[:, NT * E:2 * NT * E], ones[:, :], chosen, start=True, stop=True).then_inc(s["count_mm"], 1)
            pe.wait_ge(s["wgu_lo"], 2 * E)
            pe.wait_ge(s["wd_in"], 16)
            pe.wait_ge(s["slots_ready"], 2)

            def transposes(k, n, i):
                pe.wait_ge(s[f"gather{i % UE}"], (k + i // UE) * 16 + 16)
                if not isinstance(n, int) or n >= 2:
                    pe.wait_ge(s["hT_lo"], n - 1)
                for c in range(HC):
                    last = nc.tensor.transpose(hT_ps[i % 2][:, c * P:(c + 1) * P], hs[:, i % UE, c * P:(c + 1) * P], ident)
                last.then_inc(s["hT_mm"], 1)

            def up(n, i, e):
                pe.wait_ge(s["hT_lo"], n + 1)
                if not isinstance(n, int) or n >= 2:
                    pe.wait_ge(s["gated"], n - 1)
                for c in range(HC):
                    a = both(hT, every, i % 2, c, every)
                    w = [wgu[j][:, bass.ds(e * HC + c, 1), :].rearrange("p a f -> p (a f)") for j in range(2)]
                    last = product(nc, gu_ps[i % 2][:, :], a, w, c == 0, c == HC - 1)
                last.then_inc(s["gu_mm"], 1)

            def down(n, i, e):
                pe.wait_ge(s["aT"], n + 1)
                if not isinstance(n, int) or n >= 2:
                    pe.wait_ge(s["y_sb"], n - 1)
                for c in range(FC):
                    last = nc.tensor.matmul(y_ps[i % 2][:, :], aT[:, i % 2, c, :],
                                            wd[:, bass.ds(e * FC + c, 1), :].rearrange("p a f -> p (a f)"),
                                            start=c == 0, stop=c == FC - 1)
                last.then_inc(s["y_mm"], 1)

            def gated_transposes(n, i):
                pe.wait_ge(s["gated"], n + 1)
                if not isinstance(n, int) or n >= 1:
                    pe.wait_ge(s["aT"], n)
                for c in range(FC):
                    last = nc.tensor.transpose(aT_ps[:, c * P:(c + 1) * P], gated[:, i % 2, c * P:(c + 1) * P], ident)
                last.then_inc(s["aT_mm"], 1)

            def expert_of(n):
                column = expert[0:1, n:n + 1] if isinstance(n, int) else expert[0:1, bass.ds(n, 1)]
                return pe.value_load(column, min_val=0, max_val=E - 1)

            def tile(k, i):
                n = k * UE + i
                up(n, i, expert_of(n))
                if i < UE - 1 or not isinstance(k, int) or k < NTE // UE - 1:
                    transposes(k, n + 1, i + 1)
                if not (first(k) and i == 0):
                    down(n - 1, i - 1, expert_of(n - 1))
                gated_transposes(n, i)

            transposes(0, 0, 0)
            for i in range(UE):
                tile(0, i)
            with pe.Fori(1, NTE // UE - 1) as k:
                for i in range(UE):
                    tile(k, i)
            for i in range(UE):
                tile(NTE // UE - 1, i)
            down(NTE - 1, UE - 1, expert_of(NTE - 1))


def program(nc, d, out):
    def dram(name, *shape, dt=F32):
        return nc.dram_tensor(name, shape, dt).ap()

    x1, h = dram("x1", T, H), dram("h", T + P, H)
    probs, nkv = dram("probs", NT, P, NH * S), dram("nkv", T, KVR)
    table = dram("table", P, NTE * 2, dt=U32)

    def memory(stack):
        taken = []

        def semaphore(name):
            taken.append(nc.alloc_semaphore(name))
            return taken[-1]

        def finish():
            if taken:
                nc.clear_and_free_semaphores(taken)
                nc.all_engine_barrier()

        stack.callback(finish)
        return (lambda name, shape, dt: stack.enter_context(nc.sbuf_tensor(name, shape, dt)),
                lambda name, shape, dt: stack.enter_context(nc.psum_tensor(name, shape, dt)),
                semaphore)

    with ExitStack() as stack:
        cross_attention(nc, *memory(stack), d, x1)
    with ExitStack() as stack:
        latent_scores(nc, *memory(stack), d, x1, probs, nkv)
    with ExitStack() as outer:
        sb, _, _ = memory(outer)
        logits = sb("logits", [P, NT, E], F32)
        with ExitStack() as stack:
            latent_values(nc, *memory(stack), d, x1, probs, nkv, h[0:T, :], out[0:T, :], logits)
        with ExitStack() as stack:
            experts(nc, *memory(stack), d, h, table, out, logits)


def prepare(a):
    def chunks(w):
        return np.ascontiguousarray(w.reshape(-1, P, w.shape[-1]).transpose(1, 0, 2))

    a = {k: np.asarray(v) for k, v in a.items()}
    halves = a["L0_attn_W_krope"].reshape(H, RH, 2).transpose(0, 2, 1).reshape(H, ROPE)
    rope = a["L0_attn_W_dq_rope"].reshape(QR, NH // HJ, HJ, RH, 2).transpose(0, 1, 4, 2, 3).reshape(QR, NH * ROPE)
    gate_up = np.concatenate([a["L0_ffn_w_gate"], a["L0_ffn_w_up"]], axis=2).reshape(E, HC, P, 2 * F)
    return {
        "x": np.ascontiguousarray(a["x"].reshape(T, H)),
        "ctxT": np.ascontiguousarray(a["ctx_512"][:, :S, :].reshape(T, L).T),
        "const": constants(),
        "xa_WqT": chunks(a["L0_xattn_Wq"].T),
        "xa_WkvT": np.ascontiguousarray(a["L0_xattn_Wkv_expand"].T),
        "xa_WoutT": chunks(a["L0_xattn_Wout"].T),
        "q_scale": np.ascontiguousarray(a["L0_attn_q_scale"].reshape(QC, P).T),
        "kv_scale": a["L0_attn_kv_scale"].reshape(P, 1),
        "ls_Wc": chunks(np.concatenate([a["L0_attn_W_cq"], a["L0_attn_W_ckv"], halves], axis=1)),
        "ls_WdqT": np.ascontiguousarray(a["L0_attn_W_dq_nope"].reshape(QR, NH, NOPE).transpose(2, 1, 0)),
        "ls_WdkT": np.ascontiguousarray(a["L0_attn_W_dk_nope"].reshape(KVR, NH, NOPE).transpose(2, 1, 0)),
        "ls_Wrope": chunks(rope),
        "lv_WdvT": np.ascontiguousarray(a["L0_attn_W_dv"].reshape(KVR, NH, VD).transpose(2, 1, 0)),
        "lv_Wo": np.ascontiguousarray(a["L0_attn_W_o"].reshape(NH, VD, H).transpose(1, 0, 2)),
        "lv_Wgu": chunks(np.concatenate([a["L0_ffn_sw_gate"], a["L0_ffn_sw_up"]], axis=1)),
        "lv_Wd": chunks(a["L0_ffn_sw_down"]),
        "lv_Wr": chunks(a["L0_ffn_router_w"]),
        "rms_weight": np.ascontiguousarray(a["L0_ffn_rms_weight"].reshape(HC, P).T),
        "ex_Wgu": np.ascontiguousarray(gate_up.transpose(2, 0, 1, 3).reshape(P, E * HC, 2 * F)),
        "ex_Wd": np.ascontiguousarray(a["L0_ffn_w_down"].reshape(E, FC, P, H).transpose(2, 0, 1, 3).reshape(P, E * FC, H)),
    }


def kernel(**inputs):
    import concourse.bacc as bacc
    from concourse.bass_utils import run_bass_kernel_spmd

    nc = bacc.Bacc("TRN2", target_bir_lowering=False, num_devices=1)
    arrays = {f"in_{name}": a for name, a in prepare(inputs).items()}
    d = {name[3:]: nc.dram_tensor(name, a.shape, mybir.dt.from_np(a.dtype), kind="ExternalInput").ap()
         for name, a in arrays.items()}
    out = nc.dram_tensor("out", (T + P, H), F32, kind="ExternalOutput").ap()
    program(nc, d, out)
    r = run_bass_kernel_spmd(nc, [arrays], core_ids=[0])
    return r.results[0]["out"][:T].reshape(B, S, H)
```

```python
from contextlib import ExitStack

import numpy as np

import concourse.bass as bass
from concourse import mybir

F32 = mybir.dt.float32
F32R = mybir.dt.float32r
I32 = mybir.dt.int32
U32 = mybir.dt.uint32
ALU = mybir.AluOpType
ACT = mybir.ActivationFunctionType
AX = mybir.AxisListType

B, S, H = 128, 32, 512
T = B * S
P = 128
HC = H // P
NT = T // P
TG = 4
G = NT // TG
GW = TG * P
BT = P // S
NH = 16
HD = H // NH
L = 128
QR, KVR, NOPE, ROPE, VD = 256, 128, 128, 64, 128
QC = QR // P
RH = ROPE // 2
CW = QR + KVR + ROPE
HJ = P // HD
E, F = 8, 256
FC = F // P
TOPK = 2
NTE = T * TOPK // P + E
SLOTS = NTE * P
LN_EPS = 1e-5
RMS_EPS = 1e-6
MASKED = -1e30
XA_SCALE = float(np.float32(1.0) / np.sqrt(np.float32(HD)))
MLA_SCALE = float(np.float32(1.0) / np.sqrt(np.float32(NOPE + ROPE)))
RSQRT_MAGIC = float(0x5F3759DF)

C_IDENT, C_TRI, C_MASK = 0, P, 2 * P
C_COS_D = C_MASK + S
C_SIN_D = C_COS_D + S
C_COS_P = C_SIN_D + S
C_SIN_P = C_COS_P + RH
C_COUNT = C_SIN_P + RH
C_TOKEN = C_COUNT + P
C_FIRST = C_TOKEN + NT
C_PAD = C_FIRST + E
C_END = C_PAD + 1


def constants():
    c = np.zeros((P, C_END), np.float32)
    row = np.arange(P)
    pos = row % S
    c[:, C_IDENT:C_IDENT + P] = np.eye(P)
    c[:, C_TRI:C_TRI + P] = row[:, None] < row[None, :]
    c[:, C_MASK:C_MASK + S] = np.where(np.arange(S)[None, :] <= pos[:, None], 0.0, MASKED)
    freq = (np.float32(1.0) / np.power(np.float32(10000.0), np.arange(RH, dtype=np.float32) * np.float32(2.0) / np.float32(ROPE))).astype(np.float32)
    angle = np.arange(S, dtype=np.float32)[:, None] * freq[None, :]
    cos, sin = np.cos(angle).astype(np.float32), np.sin(angle).astype(np.float32)
    c[:, C_COS_D:C_COS_D + S] = cos.T[row % RH]
    c[:, C_SIN_D:C_SIN_D + S] = sin.T[row % RH]
    c[:, C_COS_P:C_COS_P + RH] = cos[pos] / NH
    c[:, C_SIN_P:C_SIN_P + RH] = sin[pos] / NH
    c[:, C_COUNT:C_COUNT + P] = np.arange(P)[None, :]
    c[:, C_TOKEN:C_TOKEN + NT] = np.arange(NT)[None, :] * P + row[:, None] + 1
    c[:, C_FIRST:C_FIRST + E] = E - np.arange(E)[None, :]
    c[:, C_PAD] = T + row + 1
    return c


class Steps:

    def __init__(self, engine, semaphore, done_before):
        self.engine, self.semaphore, self.value = engine, semaphore, done_before

    def __call__(self, instruction):
        self.value = self.value + 1
        instruction.then_inc(self.semaphore, 1)
        self.engine.wait_ge(self.semaphore, self.value)


def settle(engine, semaphore):
    engine.nop().then_inc(semaphore, 1)


RSQRT_STEPS = 10


def rsqrt(nc, step, y, u, v):
    step(nc.vector.tensor_scalar(y.bitcast(I32), v.bitcast(I32), -0.5, RSQRT_MAGIC, ALU.mult, ALU.add))
    for _ in range(3):
        step(nc.vector.tensor_tensor(u, y, y, ALU.mult))
        step(nc.vector.scalar_tensor_tensor(u, u, -0.5, v, ALU.mult, ALU.mult))
        step(nc.vector.scalar_tensor_tensor(y, u, 1.5, y, ALU.add, ALU.mult))


def product(nc, out, a, b, first=True, last=True):
    nc.tensor.matmul(out, a[0], b[0], start=first, stop=False)
    nc.tensor.matmul(out, a[0], b[1], start=False, stop=False)
    return nc.tensor.matmul(out, a[1], b[0], start=False, stop=last)


def both(pair, *index):
    return pair[0][index], pair[1][index]


def dyn(g):
    return g if isinstance(g, int) else bass.ds(g, 1)


def group_of(view, g):
    if isinstance(g, int):
        return view[g]
    return view[bass.ds(g, 1)].rearrange("a p t d -> p (a t) d")


def columns_of(view, g):
    return view[:, g * GW:(g + 1) * GW] if isinstance(g, int) else view[:, bass.ds(g * GW, GW)]


def cross_attention(nc, sb, pb, sem, d, x1_dram, front, carried):
    x_v = d["x"].rearrange("(g t p) d -> g p t d", t=TG, p=P)
    x1_v = x1_dram.rearrange("(g t p) d -> g p t d", t=TG, p=P)

    const = sb("xa_const", [P, C_END], F32)
    ident = const[:, C_IDENT:C_IDENT + P]
    mask = const[:, C_MASK:C_MASK + S]
    stage = sb("xa_stage", [P, HC, H], F32)
    wq = [sb(f"xa_wq{i}", [P, HC, H], F32R) for i in range(2)]
    wkv = [sb(f"xa_wkv{i}", [P, 2 * H], F32R) for i in range(2)]
    wo = [sb(f"xa_wo{i}", [P, HC, H], F32R) for i in range(2)]
    x_in, xn = front
    xres = sb("xa_xres", [P, TG, H], F32)
    xT = [sb(f"xa_xT{i}", [P, HC, GW], F32R) for i in range(2)]
    cin = sb("xa_ctx", [P, GW], F32)
    cT = [sb(f"xa_cT{i}", [P, GW], F32R) for i in range(2)]
    qT = sb("xa_qT", [P, HC, GW], F32)
    kbd = sb("xa_kbd", [P, TG * BT, HC, P], F32)
    val = sb("xa_v", [P, TG, H], F32)
    sc = sb("xa_sc", [P, 2, NH, S], F32)
    ex = sb("xa_ex", [P, 2, NH, S], F32)
    smx = sb("xa_max", [P, 2, NH], F32)
    ssum = sb("xa_sum", [P, NH], F32)
    srec = sb("xa_rec", [P, 2, NH], F32)
    pTc = sb("xa_pTc", [P, 2, NH, S], F32)
    pT = sb("xa_pT", [P, TG, NH, P], F32)
    oT = [sb(f"xa_oT{i}", [P, HC, P], F32R) for i in range(2)]
    st = sb("xa_st", [P, TG, 6], F32)
    mv = sb("xa_mv", [P, TG, 2], F32)
    var = sb("xa_var", [P, TG], F32)
    rstd = sb("xa_rstd", [P, TG], F32)
    tmp = sb("xa_tmp", [P, TG], F32)
    nbias = sb("xa_nb", [P, TG], F32)

    ring = [pb(f"xa_ring{i}", [P, H], F32) for i in range(4)]
    s_ps = [pb(f"xa_s{i}", [P, H], F32) for i in range(2)]
    pv_ps = pb("xa_pv", [P, H], F32)
    out_ps = pb("xa_out", [P, H], F32)

    k_ps = [s_ps[0], s_ps[1], pv_ps, out_ps]

    names = """const_in wkv_in wq_in wo_in x_in ctx_in xres_in x1_out zeroed w_hi w_lo moments stats xn ctx_hi ctx_lo
        xT_mm xT_hi xT_lo q_mm q_sb k_mm k_bd v_mm v_sb s_mm s_read s_max s_sub s_exp s_rec s_prob pT expanded
        pv_mm o_hi o_lo out_mm x1 ln_step sm_step settled""".split()
    s = {n: sem("xa_" + n) for n in names}
    weights = [("xa_WkvT", "wkv_in", wkv[0][:, :], wkv[1][:, :], xres[:, 0:2, :].rearrange("p a b -> p (a b)")),
               ("xa_WqT", "wq_in", wq[0][:, :, :], wq[1][:, :, :], stage[:, :, :]),
               ("xa_WoutT", "wo_in", wo[0][:, :, :], wo[1][:, :, :], stage[:, :, :])]

    def first(g):
        return isinstance(g, int) and g == 0

    def heads(a):
        return a.unsqueeze(2).broadcast_to([P, NH, S])

    def place_keys(copy, m, js):
        for j in js:
            rows = slice(j * HD, (j + 1) * HD)
            last = copy(kbd[rows, :, m, j * S:(j + 1) * S], k_ps[m][rows, :].rearrange("p (b k) -> p b k", k=S))
        last.then_inc(s["k_bd"], 1)

    block = nc.Block()
    with block:

        @block.sync
        def _(sp):
            def load_x(g):
                if not first(g):
                    sp.wait_ge(s["xn"], g * TG)
                sp.dma_start(x_in[:, :, :], group_of(x_v, g)).then_inc(s["x_in"], 16)

            def load_context(g):
                if not first(g):
                    sp.wait_ge(s["ctx_lo"], g)
                sp.dma_start(cin[:, :], columns_of(d["ctxT"], g)).then_inc(s["ctx_in"], 16)

            def store(g):
                sp.wait_ge(s["x1"], g * TG + TG + 1)
                sp.dma_start(group_of(x1_v, g), xres[:, :, :]).then_inc(s["x1_out"], 16)

            def residual(g):
                if not first(g):
                    sp.wait_ge(s["x1_out"], g * 16)
                sp.dma_start(xres[:, :, :], group_of(x_v, g)).then_inc(s["xres_in"], 16)

            load_x(0)
            sp.dma_start(const[:, :], d["const"]).then_inc(s["const_in"], 16)
            load_context(0)
            for n, (name, loaded, _, _, dst) in enumerate(weights):
                if n == 2:
                    sp.wait_ge(s["w_lo"], 2)
                sp.dma_start(dst, d[name]).then_inc(s[loaded], 16)
                if n == 1:
                    load_x(1)
            residual(0)
            load_context(1)
            load_x(2)
            load_context(2)
            with sp.Fori(2, G - 1) as g:
                load_x(g + 1)
                store(g - 2)
                load_context(g + 1)
                residual(g - 1)
            store(G - 3)
            residual(G - 2)
            sp.wait_ge(s["xn"], G * TG)
            sp.wait_ge(s["x1_out"], 16)
            sp.dma_start(x_in[:, :, :], x1_v[0]).then_inc(carried["x1_in"], 16)
            store(G - 2)
            residual(G - 1)
            for t in range(TG):
                sp.wait_ge(s["x1"], (G - 1) * TG + t + 2)
                sp.dma_start(x1_v[G - 1][:, t, :], xres[:, t, :]).then_inc(s["x1_out"], 16)
            sp.wait_ge(s["x1_out"], (G - 1 + TG) * 16)

        @block.gpsimd
        def _(pool):
            nc.gpsimd.memset(kbd[:, :, :, :], 0.0).then_inc(s["zeroed"], 1)

            def context_low(g):
                pool.wait_ge(s["ctx_hi"], g + 1)
                nc.gpsimd.tensor_tensor(cT[1][:, :], cin[:, :], cT[0][:, :].bitcast(F32),
                                        ALU.subtract).then_inc(s["ctx_lo"], 1)

            def subtract(g, t):
                pool.wait_ge(s["s_max"], g * TG + t + 1)
                nc.gpsimd.tensor_tensor(sc[:, t % 2], sc[:, t % 2], heads(smx[:, t % 2]),
                                        ALU.subtract).then_inc(s["s_sub"], 1)

            def normalise(g, t):
                pool.wait_ge(s["s_rec"], g * TG + t + 1)
                nc.gpsimd.tensor_tensor(ex[:, t % 2], ex[:, t % 2], heads(srec[:, t % 2]),
                                        ALU.mult).then_inc(s["s_prob"], 1)

            def body(g, back, ahead):
                if back:
                    normalise(g - 1, 2)
                    normalise(g - 1, 3)
                subtract(g, 0)
                subtract(g, 1)
                normalise(g, 0)
                subtract(g, 2)
                normalise(g, 1)
                subtract(g, 3)
                if ahead:
                    context_low(g + 1)

            context_low(0)
            nc.gpsimd.memset(pT[:, :, :, :], 0.0).then_inc(s["zeroed"], 1)
            body(0, False, True)
            with pool.Fori(1, G - 1) as g:
                body(g, True, True)
            body(G - 1, True, False)
            normalise(G - 1, 2)
            normalise(G - 1, 3)

        @block.scalar
        def _(act):
            def normalise(g, t):
                if t == 0:
                    act.wait_ge(s["stats"], g + 1)
                    if not first(g):
                        act.wait_ge(s["xT_mm"], g * TG)
                nc.scalar.activation(xn[:, t, :], x_in[:, t, :], ACT.Identity, bias=nbias[:, t:t + 1],
                                     scale=rstd[:, t:t + 1]).then_inc(s["xn"], 1)

            def weight_high(n):
                _, loaded, hi, _, src = weights[n]
                act.wait_ge(s[loaded], 16)
                nc.scalar.copy(hi, src).then_inc(s["w_hi"], 1)

            def context_high(g):
                act.wait_ge(s["ctx_in"], g * 16 + 16)
                if not first(g):
                    act.wait_ge(s["v_mm"], g * TG)
                nc.scalar.copy(cT[0][:, :], cin[:, :]).then_inc(s["ctx_hi"], 1)

            def x_high(g, t):
                act.wait_ge(s["xT_mm"], g * TG + t + 1)
                nc.scalar.copy(xT[0][:, :, t * P:(t + 1) * P],
                               ring[t][:, :].rearrange("p (c q) -> p c q", c=HC)).then_inc(s["xT_hi"], 1)

            def keys(g, m):
                act.wait_ge(s["k_mm"], g * HC + m + 1)
                place_keys(nc.scalar.copy, m, (0, 1))

            def query(g, m):
                act.wait_ge(s["q_mm"], g * HC + m + 1)
                nc.scalar.copy(qT[:, m, :], ring[m][:, :]).then_inc(s["q_sb"], 1)

            def exponent(g, t):
                act.wait_ge(s["s_sub"], g * TG + t + 1)
                if not (first(g) and t < 2):
                    act.wait_ge(s["pT"], g * TG + t - 1)
                nc.scalar.activation(ex[:, t % 2], sc[:, t % 2], ACT.Exp, scale=XA_SCALE).then_inc(s["s_exp"], 1)

            def expand(g, t):
                act.wait_ge(s["pT"], g * TG + t + 1)
                act.wait_ge(s["pv_mm"], g * TG + t + 1)
                for b in range(BT):
                    rows = slice(b * S, (b + 1) * S)
                    last = nc.scalar.copy(pT[rows, t, :, b * S:(b + 1) * S], pTc[rows, t % 2])
                last.then_inc(s["expanded"], 1)

            def value(g, t):
                act.wait_ge(s["v_mm"], g * TG + t + 1)
                nc.scalar.copy(val[:, t, :], ring[t][:, :]).then_inc(s["v_sb"], 1)

            def out_high(g, t):
                act.wait_ge(s["pv_mm"], (g + 1) * TG + t + 1)
                nc.scalar.copy(oT[0][:, :, :], pv_ps[:, :].rearrange("p (c q) -> p c q", c=HC)).then_inc(s["o_hi"], 1)

            def body(g, back, ahead):
                x_high(g, 0)
                x_high(g, 1)
                if back:
                    exponent(g - 1, 3)
                x_high(g, 2)
                x_high(g, 3)
                if first(g):
                    act.wait_ge(s["zeroed"], 1)
                keys(g, 0)
                keys(g, 1)
                query(g, 0)
                if back:
                    expand(g - 1, 1)
                keys(g, 2)
                query(g, 1)
                keys(g, 3)
                query(g, 2)
                if back:
                    expand(g - 1, 2)
                query(g, 3)
                if first(g):
                    weight_high(2)
                for t in range(TG):
                    if back:
                        out_high(g - 1, t)
                    value(g, t)
                    if t == TG - 1 and ahead:
                        context_high(g + 1)
                    if t == 0 and back:
                        expand(g - 1, 3)
                    if t > 0:
                        exponent(g, t - 1)
                    if t >= 2 and ahead:
                        normalise(g + 1, 2 * t - 4)
                        normalise(g + 1, 2 * t - 3)
                if first(g):
                    act.wait_ge(s["zeroed"], 2)
                expand(g, 0)

            for t in range(TG):
                normalise(0, t)
            context_high(0)
            weight_high(0)
            weight_high(1)
            body(0, False, True)
            with act.Fori(1, G - 1) as g:
                body(g, True, True)
            body(G - 1, True, False)
            exponent(G - 1, 3)
            for t in range(TG):
                if t > 0:
                    expand(G - 1, t)
                out_high(G - 1, t)

        @block.vector
        def _(dve):
            dve.nop().then_inc(s["o_lo"], 1)
            dve.nop().then_inc(s["x1"], 1)

            def moments(g):
                dve.wait_ge(s["x_in"], g * 16 + 16)
                for t in range(TG):
                    last = nc.vector.bn_stats(st[:, t, :], x_in[:, t, :])
                last.then_inc(s["moments"], 1)

            def variance(g):
                step = Steps(dve, s["ln_step"], g * (RSQRT_STEPS + 3))
                dve.wait_ge(s["moments"], g + 1)
                if not first(g):
                    dve.wait_ge(s["xn"], g * TG)
                settle(dve, s["settled"])
                for t in range(TG):
                    last = nc.vector.bn_aggr(mv[:, t, :], st[:, t, :])
                step(last)
                step(nc.vector.tensor_scalar(var[:, :], mv[:, :, 1], LN_EPS, None, ALU.add))

            def scale(g):
                step = Steps(dve, s["ln_step"], g * (RSQRT_STEPS + 3) + 2)
                rsqrt(nc, step, rstd[:, :], tmp[:, :], var[:, :])
                step(nc.vector.scalar_tensor_tensor(nbias[:, :], mv[:, :, 0], -1.0, rstd[:, :], ALU.mult, ALU.mult))
                dve.nop().then_inc(s["stats"], 1)

            def weight_low(n):
                _, _, hi, lo, src = weights[n]
                dve.wait_ge(s["w_hi"], n + 1)
                nc.vector.tensor_tensor(lo, src, hi.bitcast(F32), ALU.subtract).then_inc(s["w_lo"], 1)

            def x_low(g, t):
                dve.wait_ge(s["xT_hi"], g * TG + t + 1)
                part = (slice(None), slice(None), slice(t * P, (t + 1) * P))
                nc.vector.tensor_tensor(xT[1][part], ring[t][:, :].rearrange("p (c q) -> p c q", c=HC),
                                        xT[0][part].bitcast(F32), ALU.subtract).then_inc(s["xT_lo"], 1)

            def keys(g, m):
                dve.wait_ge(s["k_mm"], g * HC + m + 1)
                place_keys(nc.vector.tensor_copy, m, (2, 3))

            def maximum(g, t):
                dve.wait_ge(s["s_mm"], g * TG + t + 1)
                if not (first(g) and t < 2):
                    dve.wait_ge(s["s_exp"], g * TG + t - 1)
                nc.vector.tensor_tensor(sc[:, t % 2], s_ps[t % 2][:, :].rearrange("p (h k) -> p h k", h=NH),
                                        mask.unsqueeze(1).broadcast_to([P, NH, S]), ALU.add).then_inc(s["s_read"], 1)
                dve.wait_ge(s["s_read"], g * TG + t + 1)
                nc.vector.tensor_reduce(smx[:, t % 2], sc[:, t % 2], AX.X, ALU.max).then_inc(s["s_max"], 1)

            def total(g, t):
                dve.wait_ge(s["s_exp"], g * TG + t + 1)
                nc.vector.tensor_reduce(ssum[:, :], ex[:, t % 2], AX.X, ALU.add).then_inc(s["sm_step"], 1)
                dve.wait_ge(s["sm_step"], g * TG + t + 1)
                nc.vector.reciprocal(srec[:, t % 2], ssum[:, :]).then_inc(s["s_rec"], 1)

            def turn(g, t):
                dve.wait_ge(s["s_prob"], g * TG + t + 1)
                if not (first(g) and t < 2):
                    dve.wait_ge(s["expanded"], g * TG + t - 1)
                nc.vector.transpose(pTc[:, t % 2], ex[:, t % 2]).then_inc(s["pT"], 1)

            def out_low(g, t):
                dve.wait_ge(s["o_hi"], g * TG + t + 1)
                nc.vector.tensor_tensor(oT[1][:, :, :], pv_ps[:, :].rearrange("p (c q) -> p c q", c=HC),
                                        oT[0][:, :, :].bitcast(F32), ALU.subtract).then_inc(s["o_lo"], 1)

            def add(g, t):
                if t == 0:
                    dve.wait_ge(s["xres_in"], g * 16 + 16)
                dve.wait_ge(s["out_mm"], g * TG + t + 1)
                nc.vector.tensor_tensor(xres[:, t, :], out_ps[:, :], xres[:, t, :], ALU.add).then_inc(s["x1"], 1)

            def body(g, back, ahead):
                if back:
                    total(g - 1, 2)
                for t in range(TG):
                    x_low(g, t)
                if back:
                    turn(g - 1, 2)
                if first(g):
                    dve.wait_ge(s["zeroed"], 1)
                keys(g, 0)
                keys(g, 1)
                if back:
                    total(g - 1, 3)
                keys(g, 2)
                keys(g, 3)
                if back:
                    turn(g - 1, 3)
                if ahead:
                    moments(g + 1)
                if first(g):
                    weight_low(2)
                for t in range(TG):
                    if back:
                        out_low(g - 1, t)
                    if t >= 2:
                        total(g, t - 2)
                    maximum(g, t)
                    if t >= 2:
                        turn(g, t - 2)
                    if back:
                        add(g - 1, t)
                    if t == 0 and ahead:
                        variance(g + 1)
                    if t == 1 and ahead:
                        scale(g + 1)

            moments(0)
            variance(0)
            scale(0)
            weight_low(0)
            weight_low(1)
            body(0, False, True)
            with dve.Fori(1, G - 1) as g:
                body(g, True, True)
            body(G - 1, True, False)
            total(G - 1, 2)
            turn(G - 1, 2)
            total(G - 1, 3)
            turn(G - 1, 3)
            for t in range(TG):
                out_low(G - 1, t)
                add(G - 1, t)

        @block.tensor
        def _(pe):
            pe.nop().then_inc(s["pv_mm"], TG)
            pe.wait_ge(s["const_in"], 16)

            def transposes(g, t):
                pe.wait_ge(s["xn"], g * TG + t + 1)
                if not first(g):
                    pe.wait_ge(s["v_sb"], (g - 1) * TG + t + 1)
                for c in range(HC):
                    last = nc.tensor.transpose(ring[t][:, c * P:(c + 1) * P], xn[:, t, c * P:(c + 1) * P], ident)
                last.then_inc(s["xT_mm"], 1)

            def keys(g, m):
                if m == 0:
                    pe.wait_ge(s["ctx_lo"], g + 1)
                if not first(g):
                    name, value = [("s_read", g * TG - 1), ("s_read", g * TG), ("o_lo", (g - 1) * TG + 1),
                                   ("x1", (g - 1) * TG + 1)][m]
                    pe.wait_ge(s[name], value)
                product(nc, k_ps[m][:, :], both(wkv, slice(None), slice(m * P, (m + 1) * P)),
                        both(cT, slice(None), slice(None))).then_inc(s["k_mm"], 1)

            def queries(g, m):
                pe.wait_ge(s["xT_lo"], g * TG + TG)
                for c in range(HC):
                    last = product(nc, ring[m][:, :], both(wq, slice(None), c, slice(m * P, (m + 1) * P)),
                                   both(xT, slice(None), c, slice(None)), c == 0, c == HC - 1)
                last.then_inc(s["q_mm"], 1)

            def values(g, t):
                pe.wait_ge(s["q_sb"], g * HC + t + 1)
                product(nc, ring[t][:, :], both(cT, slice(None), slice(t * P, (t + 1) * P)),
                        both(wkv, slice(None), slice(H, 2 * H))).then_inc(s["v_mm"], 1)

            def scores(g, t):
                if t == 0:
                    pe.wait_ge(s["q_sb"], g * HC + HC)
                if t >= 2:
                    pe.wait_ge(s["s_read"], g * TG + t - 1)
                for b in range(BT):
                    token = t * P + b * S
                    for m in range(HC):
                        last = nc.tensor.matmul(s_ps[t % 2][b * S:(b + 1) * S, m * P:(m + 1) * P],
                                                qT[:, m, token:token + S], kbd[:, t * BT + b, m, :],
                                                start=True, stop=True)
                last.then_inc(s["s_mm"], 1)

            def weighted(g, t):
                pe.wait_ge(s["expanded"], g * TG + t + 1)
                if t == 0:
                    pe.wait_ge(s["v_sb"], g * TG + TG)
                pe.wait_ge(s["o_lo"], g * TG + t + 1)
                for m in range(HC):
                    for j in range(HJ):
                        h = m * HJ + j
                        last = nc.tensor.matmul(pv_ps[j * HD:(j + 1) * HD, m * P:(m + 1) * P],
                                                val[:, t, h * HD:(h + 1) * HD], pT[:, t, h, :],
                                                start=True, stop=True)
                last.then_inc(s["pv_mm"], 1)

            def outputs(g, t):
                pe.wait_ge(s["o_lo"], g * TG + t + 2)
                pe.wait_ge(s["x1"], g * TG + t + 1)
                for m in range(HC):
                    last = product(nc, out_ps[:, :], both(oT, slice(None), m, slice(None)),
                                   both(wo, slice(None), m, slice(None)), m == 0, m == HC - 1)
                last.then_inc(s["out_mm"], 1)

            def body(g, back):
                for t in range(TG):
                    transposes(g, t)
                if first(g):
                    pe.wait_ge(s["w_lo"], 1)
                for m in range(HC):
                    keys(g, m)
                if first(g):
                    pe.wait_ge(s["w_lo"], 2)
                for m in range(HC):
                    queries(g, m)
                pe.wait_ge(s["k_bd"], (g * HC + HC) * 2)
                for t in range(TG):
                    if back:
                        weighted(g - 1, t)
                    values(g, t)
                    scores(g, t)
                    if back:
                        outputs(g - 1, t)

            body(0, False)
            pe.wait_ge(s["w_lo"], 3)
            with pe.Fori(1, G) as g:
                body(g, True)
            for t in range(TG):
                weighted(G - 1, t)
                outputs(G - 1, t)


RMS_STEPS = RSQRT_STEPS


def value_weights(front):
    return front[1][:, :, :].rearrange("p a b -> p (a b)").rearrange("p (h k) -> p h k", h=NH)


def latent_scores(nc, sb, pb, sem, d, x1_dram, probs_dram, nkv_dram, front, carried):
    x_v = x1_dram.rearrange("(g t p) d -> g p t d", t=TG, p=P)
    nkv_v = nkv_dram.rearrange("(g t p) d -> g p t d", t=TG, p=P)

    const = sb("ls_const", [P, C_COUNT], F32)
    ident = const[:, C_IDENT:C_IDENT + P]
    mask = const[:, C_MASK:C_MASK + S]
    cos_d, sin_d = (const[:, c:c + S].unsqueeze(1).broadcast_to([P, GW // S, S]) for c in (C_COS_D, C_SIN_D))
    cos_p, sin_p = (const[:, c:c + RH].unsqueeze(1).broadcast_to([P, TG, RH]) for c in (C_COS_P, C_SIN_P))
    qscale = sb("ls_qscale", [P, QC], F32)
    kvscale = sb("ls_kvscale", [P, 1], F32)
    wc = [sb(f"ls_wc{i}", [P, HC, CW], F32R) for i in range(2)]
    wabs = [sb(f"ls_wabs{i}", [P, QC, NH * KVR], F32R) for i in range(2)]
    wrope = [sb(f"ls_wrope{i}", [P, QC, NH * ROPE], F32R) for i in range(2)]
    x_in, xn = front
    xT = [sb(f"ls_xT{i}", [P, HC, GW], F32R) for i in range(2)]
    craw = sb("ls_craw", [P, TG, CW], F32)
    kprod = [sb(f"ls_kprod{i}", [P, TG, RH], F32) for i in range(4)]
    cqT = [sb(f"ls_cqT{i}", [P, QC, GW], F32R) for i in range(2)]
    nkvT = sb("ls_nkvT", [P, GW], F32)
    krz = [sb(f"ls_krz{i}", [P, HJ, GW], F32) for i in range(2)]
    qr = [sb(f"ls_qr{i}", [P, NH // HJ, GW], F32) for i in range(2)]
    rot = [sb(f"ls_rot{i}", [P, GW], F32) for i in range(4)]
    krep = [r[:, :].rearrange("p (t j r) -> p t j r", t=TG, j=HJ) for r in rot[0:2]]
    qa = sb("ls_qa", [P, NH, GW], F32)
    sc = sb("ls_sc", [P, 2, NH, S], F32)
    ex = sb("ls_ex", [P, 2, NH, S], F32)
    smx = sb("ls_max", [P, 2, NH], F32)
    ssum = sb("ls_sum", [P, NH], F32)
    srec = sb("ls_rec", [P, 2, NH], F32)
    pT = sb("ls_pT", [P, NH * S], F32)
    parts = [sb(f"ls_parts{i}", [P, 2, NH * S], F32R) for i in range(2)]
    st = sb("ls_st", [P, TG, 6], F32)
    mv = sb("ls_mv", [P, TG, 2], F32)
    var = sb("ls_var", [P, TG], F32)
    rstd = sb("ls_rstd", [P, TG], F32)
    tmp = sb("ls_tmp", [P, TG], F32)
    nbias = sb("ls_nb", [P, TG], F32)
    squares = sb("ls_squares", [P, QR], F32)
    sumsq = sb("ls_sumsq", [P, 2, TG], F32)
    rvar = sb("ls_rvar", [P, 2, TG], F32)
    rrms = sb("ls_rrms", [P, 2, TG], F32)
    rtmp = sb("ls_rtmp", [P, 2, TG], F32)

    wdq_st, wdk_st = qa[:, :, 0:QR], qa[:, :, QR:QR + KVR]
    wrope_st = qr[0][:, :, :].rearrange("p a b -> p (a b)").rearrange("p (c n) -> p c n", c=QC)
    wc_st = qr[1][:, :, 0:CW]

    ring = [pb(f"ls_ring{i}", [P, H], F32) for i in range(4)]
    s_ps = [pb(f"ls_s{i}", [P, H], F32) for i in range(2)]
    spare = [pb(f"ls_spare{i}", [P, H], F32) for i in range(2)]
    qa_ps = [ring[3], ring[0], spare[0], spare[1]]
    kr_ps = [ring[3], spare[0]]
    fold_ps = [spare[0], spare[1], s_ps[0], s_ps[1]]

    names = """const_in wc_in wdq_in wrope_in nkv_out probs_out0 probs_out1 zeroed wc_hi wc_lo wrope_hi wrope_lo
        wabs_mm wabs_hi wabs_lo moments stats xn xT_mm xT_hi xT_lo c_mm c_sq c_raw c_ready cq_T nkv_T kr_T cq_hi cq_lo
        nkv_sb kr_sb rope_mm rope_prod rope_sb qa_mm qa_sb s_mm s_out s_masked s_max s_sub s_exp s_sum s_rec s_prob pT p_hi p_lo
        ln_step rms_step key_step settled""".split()
    s = {n: sem("ls_" + n) for n in names}
    s["x_in"] = carried["x1_in"]
    every = slice(None)

    def first(g):
        return isinstance(g, int) and g == 0

    def heads(a):
        return a.unsqueeze(2).broadcast_to([P, NH, S])

    block = nc.Block()
    with block:

        @block.sync
        def _(sp):
            for i in range(2):
                sp.nop().then_inc(s[f"probs_out{i}"], 32)

            def loads(g):
                if not first(g):
                    sp.wait_ge(s["xn"], g * TG)
                sp.dma_start(x_in[:, :, :], group_of(x_v, g)).then_inc(s["x_in"], 16)

            def stores(g):
                sp.wait_ge(s["c_ready"], g + 1)
                sp.dma_start(group_of(nkv_v, g), craw[:, :, QR:QR + KVR]).then_inc(s["nkv_out"], 16)

            def probs(g):
                for t in range(TG):
                    n = g * TG + t
                    sp.wait_ge(s["p_lo"], n + 2)
                    for part, dram in zip(parts, probs_dram):
                        dst = dram[n] if isinstance(n, int) else dram[bass.ds(n, 1)].rearrange("a p n -> p (a n)")
                        sp.dma_start(dst, part[:, t % 2, :].bitcast(F32)).then_inc(s[f"probs_out{t % 2}"], 16)

            sp.dma_start(const[:, :], d["const"][:, 0:C_COUNT]).then_inc(s["const_in"], 16)
            sp.dma_start(qscale[:, :], d["q_scale"]).then_inc(s["const_in"], 16)
            sp.dma_start(kvscale[:, :], d["kv_scale"]).then_inc(s["const_in"], 16)
            sp.dma_start(wdq_st, d["ls_WdqT"]).then_inc(s["wdq_in"], 16)
            sp.dma_start(wdk_st, d["ls_WdkT"]).then_inc(s["wdq_in"], 16)
            sp.dma_start(wc_st, d["ls_Wc"]).then_inc(s["wc_in"], 16)
            sp.dma_start(wrope_st, d["ls_Wrope"]).then_inc(s["wrope_in"], 16)
            loads(1)
            stores(0)
            with sp.Fori(1, G - 1) as g:
                loads(g + 1)
                stores(g)
                probs(g - 1)
            stores(G - 1)
            probs(G - 2)
            sp.wait_ge(s["xT_mm"], G * TG)
            sp.dma_start(value_weights(front), d["lv_WdvT"]).then_inc(carried["wdv_in"], 16)
            sp.wait_ge(s["xn"], G * TG)
            sp.dma_start(front[0][:, :, :], d["lv_Wo"][:, 0:TG, :]).then_inc(carried["wo_in0"], 16)
            probs(G - 1)
            sp.wait_ge(s["nkv_out"], G * 16)
            for i in range(2):
                sp.wait_ge(s[f"probs_out{i}"], (NT // 2 + 1) * 32)

        @block.gpsimd
        def _(pool):
            for i in range(2):
                nc.gpsimd.memset(krz[i][:, :, :], 0.0).then_inc(s["zeroed"], 1)

            def rotate(g, i):
                pool.wait_ge(s["rope_prod"], g * 4 + i + 1)
                nc.gpsimd.tensor_tensor(qr[0][:, i, :], rot[0][:, :], rot[1][:, :], ALU.subtract)
                nc.gpsimd.tensor_tensor(qr[1][:, i, :], rot[2][:, :], rot[3][:, :], ALU.add).then_inc(s["rope_sb"], 1)

            def subtract(g, t):
                pool.wait_ge(s["s_max"], g * TG + t + 1)
                nc.gpsimd.tensor_tensor(sc[:, t % 2], sc[:, t % 2], heads(smx[:, t % 2]),
                                        ALU.subtract).then_inc(s["s_sub"], 1)

            def normalise(g, t):
                pool.wait_ge(s["s_rec"], g * TG + t + 1)
                nc.gpsimd.tensor_tensor(ex[:, t % 2], ex[:, t % 2], heads(srec[:, t % 2]),
                                        ALU.mult).then_inc(s["s_prob"], 1)

            def softmax(g):
                subtract(g, 0)
                subtract(g, 1)
                normalise(g, 0)
                subtract(g, 2)
                normalise(g, 1)

            def body(g, back):
                if back:
                    softmax(g - 1)
                rotate(g, 0)
                if back:
                    subtract(g - 1, 3)
                    normalise(g - 1, 2)
                rotate(g, 1)
                if back:
                    normalise(g - 1, 3)
                rotate(g, 2)
                rotate(g, 3)

            body(0, False)
            with pool.Fori(1, G) as g:
                body(g, True)
            softmax(G - 1)
            subtract(G - 1, 3)
            normalise(G - 1, 2)
            normalise(G - 1, 3)

        @block.scalar
        def _(act):
            def normalise(g, t):
                if t == 0:
                    act.wait_ge(s["stats"], g + 1)
                    if not first(g):
                        act.wait_ge(s["xT_mm"], g * TG)
                nc.scalar.activation(xn[:, t, :], x_in[:, t, :], ACT.Identity, bias=nbias[:, t:t + 1],
                                     scale=rstd[:, t:t + 1]).then_inc(s["xn"], 1)

            act.nop().then_inc(s["s_exp"], 2)

            def exponent(g, t):
                act.wait_ge(s["s_sub"], g * TG + t + 1)
                act.wait_ge(s["pT"], g * TG + t + 1)
                nc.scalar.activation(ex[:, t % 2], sc[:, t % 2], ACT.Exp, scale=MLA_SCALE).then_inc(s["s_exp"], 1)

            def probs_high(g, t):
                act.wait_ge(s["pT"], g * TG + t + 3)
                act.wait_ge(s[f"probs_out{t % 2}"], (g * 2 + t // 2 + 1) * 32)
                nc.scalar.copy(parts[0][:, t % 2, :], pT[:, :]).then_inc(s["p_hi"], 1)

            def weights_high():
                act.wait_ge(s["wc_in"], 16)
                nc.scalar.copy(wc[0][:, :, :], wc_st).then_inc(s["wc_hi"], 1)
                for n in range(QC * 4):
                    c, q = divmod(n, 4)
                    act.wait_ge(s["wabs_mm"], n + 1)
                    nc.scalar.activation(wabs[0][:, c, q * H:(q + 1) * H], fold_ps[n % 4][:, :], ACT.Copy,
                                         scale=qscale[:, c:c + 1]).then_inc(s["wabs_hi"], 1)
                act.wait_ge(s["wrope_in"], 16)
                for c in range(QC):
                    nc.scalar.activation(wrope[0][:, c, :], wrope_st[:, c, :], ACT.Copy,
                                         scale=qscale[:, c:c + 1]).then_inc(s["wrope_hi"], 1)

            def body(g, back, ahead):
                for t in range(TG):
                    act.wait_ge(s["xT_mm"], g * TG + t + 1)
                    nc.scalar.copy(xT[0][:, :, t * P:(t + 1) * P],
                                   ring[t][:, :].rearrange("p (c q) -> p c q", c=HC)).then_inc(s["xT_hi"], 1)
                if first(g):
                    weights_high()
                if back:
                    exponent(g - 1, 0)
                for t in range(TG):
                    act.wait_ge(s["c_mm"], g * TG + t + 1)
                    if t == 0 and not first(g):
                        act.wait_ge(s["kr_T"], g * 2)
                        act.wait_ge(s["nkv_out"], g * 16)
                    for n, (a, z) in enumerate(((0, QR), (QR, QR + KVR))):
                        if not (first(g) and t == 0 and n == 0):
                            act.wait_ge(s["c_sq"], (g * TG + t) * 2 + n)
                        nc.scalar.activation(squares[:, 0:z - a], ring[t][:, a:z], ACT.Square,
                                             accum_out=sumsq[:, n, t:t + 1]).then_inc(s["c_sq"], 1)
                    nc.scalar.copy(craw[:, t, :], ring[t][:, 0:CW]).then_inc(s["c_raw"], 1)
                if back:
                    exponent(g - 1, 1)
                for n in range(2):
                    act.wait_ge(s["cq_T"], g * 2 + n + 1)
                    tok = slice(n * 2 * P, (n + 1) * 2 * P)
                    nc.scalar.copy(cqT[0][:, :, tok],
                                   ring[n][:, :].rearrange("p (t c q) -> p c t q", t=2, c=QC)
                                   ).then_inc(s["cq_hi"], 1)
                act.wait_ge(s["nkv_T"], g + 1)
                nc.scalar.activation(nkvT[:, :], ring[2][:, :], ACT.Copy, scale=kvscale[:, 0:1]).then_inc(s["nkv_sb"], 1)
                if first(g):
                    act.wait_ge(s["zeroed"], 2)
                for n in range(2):
                    act.wait_ge(s["kr_T"], g * 2 + n + 1)
                    for j in range(HJ):
                        rows = slice(j * RH, (j + 1) * RH)
                        last = nc.scalar.copy(krz[n][rows, j, :], kr_ps[n][rows, :])
                    last.then_inc(s["kr_sb"], 1)
                if back:
                    probs_high(g - 1, 0)
                    exponent(g - 1, 2)
                for h in range(NH):
                    act.wait_ge(s["qa_mm"], g * NH + h + 1)
                    nc.scalar.copy(qa[:, h, :], qa_ps[h % 4][:, :]).then_inc(s["qa_sb"], 1)
                    if back and h == 3:
                        probs_high(g - 1, 1)
                        exponent(g - 1, 3)
                    if back and h in (7, 11):
                        probs_high(g - 1, h // 4 + 1)
                    if h >= NH - TG and ahead:
                        normalise(g + 1, h - (NH - TG))

            for t in range(TG):
                normalise(0, t)
            act.wait_ge(s["const_in"], 48)
            body(0, False, True)
            with act.Fori(1, G - 1) as g:
                body(g, True, True)
            body(G - 1, True, False)
            for t in range(TG):
                exponent(G - 1, t)
                if t:
                    probs_high(G - 1, t - 1)
            probs_high(G - 1, 3)

        @block.vector
        def _(dve):
            def moments(g):
                dve.wait_ge(s["x_in"], g * 16 + 16)
                for t in range(TG):
                    last = nc.vector.bn_stats(st[:, t, :], x_in[:, t, :])
                last.then_inc(s["moments"], 1)

            def statistics(g):
                step = Steps(dve, s["ln_step"], g * (RSQRT_STEPS + 3))
                dve.wait_ge(s["moments"], g + 1)
                if not first(g):
                    dve.wait_ge(s["xn"], g * TG)
                settle(dve, s["settled"])
                for t in range(TG):
                    last = nc.vector.bn_aggr(mv[:, t, :], st[:, t, :])
                step(last)
                step(nc.vector.tensor_scalar(var[:, :], mv[:, :, 1], LN_EPS, None, ALU.add))
                rsqrt(nc, step, rstd[:, :], tmp[:, :], var[:, :])
                step(nc.vector.scalar_tensor_tensor(nbias[:, :], mv[:, :, 0], -1.0, rstd[:, :], ALU.mult, ALU.mult))
                dve.nop().then_inc(s["stats"], 1)

            def weights_low():
                dve.wait_ge(s["wc_hi"], 1)
                nc.vector.tensor_tensor(wc[1][:, :, :], wc_st, wc[0][:, :, :].bitcast(F32),
                                        ALU.subtract).then_inc(s["wc_lo"], 1)
                for n in range(QC * 4):
                    c, q = divmod(n, 4)
                    dve.wait_ge(s["wabs_hi"], n + 1)
                    nc.vector.scalar_tensor_tensor(wabs[1][:, c, q * H:(q + 1) * H], fold_ps[n % 4][:, :],
                                                   qscale[:, c:c + 1], wabs[0][:, c, q * H:(q + 1) * H].bitcast(F32),
                                                   ALU.mult, ALU.subtract).then_inc(s["wabs_lo"], 1)
                for c in range(QC):
                    dve.wait_ge(s["wrope_hi"], c + 1)
                    nc.vector.scalar_tensor_tensor(wrope[1][:, c, :], wrope_st[:, c, :], qscale[:, c:c + 1],
                                                   wrope[0][:, c, :].bitcast(F32), ALU.mult,
                                                   ALU.subtract).then_inc(s["wrope_lo"], 1)

            def xT_low(g):
                for t in range(TG):
                    dve.wait_ge(s["xT_hi"], g * TG + t + 1)
                    part = (every, every, slice(t * P, (t + 1) * P))
                    nc.vector.tensor_tensor(xT[1][part], ring[t][:, :].rearrange("p (c q) -> p c q", c=HC),
                                            xT[0][part].bitcast(F32), ALU.subtract).then_inc(s["xT_lo"], 1)

            def latents(g):
                step = Steps(dve, s["rms_step"], g * (RMS_STEPS + 2))
                dve.wait_ge(s["c_raw"], g * TG + TG)
                for n, width in enumerate((QR, KVR)):
                    last = nc.vector.tensor_scalar(rvar[:, n, :], sumsq[:, n, :], 1.0 / width, RMS_EPS, ALU.mult, ALU.add)
                    step(last)
                rsqrt(nc, step, rrms[:, :, :], rtmp[:, :, :], rvar[:, :, :])
                for t in range(TG):
                    for n, (a, z) in enumerate(((0, QR), (QR, QR + KVR))):
                        last = nc.vector.tensor_scalar(craw[:, t, a:z], craw[:, t, a:z], rrms[:, n, t:t + 1], None, ALU.mult)
                last.then_inc(s["c_ready"], 1)

            def keys(g):
                if not first(g):
                    dve.wait_ge(s["rope_sb"], g * 4)
                step = Steps(dve, s["key_step"], g * 2)
                k1, k2 = (craw[:, :, a:a + RH] for a in (QR + KVR, QR + KVR + RH))
                nc.vector.tensor_tensor(kprod[0][:, :, :], k1, cos_p, ALU.mult)
                nc.vector.tensor_tensor(kprod[1][:, :, :], k2, sin_p, ALU.mult)
                nc.vector.tensor_tensor(kprod[2][:, :, :], k1, sin_p, ALU.mult)
                step(nc.vector.tensor_tensor(kprod[3][:, :, :], k2, cos_p, ALU.mult))
                for n, op in enumerate((ALU.subtract, ALU.add)):
                    a, b = (kprod[2 * n + i][:, :, :].unsqueeze(2).broadcast_to([P, TG, HJ, RH]) for i in range(2))
                    last = nc.vector.tensor_tensor(krep[n][:, :, :, :], a, b, op)
                step(last)

            def maximum(g, t):
                dve.wait_ge(s["s_exp"], g * TG + t + 1)
                dve.wait_ge(s["s_mm"], g * TG + t + 1)
                nc.vector.transpose(sc[:, t % 2].rearrange("p h k -> p (h k)"), s_ps[t % 2][:, :]).then_inc(s["s_out"], 1)
                dve.wait_ge(s["s_out"], g * TG + t + 3)
                nc.vector.tensor_tensor(sc[:, t % 2], sc[:, t % 2], mask.unsqueeze(1).broadcast_to([P, NH, S]),
                                        ALU.add).then_inc(s["s_masked"], 1)
                dve.wait_ge(s["s_masked"], g * TG + t + 1)
                nc.vector.tensor_reduce(smx[:, t % 2], sc[:, t % 2], AX.X, ALU.max).then_inc(s["s_max"], 1)

            def total(g, t):
                dve.wait_ge(s["s_exp"], g * TG + t + 3)
                nc.vector.tensor_reduce(ssum[:, :], ex[:, t % 2], AX.X, ALU.add).then_inc(s["s_sum"], 1)
                dve.wait_ge(s["s_sum"], g * TG + t + 1)
                nc.vector.reciprocal(srec[:, t % 2], ssum[:, :]).then_inc(s["s_rec"], 1)

            def turn(g, t):
                dve.wait_ge(s["s_prob"], g * TG + t + 1)
                dve.wait_ge(s["p_lo"], g * TG + t + 1)
                nc.vector.transpose(pT[:, :], ex[:, t % 2].rearrange("p h k -> p (h k)")).then_inc(s["pT"], 1)

            def probs_low(g, t):
                dve.wait_ge(s["p_hi"], g * TG + t + 1)
                nc.vector.tensor_tensor(parts[1][:, t % 2, :], pT[:, :], parts[0][:, t % 2, :].bitcast(F32),
                                        ALU.subtract).then_inc(s["p_lo"], 1)

            def rotary(g, i):
                dve.wait_ge(s["rope_mm"], g * 8 + 2 * i + 2)
                if not (first(g) and i == 0):
                    dve.wait_ge(s["rope_sb"], g * 4 + i)
                for n, (half, table) in enumerate(((0, cos_d), (1, sin_d), (0, sin_d), (1, cos_d))):
                    last = nc.vector.tensor_tensor(rot[n][:, :].rearrange("p (b q) -> p b q", q=S),
                                                   ring[1 + half][:, :].rearrange("p (b q) -> p b q", q=S), table, ALU.mult)
                last.then_inc(s["rope_prod"], 1)

            def query_low(g, n):
                dve.wait_ge(s["cq_hi"], g * 2 + n + 1)
                tok = slice(n * 2 * P, (n + 1) * 2 * P)
                nc.vector.tensor_tensor(cqT[1][:, :, tok],
                                        ring[n][:, :].rearrange("p (t c q) -> p c t q", t=2, c=QC),
                                        cqT[0][:, :, tok].bitcast(F32).rearrange("p c (t q) -> p c t q", t=2),
                                        ALU.subtract).then_inc(s["cq_lo"], 1)

            def body(g, back, ahead):
                xT_low(g)
                if first(g):
                    weights_low()
                if back:
                    maximum(g - 1, 0)
                latents(g)
                if back:
                    maximum(g - 1, 1)
                    total(g - 1, 0)
                keys(g)
                query_low(g, 0)
                query_low(g, 1)
                if back:
                    maximum(g - 1, 2)
                    turn(g - 1, 0)
                    total(g - 1, 1)
                rotary(g, 0)
                if back:
                    probs_low(g - 1, 0)
                    maximum(g - 1, 3)
                    turn(g - 1, 1)
                    total(g - 1, 2)
                    probs_low(g - 1, 1)
                    turn(g - 1, 2)
                rotary(g, 1)
                if back:
                    total(g - 1, 3)
                    probs_low(g - 1, 2)
                    turn(g - 1, 3)
                rotary(g, 2)
                if ahead:
                    moments(g + 1)
                if back:
                    probs_low(g - 1, 3)
                if ahead:
                    statistics(g + 1)
                rotary(g, 3)

            dve.nop().then_inc(s["s_out"], 2)
            dve.nop().then_inc(s["pT"], 2)
            dve.nop().then_inc(s["p_lo"], 1)
            moments(0)
            statistics(0)
            dve.wait_ge(s["const_in"], 48)
            body(0, False, True)
            with dve.Fori(1, G - 1) as g:
                body(g, True, True)
            body(G - 1, True, False)
            maximum(G - 1, 0)
            maximum(G - 1, 1)
            total(G - 1, 0)
            maximum(G - 1, 2)
            turn(G - 1, 0)
            total(G - 1, 1)
            probs_low(G - 1, 0)
            maximum(G - 1, 3)
            turn(G - 1, 1)
            total(G - 1, 2)
            probs_low(G - 1, 1)
            turn(G - 1, 2)
            total(G - 1, 3)
            probs_low(G - 1, 2)
            turn(G - 1, 3)
            probs_low(G - 1, 3)

        @block.tensor
        def _(pe):
            pe.wait_ge(s["const_in"], 48)

            def fold():
                pe.wait_ge(s["wdq_in"], 32)
                for n in range(QC * 4):
                    c, q = divmod(n, 4)
                    if n >= 4:
                        pe.wait_ge(s["wabs_lo"], n - 3)
                    for i in range(4):
                        h = q * 4 + i
                        last = nc.tensor.matmul(fold_ps[n % 4][:, i * KVR:(i + 1) * KVR], wdq_st[:, h, c * P:(c + 1) * P],
                                                wdk_st[:, h, :], start=True, stop=True)
                    last.then_inc(s["wabs_mm"], 1)

            def scores(g, t):
                if t == 0:
                    pe.wait_ge(s["qa_sb"], g * NH + NH)
                    pe.wait_ge(s["rope_sb"], g * 4 + 4)
                    pe.wait_ge(s["kr_sb"], g * 2 + 2)
                pe.wait_ge(s["s_out"], g * TG + t + 1)
                for b in range(BT):
                    tok = slice(t * P + b * S, t * P + (b + 1) * S)
                    out = s_ps[t % 2][b * S:(b + 1) * S, :]
                    nc.tensor.matmul(out, nkvT[:, tok], qa[:, :, tok], start=True, stop=False)
                    for n in range(2):
                        for j in range(HJ):
                            last = nc.tensor.matmul(out.rearrange("p (i j q) -> p i j q", j=HJ, q=S)[:, :, j, :],
                                                    krz[n][:, j, tok], qr[n][:, :, tok], start=False,
                                                    stop=n == 1 and j == HJ - 1)
                last.then_inc(s["s_mm"], 1)

            def body(g, back):
                for t in range(TG):
                    pe.wait_ge(s["xn"], g * TG + t + 1)
                    if first(g):
                        pass
                    elif t in (1, 2):
                        pe.wait_ge(s["rope_prod"], g * 4)
                    else:
                        pe.wait_ge(s["qa_sb"], g * NH - 2)
                    for c in range(HC):
                        last = nc.tensor.transpose(ring[t][:, c * P:(c + 1) * P], xn[:, t, c * P:(c + 1) * P], ident)
                    last.then_inc(s["xT_mm"], 1)
                if back:
                    scores(g - 1, 0)
                if first(g):
                    fold()
                    pe.wait_ge(s["wc_lo"], 1)
                for t in range(TG):
                    pe.wait_ge(s["xT_lo"], g * TG + t + 1)
                    for c in range(HC):
                        last = product(nc, ring[t][:, 0:CW], both(xT, every, c, slice(t * P, (t + 1) * P)),
                                       both(wc, every, c, every), c == 0, c == HC - 1)
                    last.then_inc(s["c_mm"], 1)
                if back:
                    for t in range(1, TG):
                        scores(g - 1, t)
                if first(g):
                    pe.wait_ge(s["wabs_lo"], QC * 4)
                pe.wait_ge(s["c_ready"], g + 1)
                for n in range(2):
                    for i in range(2):
                        for c in range(QC):
                            last = nc.tensor.transpose(ring[n][:, (i * QC + c) * P:(i * QC + c + 1) * P],
                                                       craw[:, 2 * n + i, c * P:(c + 1) * P], ident)
                    last.then_inc(s["cq_T"], 1)
                for t in range(TG):
                    last = nc.tensor.transpose(ring[2][:, t * P:(t + 1) * P], craw[:, t, QR:QR + KVR], ident)
                last.then_inc(s["nkv_T"], 1)
                pe.wait_ge(s["key_step"], g * 2 + 2)
                for n in range(2):
                    for t in range(TG):
                        last = nc.tensor.transpose(kr_ps[n][:, t * P:(t + 1) * P],
                                                   krep[n][:, t, :, :].rearrange("p j r -> p (j r)"), ident)
                    last.then_inc(s["kr_T"], 1)
                if first(g):
                    pe.wait_ge(s["wrope_lo"], QC)
                for i in range(NH // HJ):
                    if i == 0:
                        pe.wait_ge(s["cq_lo"], g * 2 + 2)
                        pe.wait_ge(s["nkv_sb"], g + 1)
                    else:
                        pe.wait_ge(s["rope_prod"], g * 4 + i)
                    for half in range(2):
                        m = 2 * i + half
                        for c in range(QC):
                            last = product(nc, ring[1 + half][:, :], both(wrope, every, c, slice(m * P, (m + 1) * P)),
                                           both(cqT, every, c, every), c == 0, c == QC - 1)
                        last.then_inc(s["rope_mm"], 1)
                    for h in range(4 * i, 4 * i + 4):
                        if h in (0, 2):
                            pe.wait_ge(s["kr_sb"], g * 2 + h // 2 + 1)
                        elif h >= 4:
                            pe.wait_ge(s["qa_sb"], g * NH + h - 3)
                        for c in range(QC):
                            last = product(nc, qa_ps[h % 4][:, :], both(wabs, every, c, slice(h * KVR, (h + 1) * KVR)),
                                           both(cqT, every, c, every), c == 0, c == QC - 1)
                        last.then_inc(s["qa_mm"], 1)

            body(0, False)
            with pe.Fori(1, G) as g:
                body(g, True)
            for t in range(TG):
                scores(G - 1, t)


FFN_STEPS = 2 * RSQRT_STEPS + 7


def latent_values(nc, sb, pb, sem, d, x1_dram, probs_dram, nkv_dram, h_dram, base_dram, logits, front, carried):
    x1_v, h_v, base_v = (a.rearrange("(g t p) d -> g p t d", t=TG, p=P) for a in (x1_dram, h_dram, base_dram))
    nkv_v = nkv_dram.rearrange("(n b k) d -> n k b d", b=BT, k=S)
    probs_v = [a.rearrange("n (b k) q -> n k b q", b=BT) for a in probs_dram]

    ident = sb("lv_ident", [P, P], F32)
    kvscale = sb("lv_kvscale", [P, 1], F32)
    rms_w = sb("lv_rms_w", [P, HC], F32)
    wvo = [sb(f"lv_wvo{i}", [P, NH, H], F32R) for i in range(2)]
    wgu = [sb(f"lv_wgu{i}", [P, HC, 2 * F], F32R) for i in range(2)]
    wd = [sb(f"lv_wd{i}", [P, FC, H], F32R) for i in range(2)]
    wr = [sb(f"lv_wr{i}", [P, HC * E + P - E], F32R) for i in range(2)]
    probs = [sb(f"lv_probs{i}", [P, BT, NH * S], F32R) for i in range(2)]
    nf = [sb(f"lv_nf{i}", [P, BT, KVR], F32) for i in range(2)]
    nkv = [sb(f"lv_nkv{i}", [P, BT, KVR], F32R) for i in range(2)]
    oT = [sb(f"lv_oT{i}", [P, 2, NH, P], F32R) for i in range(2)]
    xres = sb("lv_xres", [P, TG, H], F32)
    x2 = sb("lv_x2", [P, TG, H], F32)
    h, xb = front
    hT = [sb(f"lv_hT{i}", [P, HC, GW], F32R) for i in range(2)]
    act_f = sb("lv_act", [P, FC, GW], F32)
    aT = [sb(f"lv_aT{i}", [P, FC, GW], F32R) for i in range(2)]
    lgT = h[0:E, 0, :]
    st = sb("lv_st", [P, TG, 6], F32)
    mv = sb("lv_mv", [P, TG, 2], F32)
    var = sb("lv_var", [P, TG], F32)
    rstd = sb("lv_rstd", [P, TG], F32)
    tmp = sb("lv_tmp", [P, TG], F32)
    rvar = sb("lv_rvar", [P, TG], F32)
    rrms = sb("lv_rrms", [P, TG], F32)
    nbias = sb("lv_nb", [P, TG], F32)

    wo_st = h
    wo_stages = [wo_st, x2]
    wdv_st = value_weights(front)
    wr_st = xb[:, FC, 0:HC * E].rearrange("p (c e) -> p c e", c=HC)

    ring = [pb(f"lv_ring{i}", [P, H], F32) for i in range(4)]
    pv_ps = [pb(f"lv_pv{i}", [P, H], F32) for i in range(2)]
    out_ps = pb("lv_out", [P, H], F32)
    lg_ps = pb("lv_lg", [P, H], F32)

    names = """const_in wo_in1 wr_in wgu_in wd_in x1_in p_in0 p_in1 n_in0 n_in1 h_out base_out zeroed
        wvo_mm wvo_hi wvo_lo w_hi w_lo n_hi n_lo pv_mm o_hi o_lo out_mm x2 moments copied stats hn hT_mm hT_hi
        hT_lo lg_mm lg_sb lgT_mm logits gu_mm silu gated a_hi a_lo down_mm base ln_step settled settled_pe
        settled_pool""".split()
    s = {n: sem("lv_" + n) for n in names}
    s.update({n: carried[n] for n in ("wdv_in", "wo_in0")})
    every = slice(None)
    WO_PART = TG
    WO_PARTS = NH // WO_PART
    HP = NH // BT
    W_PARTS = 2 * HC + 1

    COPIES = 3
    BY_COPY = [slice(i * S, (i + 1) * S) for i in range(COPIES)]
    STACK = slice(0, COPIES * S)

    def router_weights(pair, c):
        return both(pair, slice(None), slice(c * E, c * E + P))

    def first(g):
        return isinstance(g, int) and g == 0

    def after(g, t):
        return (g, t + 1) if t < TG - 1 else (g + 1, 0)

    def at_end(g, t):
        return isinstance(g, int) and g == G - 1 and t == TG - 1

    block = nc.Block()
    with block:

        @block.sync
        def _(sp):
            sp.nop().then_inc(s["h_out"], 16)
            sp.nop().then_inc(s["base_out"], 16)
            sp.dma_start(ident[:, :], d["const"][:, C_IDENT:C_IDENT + P]).then_inc(s["const_in"], 16)
            sp.dma_start(kvscale[:, :], d["kv_scale"]).then_inc(s["const_in"], 16)
            sp.dma_start(rms_w[:, :], d["rms_weight"]).then_inc(s["const_in"], 16)

            def tile_loads(g, t):
                n = g * TG + t
                if not (first(g) and t < 2):
                    sp.wait_ge(s["pv_mm"], (n - 1) * BT)

                def rows(view):
                    return view[n] if isinstance(n, int) else view[bass.ds(n, 1)].rearrange("a k b q -> k (a b) q")

                for i, part in enumerate((0, 0, 1)):
                    sp.dma_start(probs[t % 2][BY_COPY[i], :, :].bitcast(F32), rows(probs_v[part])).then_inc(s[f"p_in{t % 2}"], 16)
                for i in range(COPIES):
                    sp.dma_start(nf[t % 2][BY_COPY[i], :, :], rows(nkv_v)).then_inc(s[f"n_in{t % 2}"], 16)

            for n in range(1, WO_PARTS):
                if n >= 2:
                    sp.wait_ge(s["wvo_mm"], (n - 1) * WO_PART)
                sp.dma_start(wo_stages[n % 2][:, :, :], d["lv_Wo"][:, n * WO_PART:(n + 1) * WO_PART, :]).then_inc(s[f"wo_in{n % 2}"], 16)
            tile_loads(0, 0)
            tile_loads(0, 1)
            sp.dma_start(xres[:, :, :], x1_v[0]).then_inc(s["x1_in"], 16)
            sp.wait_ge(s["wvo_mm"], NH)
            sp.dma_start(h[:, :, :], d["lv_Wgu"]).then_inc(s["wgu_in"], 16)
            sp.dma_start(xb[:, 0:FC, :], d["lv_Wd"]).then_inc(s["wd_in"], 16)
            sp.dma_start(wr_st, d["lv_Wr"]).then_inc(s["wr_in"], 16)

            def residual(g):
                sp.wait_ge(s["x2"], g * TG)
                sp.dma_start(xres[:, :, :], group_of(x1_v, g)).then_inc(s["x1_in"], 16)

            def h_store(g):
                sp.wait_ge(s["hn"], (g + 2) * TG)
                sp.dma_start(group_of(h_v, g), h[:, :, :]).then_inc(s["h_out"], 16)

            def base_store(g):
                sp.wait_ge(s["base"], g * TG + 2 * TG)
                sp.dma_start(group_of(base_v, g), xb[:, :, :]).then_inc(s["base_out"], 16)

            def last_base_store():
                for t in range(TG):
                    sp.wait_ge(s["base"], G * TG + t + 1)
                    sp.dma_start(base_v[G - 1][:, t, :], xb[:, t, :]).then_inc(s["base_out"], 16)

            def body(g, back, ahead):
                if back:
                    residual(g)
                tile_loads(g, 3)
                if back:
                    h_store(g - 1)
                if ahead:
                    for t in range(TG - 1):
                        tile_loads(g + 1, t)
                if back:
                    base_store(g - 1)

            tile_loads(0, 2)
            body(0, False, True)
            with sp.Fori(1, G - 1) as g:
                body(g, True, True)
            body(G - 1, True, False)
            h_store(G - 1)
            last_base_store()
            sp.wait_ge(s["h_out"], (G + 1) * 16)
            sp.wait_ge(s["base_out"], (G + TG) * 16)

        @block.gpsimd
        def _(pool):
            pool.nop().then_inc(s["copied"], TG)
            for i in range(2):
                nc.gpsimd.memset(wr[i][:, :].bitcast(F32), 0.0).then_inc(s["zeroed"], 1)

            def copy(g):
                pool.wait_ge(s["base_out"], g * 16 + 16)
                for t in range(TG):
                    pool.wait_ge(s["x2"], g * TG + t + 1)
                    settle(pool, s["settled_pool"])
                    nc.gpsimd.tensor_copy(xb[:, t, :], x2[:, t, :]).then_inc(s["copied"], 1)

            pool.wait_ge(s["w_lo"], W_PARTS)
            copy(0)
            with pool.Fori(1, G) as g:
                copy(g)

        @block.scalar
        def _(act):
            act.nop().then_inc(s["hn"], TG)
            act.wait_ge(s["const_in"], 48)
            for n in range(NH):
                act.wait_ge(s["wvo_mm"], n + 1)
                nc.scalar.activation(wvo[0][:, n, :], ring[n % 4][:, :], ACT.Copy,
                                     scale=kvscale[:, 0:1]).then_inc(s["wvo_hi"], 1)

            def later_weights():
                act.wait_ge(s["wgu_in"], 16)
                for c in range(HC):
                    nc.scalar.activation(wgu[0][:, c, :], h[:, c, :], ACT.Copy, scale=rms_w[:, c:c + 1]).then_inc(s["w_hi"], 1)
                act.wait_ge(s["wd_in"], 16)
                nc.scalar.copy(wd[0][:, :, :], xb[:, 0:FC, :]).then_inc(s["w_hi"], 1)
                act.wait_ge(s["wr_in"], 16)
                act.wait_ge(s["zeroed"], 2)
                for c in range(HC):
                    nc.scalar.activation(wr[0][:, c * E:(c + 1) * E], wr_st[:, c, :], ACT.Copy, scale=rms_w[:, c:c + 1]).then_inc(s["w_hi"], 1)

            def latents_high(g, t):
                act.wait_ge(s[f"n_in{t % 2}"], (g * 2 + t // 2 + 1) * 16 * COPIES)
                if not (first(g) and t < 2):
                    act.wait_ge(s["pv_mm"], (g * TG + t) * BT - BT)
                nc.scalar.copy(nkv[t % 2][STACK, :, :], nf[t % 2][STACK, :, :]).then_inc(s["n_hi"], 1)

            def sum_high(g, t, b):
                act.wait_ge(s["pv_mm"], (g * TG + t) * BT + b + 1)
                nc.scalar.copy(oT[0][:, t % 2, :, b * S:(b + 1) * S],
                               pv_ps[b % 2][:, :].rearrange("p (h q) -> p h q", h=NH)).then_inc(s["o_hi"], 1)

            def normalise(g):
                act.wait_ge(s["stats"], g + 1)
                act.wait_ge(s["h_out"], g * 16 + 16)
                act.wait_ge(s["hT_mm"], g * TG + TG)
                for t in range(TG):
                    nc.scalar.activation(h[:, t, :], x2[:, t, :], ACT.Identity, bias=nbias[:, t:t + 1],
                                         scale=rstd[:, t:t + 1]).then_inc(s["hn"], 1)

            def h_high(g):
                for t in range(TG):
                    act.wait_ge(s["hT_mm"], (g + 1) * TG + t + 1)
                    nc.scalar.copy(hT[0][:, :, t * P:(t + 1) * P],
                                   ring[t][:, :].rearrange("p (c q) -> p c q", c=HC)).then_inc(s["hT_hi"], 1)

            def logit_copy(g):
                act.wait_ge(s["lg_mm"], g + 1)
                act.wait_ge(s["h_out"], (g + 2) * 16)
                nc.scalar.copy(lgT, lg_ps[0:E, :]).then_inc(s["lg_sb"], 1)

            def silu(g, m):
                act.wait_ge(s["gu_mm"], g * 2 * FC + m + 1)
                nc.scalar.activation(act_f[:, m, :], ring[m][:, :], ACT.Silu).then_inc(s["silu"], 1)

            def gated_high(g, m):
                act.wait_ge(s["gated"], g * FC + m + 1)
                if m == FC - 1:
                    act.wait_ge(s["lgT_mm"], g + 1)
                nc.scalar.copy(aT[0][:, m, :], act_f[:, m, :]).then_inc(s["a_hi"], 1)

            def shared(g, t, q):
                if (t, q) == (0, 3):
                    normalise(g)
                elif (t, q) == (1, 0):
                    h_high(g)
                elif (t, q) == (1, 2):
                    logit_copy(g)
                    silu(g, 0)
                elif (t, q) == (1, 3):
                    silu(g, 1)
                elif (t, q) == (2, 1):
                    gated_high(g, 0)
                elif (t, q) == (2, 2):
                    gated_high(g, 1)

            def body(g, back):
                for t in range(TG):
                    for q in range(BT):
                        if not at_end(g, t):
                            sum_high(*after(g, t), q)
                        if q == 2 and t < 2:
                            latents_high(g, t + 2)
                        if q == 2 and t >= 2 and not (isinstance(g, int) and g == G - 1):
                            latents_high(g + 1, t - 2)
                        if back:
                            shared(g - 1, t, q)

            latents_high(0, 0)
            latents_high(0, 1)
            for b in range(BT):
                sum_high(0, 0, b)
            later_weights()
            body(0, False)
            with act.Fori(1, G - 1) as g:
                body(g, True)
            body(G - 1, True)
            for t in range(TG):
                for q in range(BT):
                    shared(G - 1, t, q)

        @block.vector
        def _(dve):
            dve.wait_ge(s["const_in"], 48)
            dve.nop().then_inc(s["base"], TG)
            dve.nop().then_inc(s["logits"], 1)
            for n in range(NH):
                dve.wait_ge(s["wvo_hi"], n + 1)
                nc.vector.scalar_tensor_tensor(wvo[1][:, n, :], ring[n % 4][:, :], kvscale[:, 0:1],
                                               wvo[0][:, n, :].bitcast(F32), ALU.mult, ALU.subtract).then_inc(s["wvo_lo"], 1)

            def later_weights():
                for c in range(HC):
                    dve.wait_ge(s["w_hi"], c + 1)
                    nc.vector.scalar_tensor_tensor(wgu[1][:, c, :], h[:, c, :], rms_w[:, c:c + 1],
                                                   wgu[0][:, c, :].bitcast(F32), ALU.mult,
                                                   ALU.subtract).then_inc(s["w_lo"], 1)
                dve.wait_ge(s["w_hi"], HC + 1)
                nc.vector.tensor_tensor(wd[1][:, :, :], xb[:, 0:FC, :], wd[0][:, :, :].bitcast(F32),
                                        ALU.subtract).then_inc(s["w_lo"], 1)
                for c in range(HC):
                    dve.wait_ge(s["w_hi"], HC + c + 2)
                    nc.vector.scalar_tensor_tensor(wr[1][:, c * E:(c + 1) * E], wr_st[:, c, :], rms_w[:, c:c + 1],
                                                   wr[0][:, c * E:(c + 1) * E].bitcast(F32), ALU.mult,
                                                   ALU.subtract).then_inc(s["w_lo"], 1)

            def latents_low(g, t):
                dve.wait_ge(s["n_hi"], g * TG + t + 1)
                low = nkv[t % 2][BY_COPY[1], :, :]
                nc.vector.tensor_tensor(low, nf[t % 2][BY_COPY[1], :, :], low.bitcast(F32), ALU.subtract).then_inc(s["n_lo"], 1)

            def sum_low(g, t, b):
                dve.wait_ge(s["o_hi"], (g * TG + t) * BT + b + 1)
                part = (every, t % 2, every, slice(b * S, (b + 1) * S))
                nc.vector.tensor_tensor(oT[1][part], pv_ps[b % 2][:, :].rearrange("p (h q) -> p h q", h=NH),
                                        oT[0][part].bitcast(F32), ALU.subtract).then_inc(s["o_lo"], 1)

            def add(g, t):
                if t == 0:
                    dve.wait_ge(s["x1_in"], g * 16 + 16)
                dve.wait_ge(s["hn"], g * TG + t + 1)
                dve.wait_ge(s["copied"], g * TG + t + 1)
                dve.wait_ge(s["out_mm"], g * TG + t + 1)
                nc.vector.tensor_tensor(x2[:, t, :], out_ps[:, :], xres[:, t, :], ALU.add).then_inc(s["x2"], 1)

            def moments(g, t):
                dve.wait_ge(s["x2"], g * TG + t + 1)
                nc.vector.bn_stats(st[:, t, :], x2[:, t, :]).then_inc(s["moments"], 1)

            def chain(g, done):
                return Steps(dve, s["ln_step"], g * FFN_STEPS + done)

            def variance(g):
                dve.wait_ge(s["moments"], g * TG + TG)
                settle(dve, s["settled"])
                step = chain(g, 0)
                for t in range(TG):
                    last = nc.vector.bn_aggr(mv[:, t, :], st[:, t, :])
                step(last)
                step(nc.vector.tensor_scalar(var[:, :], mv[:, :, 1], LN_EPS, None, ALU.add))

            def layer_scale(g):
                step = chain(g, 2)
                rsqrt(nc, step, rstd[:, :], tmp[:, :], var[:, :])
                step(nc.vector.tensor_tensor(rvar[:, :], rstd[:, :], rstd[:, :], ALU.mult))
                step(nc.vector.tensor_tensor(rvar[:, :], rvar[:, :], mv[:, :, 1], ALU.mult))
                step(nc.vector.tensor_scalar(rvar[:, :], rvar[:, :], RMS_EPS, None, ALU.add))

            def both_scales(g):
                step = chain(g, RSQRT_STEPS + 5)
                rsqrt(nc, step, rrms[:, :], tmp[:, :], rvar[:, :])
                step(nc.vector.tensor_tensor(rstd[:, :], rstd[:, :], rrms[:, :], ALU.mult))
                step(nc.vector.scalar_tensor_tensor(nbias[:, :], mv[:, :, 0], -1.0, rstd[:, :], ALU.mult, ALU.mult))
                dve.nop().then_inc(s["stats"], 1)

            def h_low(g):
                for t in range(TG):
                    dve.wait_ge(s["hT_hi"], g * TG + t + 1)
                    part = (every, every, slice(t * P, (t + 1) * P))
                    nc.vector.tensor_tensor(hT[1][part], ring[t][:, :].rearrange("p (c q) -> p c q", c=HC),
                                            hT[0][part].bitcast(F32), ALU.subtract).then_inc(s["hT_lo"], 1)

            def gate(g, m):
                dve.wait_ge(s["silu"], g * FC + m + 1)
                dve.wait_ge(s["gu_mm"], g * 2 * FC + FC + m + 1)
                nc.vector.tensor_tensor(act_f[:, m, :], ring[FC + m][:, :], act_f[:, m, :], ALU.mult).then_inc(s["gated"], 1)

            def gated_low(g, m):
                dve.wait_ge(s["a_hi"], g * FC + m + 1)
                nc.vector.tensor_tensor(aT[1][:, m, :], act_f[:, m, :], aT[0][:, m, :].bitcast(F32),
                                        ALU.subtract).then_inc(s["a_lo"], 1)

            def router(g):
                dve.wait_ge(s["lgT_mm"], g + 1)
                dst = logits[:, g * TG:(g + 1) * TG, :] if isinstance(g, int) else logits[:, bass.ds(g * TG, TG), :]
                nc.vector.tensor_copy(dst, lg_ps[:, 0:TG * E].rearrange("p (t e) -> p t e", t=TG)).then_inc(s["logits"], 1)

            def base(g, t):
                if t == 0:
                    dve.wait_ge(s["copied"], (g + 2) * TG)
                dve.wait_ge(s["down_mm"], g * TG + t + 1)
                nc.vector.tensor_tensor(xb[:, t, :], ring[t][:, :], xb[:, t, :], ALU.add).then_inc(s["base"], 1)

            def shared(g, t, q):
                if (t, q) == (0, 0):
                    moments(g, TG - 1)
                    variance(g)
                elif (t, q) == (0, 1):
                    layer_scale(g)
                elif (t, q) == (0, 2):
                    both_scales(g)
                elif (t, q) == (1, 0):
                    h_low(g)
                elif (t, q) == (2, 0):
                    gate(g, 0)
                elif (t, q) == (2, 1):
                    gate(g, 1)
                    gated_low(g, 0)
                elif (t, q) == (2, 2):
                    router(g)
                    gated_low(g, 1)
                elif (t, q) == (3, 0):
                    base(g, 0)
                elif (t, q) == (3, 1):
                    base(g, 1)
                elif (t, q) == (3, 2):
                    base(g, 2)
                elif (t, q) == (3, 3):
                    base(g, 3)

            def body(g, back):
                for t in range(TG):
                    for q in range(BT):
                        if q == 0 and t > 0:
                            add(g, t - 1)
                        if q == 0 and t == 0 and back:
                            add(g - 1, TG - 1)
                        if not at_end(g, t):
                            sum_low(*after(g, t), q)
                        if q == 3 and t < 2:
                            latents_low(g, t + 2)
                        if q == 3 and t >= 2 and not (isinstance(g, int) and g == G - 1):
                            latents_low(g + 1, t - 2)
                        if q == 0 and t > 0:
                            moments(g, t - 1)
                        if back:
                            shared(g - 1, t, q)

            latents_low(0, 0)
            latents_low(0, 1)
            for b in range(BT):
                sum_low(0, 0, b)
            later_weights()
            body(0, False)
            with dve.Fori(1, G - 1) as g:
                body(g, True)
            body(G - 1, True)
            add(G - 1, TG - 1)
            for t in range(TG):
                for q in range(BT):
                    shared(G - 1, t, q)

        @block.tensor
        def _(pe):
            pe.nop().then_inc(s["hT_mm"], TG)
            pe.wait_ge(s["wdv_in"], 16)
            for n in range(NH):
                if n % WO_PART == 0:
                    part = n // WO_PART
                    pe.wait_ge(s[f"wo_in{part % 2}"], 16 * (part // 2 + 1))
                if n >= 4:
                    pe.wait_ge(s["wvo_lo"], n - 3)
                nc.tensor.matmul(ring[n % 4][:, :], wdv_st[:, n, :], wo_stages[n // WO_PART % 2][:, n % WO_PART, :],
                                 start=True, stop=True).then_inc(s["wvo_mm"], 1)

            def weighted(g, t, b):
                n = g * TG + t
                if b == 0:
                    pe.wait_ge(s["n_lo"], n + 1)
                    pe.wait_ge(s[f"p_in{t % 2}"], (g * 2 + t // 2 + 1) * 16 * COPIES)
                if not (first(g) and t == 0 and b < 2):
                    pe.wait_ge(s["o_lo"], n * BT + b - 1)
                nc.tensor.matmul(pv_ps[b % 2][:, :], nkv[t % 2][STACK, b, :], probs[t % 2][STACK, b, :],
                                 start=True, stop=True).then_inc(s["pv_mm"], 1)

            def outputs(g, t, q):
                n = g * TG + t
                if q == 0:
                    pe.wait_ge(s["o_lo"], n * BT + BT)
                    if not (first(g) and t == 0):
                        pe.wait_ge(s["x2"], n)
                for i in range(q * HP, (q + 1) * HP):
                    last = product(nc, out_ps[:, :], both(oT, every, t % 2, i, every), both(wvo, every, i, every),
                                   i == 0, i == NH - 1)
                if q == BT - 1:
                    last.then_inc(s["out_mm"], 1)

            def transposes(g):
                for t in range(TG):
                    pe.wait_ge(s["hn"], (g + 1) * TG + t + 1)
                    pe.wait_ge(s["base"], g * TG + t + 1)
                    for c in range(HC):
                        last = nc.tensor.transpose(ring[t][:, c * P:(c + 1) * P], h[:, t, c * P:(c + 1) * P], ident[:, :])
                    last.then_inc(s["hT_mm"], 1)

            def router(g):
                pe.wait_ge(s["hT_lo"], g * TG + TG)
                pe.wait_ge(s["logits"], g + 1)
                for c in range(HC):
                    last = product(nc, lg_ps[:, :], router_weights(wr, c), both(hT, every, c, every), c == 0, c == HC - 1)
                last.then_inc(s["lg_mm"], 1)

            def shared_up(g, m):
                for c in range(HC):
                    last = product(nc, ring[m][:, :], both(wgu, every, c, slice(m * P, (m + 1) * P)),
                                   both(hT, every, c, every), c == 0, c == HC - 1)
                last.then_inc(s["gu_mm"], 1)

            def logit_transposes(g):
                pe.wait_ge(s["lg_sb"], g + 1)
                settle(pe, s["settled_pe"])
                for t in range(TG):
                    last = nc.tensor.transpose(lg_ps[:, t * E:(t + 1) * E], lgT[:, t * P:(t + 1) * P], ident[0:E, 0:E])
                last.then_inc(s["lgT_mm"], 1)

            def shared_down(g, t):
                pe.wait_ge(s["a_lo"], g * FC + FC)
                for m in range(FC):
                    last = product(nc, ring[t][:, :], both(aT, every, m, slice(t * P, (t + 1) * P)),
                                   both(wd, every, m, every), m == 0, m == FC - 1)
                last.then_inc(s["down_mm"], 1)

            def shared(g, t, q):
                if (t, q) == (1, 0):
                    transposes(g)
                elif (t, q) == (1, 1):
                    router(g)
                    shared_up(g, 0)
                elif (t, q) == (1, 2):
                    shared_up(g, 1)
                elif (t, q) == (1, 3):
                    shared_up(g, 2)
                elif (t, q) == (2, 0):
                    shared_up(g, 3)
                elif (t, q) == (2, 1):
                    logit_transposes(g)
                elif (t, q) == (2, 3):
                    shared_down(g, 0)
                elif (t, q) == (3, 0):
                    shared_down(g, 1)
                elif (t, q) == (3, 1):
                    shared_down(g, 2)
                elif (t, q) == (3, 2):
                    shared_down(g, 3)

            def body(g, back):
                for t in range(TG):
                    for q in range(BT):
                        if not at_end(g, t):
                            weighted(*after(g, t), q)
                        outputs(g, t, q)
                        if back:
                            shared(g - 1, t, q)

            pe.wait_ge(s["wvo_lo"], NH)
            pe.wait_ge(s["const_in"], 48)
            for b in range(BT):
                weighted(0, 0, b)
            body(0, False)
            pe.wait_ge(s["w_lo"], W_PARTS)
            with pe.Fori(1, G - 1) as g:
                body(g, True)
            body(G - 1, True)
            for t in range(TG):
                for q in range(BT):
                    shared(G - 1, t, q)


UE = 4
PB = 4


def experts(nc, sb, pb, sem, d, h_dram, out_dram, logits):
    const = sb("ex_const", [P, C_END], F32)
    ident = const[:, C_IDENT:C_IDENT + P]
    ones = sb("ex_ones", [P, P], F32)
    rms_w = sb("ex_rms_w", [P, HC], F32)
    wgu = [sb(f"ex_wgu{i}", [P, E * HC, 2 * F], F32R) for i in range(2)]
    wd = sb("ex_wd", [P, E * FC, H], F32)
    hs = sb("ex_hs", [P, UE, H], F32)
    hT = [sb(f"ex_hT{i}", [P, 2, HC, P], F32R) for i in range(2)]
    gated = sb("ex_gated", [P, 2, F], F32)
    aT = sb("ex_aT", [P, 2, FC, P], F32)
    y = sb("ex_y", [P, 2, H], F32)
    route = [sb(f"ex_route{i}", [P, NT, E], F32) for i in range(3)]
    hot = [sb(f"ex_hot{i}", [P, NT, E], F32) for i in range(2)]
    row = [sb(f"ex_row{i}", [P, NT], F32) for i in range(4)]
    per = [sb(f"ex_per{i}", [P, E], F32) for i in range(4)]
    count = sb("ex_count", [P, E], I32)
    weights = sb("ex_weights", [P, TOPK, NT], F32)
    slot_i = sb("ex_slot_i", [P, TOPK, NT], I32)
    part = [sb(f"ex_part{i}", [P, TOPK, NT], I32) for i in range(2)]
    part_f = [sb(f"ex_part_f{i}", [P, TOPK, NT], F32) for i in range(2)]
    row_hot = sb("ex_row_hot", [P, 2, PB, P], F32)
    tile_hot = sb("ex_tile_hot", [P, 2, PB, 2, NTE], F32)
    same_tile = sb("ex_same_tile", [P, 2, PB, NTE], F32)
    empty = sb("ex_empty", [P, NTE], F32)
    zeros = gated[:, :, :].rearrange("p a b -> p (a b)")
    expert_f = sb("ex_expert_f", [P, NTE], F32)
    expert = sb("ex_expert", [P, NTE], I32)
    source = sb("ex_source", [P, NTE], U32)
    share = sb("ex_share", [P, NTE], F32)
    from_row = sb("ex_from_row", [P, UE], U32)
    to_row = sb("ex_to_row", [P, UE], U32)

    hT_ps = [pb(f"ex_hT_ps{i}", [P, H], F32) for i in range(2)]
    gu_ps = [pb(f"ex_gu_ps{i}", [P, H], F32) for i in range(2)]
    aT_ps = pb("ex_aT_ps", [P, H], F32)
    y_ps = [pb(f"ex_y_ps{i}", [P, H], F32) for i in range(2)]
    count_ps = pb("ex_count_ps", [P, H], F32)
    place_ps = y_ps[0]

    names = """const_in rms_in wd_in wgu_in0 wgu_in1 wgu_in2 wgu_in3 wgu_in4
        wgu_in5 wgu_in6 wgu_in7 ones zeroed pad_rows scaled wgu_hi wgu_lo route delta gap ranked
        count_mm same hot placed placed_all indexed to_rows gather0 gather1 gather2 gather3 hT_mm hT_hi hT_lo gu_mm silu
        gated aT_mm aT y_mm y_sb summed settled""".split()
    s = {n: sem("ex_" + n) for n in names}
    every = slice(None)

    def first(g):
        return isinstance(g, int) and g == 0

    def up_weights(e):
        return (w[:, e * HC:(e + 1) * HC, :] for w in wgu)

    block = nc.Block()
    with block:

        @block.sync
        def _(sp):
            sp.dma_start(const[:, :], d["const"]).then_inc(s["const_in"], 16)
            sp.dma_start(rms_w[:, :], d["rms_weight"]).then_inc(s["rms_in"], 16)
            for e in range(E):
                _, low = up_weights(e)
                sp.dma_start(low.bitcast(F32), d["ex_Wgu"][:, e * HC:(e + 1) * HC, :]).then_inc(s[f"wgu_in{e}"], 16)
            sp.wait_ge(s["zeroed"], 1)
            sp.dma_start(h_dram[T:T + P, :], zeros).then_inc(s["pad_rows"], 16)
            sp.dma_start(out_dram[T:T + P, :], zeros).then_inc(s["pad_rows"], 16)
            sp.dma_start(wd[:, :, :], d["ex_Wd"]).then_inc(s["wd_in"], 16)

        @block.gpsimd
        def _(pool):
            nc.gpsimd.memset(zeros, 0.0).then_inc(s["zeroed"], 1)
            nc.gpsimd.memset(ones[:, :], 1.0).then_inc(s["ones"], 1)
            for e in range(E):
                high, low = up_weights(e)
                pool.wait_ge(s["wgu_hi"], e + 1)
                nc.gpsimd.tensor_tensor(low, low.bitcast(F32), high.bitcast(F32), ALU.subtract).then_inc(s["wgu_lo"], 1)
            pool.wait_ge(s["pad_rows"], 32)

            def tokens(k):
                return source[:, k * UE:(k + 1) * UE] if isinstance(k, int) else source[:, bass.ds(k * UE, UE)]

            def gather(k, i):
                pool.wait_ge(s["indexed"], k + 1)
                if not first(k):
                    pool.wait_ge(s["hT_mm"], (k - 1) * UE + i + 1)
                settle(pool, s["settled"])
                nc.gpsimd.indirect_dma_start(
                    hs[:, i, :], None, h_dram, bass.IndirectOffsetOnAxis(ap=from_row[:, i:i + 1], axis=0)
                ).then_inc(s[f"gather{i}"], 16)

            def add(k, i):
                n = k * UE + i
                pool.wait_ge(s["to_rows"], k + 1)
                pool.wait_ge(s["y_sb"], n + 1)
                if not (first(k) and i == 0):
                    pool.wait_ge(s["summed"], n * 16)
                settle(pool, s["settled"])
                nc.gpsimd.indirect_dma_start(
                    out_dram, bass.IndirectOffsetOnAxis(ap=to_row[:, i:i + 1], axis=0), y[:, i % 2, :], None,
                    compute_op=ALU.add).then_inc(s["summed"], 16)

            def turn(k, ahead):
                if ahead:
                    for i in range(UE):
                        pool.wait_ge(s[f"gather{i}"], k * 16 + 16)
                    settle(pool, s["settled"])
                    nc.gpsimd.tensor_copy(from_row[:, :], tokens(k + 1)).then_inc(s["indexed"], 1)
                if not first(k):
                    pool.wait_ge(s["summed"], k * UE * 16)
                settle(pool, s["settled"])
                nc.gpsimd.tensor_copy(to_row[:, :], tokens(k)).then_inc(s["to_rows"], 1)
                for i in range(UE):
                    if ahead:
                        gather(k + 1, i)
                    add(k, i)

            pool.wait_ge(s["placed_all"], 1)
            nc.gpsimd.tensor_copy(from_row[:, :], tokens(0)).then_inc(s["indexed"], 1)
            for i in range(UE):
                gather(0, i)
            turn(0, True)
            with pool.Fori(1, NTE // UE - 1) as k:
                turn(k, True)
            turn(NTE // UE - 1, False)
            pool.wait_ge(s["summed"], NTE * 16)

        @block.scalar
        def _(act):
            act.wait_ge(s["rms_in"], 16)
            act.wait_ge(s["delta"], 1)
            nc.scalar.activation(row[3][:, :], row[2][:, :], ACT.Exp).then_inc(s["gap"], 1)
            for e in range(E):
                high, low = up_weights(e)
                act.wait_ge(s[f"wgu_in{e}"], 16)
                for c in range(HC):
                    weight = low.bitcast(F32)[:, c, :]
                    last = nc.scalar.activation(weight, weight, ACT.Copy, scale=rms_w[:, c:c + 1])
                last.then_inc(s["scaled"], 1)
                act.wait_ge(s["scaled"], e + 1)
                nc.scalar.copy(high, low.bitcast(F32)).then_inc(s["wgu_hi"], 1)

            def hT_high(n, i):
                act.wait_ge(s["hT_mm"], n + 1)
                if not isinstance(n, int) or n >= 2:
                    act.wait_ge(s["gu_mm"], n - 1)
                nc.scalar.copy(hT[0][:, i % 2, :, :], hT_ps[i % 2][:, :].rearrange("p (c q) -> p c q", c=HC)).then_inc(s["hT_hi"], 1)

            def silu(n, i):
                act.wait_ge(s["gu_mm"], n + 1)
                if not isinstance(n, int) or n >= 2:
                    act.wait_ge(s["aT_mm"], n - 1)
                nc.scalar.activation(gated[:, i % 2, :], gu_ps[i % 2][:, 0:F], ACT.Silu).then_inc(s["silu"], 1)

            def result(n, i):
                act.wait_ge(s["y_mm"], n + 1)
                if not isinstance(n, int) or n >= 2:
                    act.wait_ge(s["summed"], (n - 1) * 16)
                nc.scalar.activation(y[:, i % 2, :], y_ps[i % 2][:, :], ACT.Copy,
                                     scale=share[:, n:n + 1] if isinstance(n, int) else share[:, bass.ds(n, 1)]
                                     ).then_inc(s["y_sb"], 1)

            def tile(k, i):
                n = k * UE + i
                if not (first(k) and i < 2):
                    result(n - 2, i)
                silu(n, i)
                if i < UE - 1 or not isinstance(k, int) or k < NTE // UE - 1:
                    hT_high(n + 1, i + 1)

            act.wait_ge(s["placed_all"], 1)
            hT_high(0, 0)
            for i in range(UE):
                tile(0, i)
            with act.Fori(1, NTE // UE - 1) as k:
                for i in range(UE):
                    tile(k, i)
            for i in range(UE):
                tile(NTE // UE - 1, i)
            result(NTE - 2, UE - 2)
            result(NTE - 1, UE - 1)

        @block.vector
        def _(dve):
            step = Steps(dve, s["route"], 0)
            dve.wait_ge(s["rms_in"], 16)
            dve.wait_ge(s["const_in"], 16)
            order = const[:, C_FIRST:C_FIRST + E].unsqueeze(1).broadcast_to([P, NT, E])

            def spread(a):
                return a[:, :].unsqueeze(2).broadcast_to([P, NT, E])

            score, scratch, base = route
            for k in range(TOPK):
                src = logits if k == 0 else score
                step(nc.vector.tensor_reduce(row[k][:, :], src[:, :, :], AX.X, ALU.max))
                step(nc.vector.tensor_tensor(scratch[:, :, :], src[:, :, :], spread(row[k]), ALU.is_equal))
                step(nc.vector.tensor_tensor(scratch[:, :, :], scratch[:, :, :], order, ALU.mult))
                step(nc.vector.tensor_reduce(row[2][:, :], scratch[:, :, :], AX.X, ALU.max))
                step(nc.vector.tensor_tensor(hot[k][:, :, :], order, spread(row[2]), ALU.is_equal))
                if k == 0:
                    step(nc.vector.scalar_tensor_tensor(score[:, :, :], hot[0][:, :, :], MASKED, logits[:, :, :],
                                                        ALU.mult, ALU.add))
            nc.vector.tensor_tensor(row[2][:, :], row[1][:, :], row[0][:, :], ALU.subtract).then_inc(s["delta"], 1)
            nc.vector.tensor_tensor(score[:, :, :], hot[0][:, :, :], hot[1][:, :, :], ALU.add).then_inc(s["ranked"], 1)
            dve.wait_ge(s["gap"], 1)
            step(nc.vector.tensor_scalar(row[0][:, :], row[3][:, :], 1.0, None, ALU.add))
            step(nc.vector.reciprocal(weights[:, 0, :], row[0][:, :]))
            step(nc.vector.tensor_tensor(weights[:, 1, :], row[3][:, :], weights[:, 0, :], ALU.mult))
            dve.wait_ge(s["count_mm"], 1)
            rank, total = (count_ps[:, a:a + NT * E].rearrange("p (t e) -> p t e", e=E) for a in (0, NT * E))
            step(nc.vector.tensor_copy(scratch[:, :, :], total))
            a, b = scratch, base
            k = 1
            while k < NT:
                nc.vector.tensor_tensor(b[:, k:, :], a[:, k:, :], a[:, :NT - k, :], ALU.add)
                step(nc.vector.tensor_copy(b[:, :k, :], a[:, :k, :]))
                a, b, k = b, a, 2 * k
            step(nc.vector.tensor_scalar(count[:, :], a[:, NT - 1, :], float(P - 1), None, ALU.add))
            step(nc.vector.tensor_scalar(count[:, :], count[:, :], P.bit_length() - 1, None, ALU.arith_shift_right))
            step(nc.vector.tensor_copy(per[0][:, :], count[:, :]))
            step(nc.vector.tensor_copy(per[1][:, :], per[0][:, :]))
            c, e = per[1], per[2]
            k = 1
            while k < E:
                nc.vector.tensor_tensor(e[:, k:], c[:, k:], c[:, :E - k], ALU.add)
                step(nc.vector.tensor_copy(e[:, :k], c[:, :k]))
                c, e, k = e, c, 2 * k
            start = per[3]
            step(nc.vector.tensor_tensor(start[:, :], c[:, :], per[0][:, :], ALU.subtract))
            step(nc.vector.tensor_tensor(a[:, :, :], a[:, :, :], total, ALU.subtract))
            step(nc.vector.tensor_tensor(a[:, :, :], a[:, :, :], rank, ALU.add))
            step(nc.vector.scalar_tensor_tensor(a[:, :, :], start[:, :].unsqueeze(1).broadcast_to([P, NT, E]),
                                                float(P), a[:, :, :], ALU.mult, ALU.add))
            for k in range(TOPK):
                step(nc.vector.tensor_tensor(b[:, :, :], hot[k][:, :, :], a[:, :, :], ALU.mult))
                step(nc.vector.tensor_reduce(part_f[0][:, k, :], b[:, :, :], AX.X, ALU.add))
            step(nc.vector.tensor_copy(slot_i[:, :, :], part_f[0][:, :, :]))
            nc.vector.tensor_scalar(part[0][:, :, :], slot_i[:, :, :], P - 1, None, ALU.bitwise_and)
            step(nc.vector.tensor_scalar(part[1][:, :, :], slot_i[:, :, :], P.bit_length() - 1, None, ALU.arith_shift_right))
            nc.vector.tensor_copy(part_f[0][:, :, :], part[0][:, :, :])
            step(nc.vector.tensor_copy(part_f[1][:, :, :], part[1][:, :, :]))
            number = const[:, C_COUNT:C_COUNT + P]
            for n in range(TOPK * NT // PB):
                k, t = divmod(n * PB, NT)
                if n >= 2:
                    dve.wait_ge(s["placed"], n - 1)

                def spread_tiles(a):
                    return a.unsqueeze(2).broadcast_to([P, PB, NTE])

                nc.vector.tensor_tensor(same_tile[:, n % 2], number[:, 0:NTE].unsqueeze(1).broadcast_to([P, PB, NTE]),
                                        spread_tiles(part_f[1][:, k, t:t + PB]), ALU.is_equal).then_inc(s["same"], 1)
                nc.vector.tensor_tensor(row_hot[:, n % 2], number.unsqueeze(1).broadcast_to([P, PB, P]),
                                        part_f[0][:, k, t:t + PB].unsqueeze(2).broadcast_to([P, PB, P]), ALU.is_equal)
                dve.wait_ge(s["same"], n + 1)
                nc.vector.tensor_tensor(tile_hot[:, n % 2, :, 0, :], same_tile[:, n % 2],
                                        spread_tiles(const[:, C_TOKEN + t:C_TOKEN + t + PB]), ALU.mult)
                nc.vector.tensor_tensor(tile_hot[:, n % 2, :, 1, :], same_tile[:, n % 2],
                                        spread_tiles(weights[:, k, t:t + PB]), ALU.mult).then_inc(s["hot"], 1)
            tiles = const[:, C_COUNT:C_COUNT + NTE]
            step(nc.vector.tensor_scalar(expert_f[:, :], tiles, start[:, 1:2], None, ALU.is_ge))
            for k in range(2, E):
                step(nc.vector.scalar_tensor_tensor(expert_f[:, :], tiles, start[:, k:k + 1], expert_f[:, :],
                                                    ALU.is_ge, ALU.add))
            step(nc.vector.tensor_copy(expert[:, :], expert_f[:, :]))
            dve.wait_ge(s["placed"], TOPK * NT // PB)
            placed, shares = place_ps[:, 0:NTE], place_ps[:, NTE:2 * NTE]
            step(nc.vector.tensor_scalar(empty[:, :], placed, 0.0, None, ALU.is_equal))
            step(nc.vector.scalar_tensor_tensor(empty[:, :], empty[:, :], const[:, C_PAD:C_PAD + 1], placed,
                                                ALU.mult, ALU.add))
            nc.vector.tensor_copy(share[:, :], shares)
            step(nc.vector.tensor_scalar(source[:, :], empty[:, :], -1.0, None, ALU.add))
            dve.nop().then_inc(s["placed_all"], 1)

            def hT_low(n, i):
                dve.wait_ge(s["hT_hi"], n + 1)
                nc.vector.tensor_tensor(hT[1][:, i % 2, :, :], hT_ps[i % 2][:, :].rearrange("p (c q) -> p c q", c=HC),
                                        hT[0][:, i % 2, :, :].bitcast(F32), ALU.subtract).then_inc(s["hT_lo"], 1)

            def gate(n, i):
                dve.wait_ge(s["silu"], n + 1)
                nc.vector.tensor_tensor(gated[:, i % 2, :], gu_ps[i % 2][:, F:2 * F], gated[:, i % 2, :],
                                        ALU.mult).then_inc(s["gated"], 1)

            def aT_copy(n, i):
                dve.wait_ge(s["aT_mm"], n + 1)
                if not isinstance(n, int) or n >= 2:
                    dve.wait_ge(s["y_mm"], n - 1)
                nc.vector.tensor_copy(aT[:, i % 2, :, :], aT_ps[:, 0:F].rearrange("p (c q) -> p c q", c=FC)).then_inc(s["aT"], 1)

            def tile(k, i):
                n = k * UE + i
                if not (first(k) and i == 0):
                    aT_copy(n - 1, i - 1)
                gate(n, i)
                if i < UE - 1 or not isinstance(k, int) or k < NTE // UE - 1:
                    hT_low(n + 1, i + 1)

            hT_low(0, 0)
            for i in range(UE):
                tile(0, i)
            with dve.Fori(1, NTE // UE - 1) as k:
                for i in range(UE):
                    tile(k, i)
            for i in range(UE):
                tile(NTE // UE - 1, i)
            aT_copy(NTE - 1, UE - 1)

        @block.tensor
        def _(pe):
            pe.wait_ge(s["const_in"], 16)
            pe.wait_ge(s["ones"], 1)
            pe.wait_ge(s["ranked"], 1)
            chosen = route[0][:, :, :].rearrange("p t e -> p (t e)")
            nc.tensor.matmul(count_ps[:, 0:NT * E], const[:, C_TRI:C_TRI + P], chosen, start=True, stop=True)
            nc.tensor.matmul(count_ps[:, NT * E:2 * NT * E], ones[:, :], chosen, start=True, stop=True).then_inc(s["count_mm"], 1)
            for n in range(TOPK * NT // PB):
                pe.wait_ge(s["hot"], n + 1)
                for i in range(PB):
                    last = nc.tensor.matmul(place_ps[:, 0:2 * NTE], row_hot[:, n % 2, i, :],
                                            tile_hot[:, n % 2, i, :, :].rearrange("p a n -> p (a n)"),
                                            start=n == 0 and i == 0, stop=n == TOPK * NT // PB - 1 and i == PB - 1)
                last.then_inc(s["placed"], 1)
            pe.wait_ge(s["wgu_lo"], E)
            pe.wait_ge(s["wd_in"], 16)
            pe.wait_ge(s["placed_all"], 1)

            def transposes(k, n, i):
                pe.wait_ge(s[f"gather{i % UE}"], (k + i // UE) * 16 + 16)
                if not isinstance(n, int) or n >= 2:
                    pe.wait_ge(s["hT_lo"], n - 1)
                for c in range(HC):
                    last = nc.tensor.transpose(hT_ps[i % 2][:, c * P:(c + 1) * P], hs[:, i % UE, c * P:(c + 1) * P], ident)
                last.then_inc(s["hT_mm"], 1)

            def up(n, i, e):
                pe.wait_ge(s["hT_lo"], n + 1)
                if not isinstance(n, int) or n >= 2:
                    pe.wait_ge(s["gated"], n - 1)
                for c in range(HC):
                    a = both(hT, every, i % 2, c, every)
                    w = [wgu[j][:, bass.ds(e * HC + c, 1), :].rearrange("p a f -> p (a f)") for j in range(2)]
                    last = product(nc, gu_ps[i % 2][:, :], a, w, c == 0, c == HC - 1)
                last.then_inc(s["gu_mm"], 1)

            def down(n, i, e):
                pe.wait_ge(s["aT"], n + 1)
                if not isinstance(n, int) or n >= 2:
                    pe.wait_ge(s["y_sb"], n - 1)
                for c in range(FC):
                    last = nc.tensor.matmul(y_ps[i % 2][:, :], aT[:, i % 2, c, :],
                                            wd[:, bass.ds(e * FC + c, 1), :].rearrange("p a f -> p (a f)"),
                                            start=c == 0, stop=c == FC - 1)
                last.then_inc(s["y_mm"], 1)

            def gated_transposes(n, i):
                pe.wait_ge(s["gated"], n + 1)
                if not isinstance(n, int) or n >= 1:
                    pe.wait_ge(s["aT"], n)
                for c in range(FC):
                    last = nc.tensor.transpose(aT_ps[:, c * P:(c + 1) * P], gated[:, i % 2, c * P:(c + 1) * P], ident)
                last.then_inc(s["aT_mm"], 1)

            def expert_of(n):
                column = expert[0:1, n:n + 1] if isinstance(n, int) else expert[0:1, bass.ds(n, 1)]
                return pe.value_load(column, min_val=0, max_val=E - 1)

            def tile(k, i):
                n = k * UE + i
                if not (first(k) and i == 0):
                    gated_transposes(n - 1, i - 1)
                up(n, i, expert_of(n))
                if i < UE - 1 or not isinstance(k, int) or k < NTE // UE - 1:
                    transposes(k, n + 1, i + 1)
                if not (first(k) and i == 0):
                    down(n - 1, i - 1, expert_of(n - 1))

            transposes(0, 0, 0)
            for i in range(UE):
                tile(0, i)
            with pe.Fori(1, NTE // UE - 1) as k:
                for i in range(UE):
                    tile(k, i)
            for i in range(UE):
                tile(NTE // UE - 1, i)
            gated_transposes(NTE - 1, UE - 1)
            down(NTE - 1, UE - 1, expert_of(NTE - 1))


def program(nc, d, out):
    def dram(name, *shape):
        return nc.dram_tensor(name, shape, F32).ap()

    x1, h = dram("x1", T, H), dram("h", T + P, H)
    probs = [nc.dram_tensor(f"probs{i}", (NT, P, NH * S), F32).ap() for i in range(2)]
    nkv = dram("nkv", T, KVR)

    def memory(stack):
        taken = []

        def semaphore(name):
            taken.append(nc.alloc_semaphore(name))
            return taken[-1]

        def finish():
            if taken:
                nc.clear_and_free_semaphores(taken)
                nc.all_engine_barrier()

        stack.callback(finish)
        return (lambda name, shape, dt: stack.enter_context(nc.sbuf_tensor(name, shape, dt)),
                lambda name, shape, dt: stack.enter_context(nc.psum_tensor(name, shape, dt)),
                semaphore)

    with ExitStack() as outer:
        logits = memory(outer)[0]("logits", [P, NT, E], F32)
        with ExitStack() as first:
            sb, _, semaphore = memory(first)
            front = [sb(f"front{i}", [P, TG, H], F32) for i in range(2)]
            carried = {n: semaphore(n) for n in ("x1_in", "wdv_in", "wo_in0")}
            with ExitStack() as stack:
                cross_attention(nc, *memory(stack), d, x1, front, carried)
            with ExitStack() as stack:
                latent_scores(nc, *memory(stack), d, x1, probs, nkv, front, carried)
            with ExitStack() as stack:
                latent_values(nc, *memory(stack), d, x1, probs, nkv, h[0:T, :], out[0:T, :], logits, front, carried)
        with ExitStack() as stack:
            experts(nc, *memory(stack), d, h, out, logits)


def prepare(a):
    def chunks(w):
        return np.ascontiguousarray(w.reshape(-1, P, w.shape[-1]).transpose(1, 0, 2))

    a = {k: np.asarray(v) for k, v in a.items()}
    halves = a["L0_attn_W_krope"].reshape(H, RH, 2).transpose(0, 2, 1).reshape(H, ROPE)
    rope = a["L0_attn_W_dq_rope"].reshape(QR, NH // HJ, HJ, RH, 2).transpose(0, 1, 4, 2, 3).reshape(QR, NH * ROPE)
    gate_up = np.concatenate([a["L0_ffn_w_gate"], a["L0_ffn_w_up"]], axis=2).reshape(E, HC, P, 2 * F)
    return {
        "x": np.ascontiguousarray(a["x"].reshape(T, H)),
        "ctxT": np.ascontiguousarray(a["ctx_512"][:, :S, :].reshape(T, L).T),
        "const": constants(),
        "xa_WqT": chunks(a["L0_xattn_Wq"].T),
        "xa_WkvT": np.ascontiguousarray(a["L0_xattn_Wkv_expand"].T),
        "xa_WoutT": chunks(a["L0_xattn_Wout"].T),
        "q_scale": np.ascontiguousarray(a["L0_attn_q_scale"].reshape(QC, P).T),
        "kv_scale": a["L0_attn_kv_scale"].reshape(P, 1),
        "ls_Wc": chunks(np.concatenate([a["L0_attn_W_cq"], a["L0_attn_W_ckv"], halves], axis=1)),
        "ls_WdqT": np.ascontiguousarray(a["L0_attn_W_dq_nope"].reshape(QR, NH, NOPE).transpose(2, 1, 0)),
        "ls_WdkT": np.ascontiguousarray(a["L0_attn_W_dk_nope"].reshape(KVR, NH, NOPE).transpose(2, 1, 0)),
        "ls_Wrope": chunks(rope),
        "lv_WdvT": np.ascontiguousarray(a["L0_attn_W_dv"].reshape(KVR, NH, VD).transpose(2, 1, 0)),
        "lv_Wo": np.ascontiguousarray(a["L0_attn_W_o"].reshape(NH, VD, H).transpose(1, 0, 2)),
        "lv_Wgu": chunks(np.concatenate([a["L0_ffn_sw_gate"], a["L0_ffn_sw_up"]], axis=1)),
        "lv_Wd": chunks(a["L0_ffn_sw_down"]),
        "lv_Wr": chunks(a["L0_ffn_router_w"]),
        "rms_weight": np.ascontiguousarray(a["L0_ffn_rms_weight"].reshape(HC, P).T),
        "ex_Wgu": np.ascontiguousarray(gate_up.transpose(2, 0, 1, 3).reshape(P, E * HC, 2 * F)),
        "ex_Wd": np.ascontiguousarray(a["L0_ffn_w_down"].reshape(E, FC, P, H).transpose(2, 0, 1, 3).reshape(P, E * FC, H)),
    }


def kernel(**inputs):
    import concourse.bacc as bacc
    from concourse.bass_utils import run_bass_kernel_spmd

    nc = bacc.Bacc("TRN2", target_bir_lowering=False, num_devices=1)
    arrays = {f"in_{name}": a for name, a in prepare(inputs).items()}
    d = {name[3:]: nc.dram_tensor(name, a.shape, mybir.dt.from_np(a.dtype), kind="ExternalInput").ap()
         for name, a in arrays.items()}
    out = nc.dram_tensor("out", (T + P, H), F32, kind="ExternalOutput").ap()
    program(nc, d, out)
    r = run_bass_kernel_spmd(nc, [arrays], core_ids=[0])
    return r.results[0]["out"][:T].reshape(B, S, H)
```
